# Optimizing a Trainium2 kernel written in Bass

```python
import numpy as np
import jax
import jax.numpy as jnp

def _softmax(x, axis=-1):
    return jax.nn.softmax(x, axis=axis)

def _gelu(x):
    return jax.nn.gelu(x, approximate=True)

def _silu(x):
    return jax.nn.silu(x)

def _sigmoid(x):
    return jax.nn.sigmoid(x)

def _layernorm(x, axis=-1, eps=1e-05):
    m = jnp.mean(x, axis=axis, keepdims=True)
    v = jnp.var(x, axis=axis, keepdims=True)
    return (x - m) / jnp.sqrt(v + eps)

def _scatter_add(tgt, idx, src, axis=0):
    return tgt.at[idx].add(src)

def _segment_sum(src, seg, n):
    return jax.ops.segment_sum(src, seg, n)
kernel_name = 'mk_decoder_preln_d1_seqx_r4_326f7d'

def setup_inputs(seed: int=0):
    np.random.seed(seed)
    _w = jnp.asarray

    def _rec_inputs():
        import jax
        import jax.numpy as jnp
        _rk = jax.random.key(seed)
        x = -0.0005207 + 1.001 * jax.random.normal(jax.random.fold_in(_rk, 1), (16, 112, 512), jnp.float32)
        _lenS = 112 - jax.random.randint(jax.random.fold_in(_rk, 7), (16,), 0, max(1, 112 // 4) + 1, jnp.int32)
        _lenS2 = 375 - jax.random.randint(jax.random.fold_in(_rk, 8), (16,), 0, max(1, 375 // 4) + 1, jnp.int32)
        _ctx_2048P = jax.random.normal(jax.random.fold_in(_rk, 11), (16, 16, 512), jnp.float32)
        _ctx_2048c = jax.random.dirichlet(jax.random.fold_in(_rk, 511), 0.3 * jnp.ones((16,), jnp.float32), (16, 375))
        _ctx_2048t = jnp.einsum('bsk,bkd->bsd', _ctx_2048c, _ctx_2048P)
        _ctx_2048t = _ctx_2048t * jax.lax.rsqrt(jnp.mean(jnp.square(_ctx_2048t)) + 1e-12) * 0.953939
        ctx_2048 = 2.81802e-05 + 1.00001 * (_ctx_2048t + 0.3 * jax.random.normal(jax.random.fold_in(_rk, 611), (16, 375, 512), jnp.float32))
        pos_BxS2 = jnp.broadcast_to(jnp.arange(375, dtype=jnp.int32), (16, 375))
        itok_BxS_4096_4607 = jax.random.randint(jax.random.fold_in(_rk, 13), (16, 112), 1024, 1152, jnp.int32)
        return (x, ctx_2048, pos_BxS2, itok_BxS_4096_4607)
    x, ctx_2048, pos_BxS2, itok_BxS_4096_4607 = _rec_inputs()

    def _L0_attn_setup():
        import jax, jax.numpy as jnp
        import numpy as np
        B, S, HID = (2, 512, 512)
        H = 16
        NOPE, ROPE, V_DIM, KV_RANK = (128, 64, 128, 128)
        Q_DIM = NOPE + ROPE
        EPS = 1e-06
        NEG = -1000000000.0

        def _rmsnorm(x, w):
            xf = x.astype(jnp.float32)
            var = jnp.mean(xf * xf, axis=-1, keepdims=True)
            return w * (xf * jax.lax.rsqrt(var + EPS)).astype(x.dtype)
        key = jax.random.key(seed)
        ks = jax.random.split(key, 5)
        return {'hidden_states': jax.random.normal(ks[0], (B, S, HID), jnp.float32), 'q_proj_w': jax.random.normal(ks[1], (H * Q_DIM, HID), jnp.float32) * HID ** (-0.5), 'kv_a_proj_w': jax.random.normal(ks[2], (KV_RANK + ROPE, HID), jnp.float32) * HID ** (-0.5), 'kv_a_ln_w': jnp.ones((KV_RANK,), jnp.float32), 'kv_b_proj_w': jax.random.normal(ks[3], (H * (NOPE + V_DIM), KV_RANK), jnp.float32) * KV_RANK ** (-0.5), 'o_proj_w': jax.random.normal(ks[4], (HID, H * V_DIM), jnp.float32) * (H * V_DIM) ** (-0.5)}
    _L0_attn_all = _L0_attn_setup()
    _L0_attn_in = {k: v for k, v in _L0_attn_all.items() if k in ('q_proj_w', 'kv_a_proj_w', 'kv_a_ln_w', 'kv_b_proj_w', 'o_proj_w')}
    del _L0_attn_all

    def _L0_xattn_setup():
        import jax, jax.numpy as jnp
        import numpy as np
        B, CTX, DRAFT, D = (2, 1024, 128, 512)
        H, KVH, HD = (16, 4, 128)
        N_REP = H // KVH
        EPS = 1e-06
        THETA = 10000.0
        SCALE = 1.0 / np.sqrt(HD).astype(np.float32)

        def _rms_norm(x, w):
            v = jnp.mean(jnp.square(x.astype(jnp.float32)), axis=-1, keepdims=True)
            return (w * (x.astype(jnp.float32) * jax.lax.rsqrt(v + EPS))).astype(x.dtype)

        def _rotate_half(x):
            x1, x2 = jnp.split(x, 2, axis=-1)
            return jnp.concatenate((-x2, x1), axis=-1)

        def _rope(x, pos):
            inv_freq = 1.0 / THETA ** (jnp.arange(0, HD, 2, dtype=jnp.float32) / HD)
            freqs = pos.astype(jnp.float32)[:, None, :, None] * inv_freq
            emb = jnp.concatenate((freqs, freqs), axis=-1)
            return x * jnp.cos(emb) + _rotate_half(x) * jnp.sin(emb)
        key = jax.random.key(seed)
        ks = jax.random.split(key, 6)
        return {'draft_hidden': jax.random.normal(ks[0], (B, DRAFT, D), jnp.float32), 'context_hidden': jax.random.normal(ks[1], (B, CTX, D), jnp.float32), 'Wq': jax.random.normal(ks[2], (H * HD, D), jnp.float32) * 0.02, 'Wk': jax.random.normal(ks[3], (KVH * HD, D), jnp.float32) * 0.02, 'Wv': jax.random.normal(ks[4], (KVH * HD, D), jnp.float32) * 0.02, 'Wo': jax.random.normal(ks[5], (D, H * HD), jnp.float32) * 0.02, 'q_norm_w': jnp.ones((HD,), jnp.float32), 'k_norm_w': jnp.ones((HD,), jnp.float32), 'context_position_ids': jnp.broadcast_to(jnp.arange(CTX, dtype=jnp.int32), (B, CTX)), 'draft_position_ids': jnp.broadcast_to(CTX + jnp.arange(DRAFT, dtype=jnp.int32), (B, DRAFT))}
    _L0_xattn_all = _L0_xattn_setup()
    _L0_xattn_in = {k: v for k, v in _L0_xattn_all.items() if k in ('Wq', 'Wk', 'Wv', 'Wo', 'q_norm_w', 'k_norm_w')}
    del _L0_xattn_all

    def _L0_ffn_setup():
        import jax, jax.numpy as jnp
        import numpy as np
        B, S, H = (2, 512, 512)
        INTER = 256
        N_ROUTED = 8
        ZERO = 4
        TOTAL = N_ROUTED + ZERO
        TOP_K = 2
        SCALE = 1.5
        key = jax.random.key(seed)
        k0, k1, k2, k3, k4, k5 = jax.random.split(key, 6)
        w = 0.02
        return {'hidden_states': jax.random.normal(k0, (B, S, H), jnp.float32), 'classifier_w': jax.random.normal(k1, (TOTAL, H), jnp.float32) * w, 'e_score_correction_bias': jax.random.normal(k2, (TOTAL,), jnp.float32) * w, 'gate_w': jax.random.normal(k3, (N_ROUTED, INTER, H), jnp.float32) * w, 'up_w': jax.random.normal(k4, (N_ROUTED, INTER, H), jnp.float32) * w, 'down_w': jax.random.normal(k5, (N_ROUTED, H, INTER), jnp.float32) * w}
    _L0_ffn_all = _L0_ffn_setup()
    _L0_ffn_in = {k: v for k, v in _L0_ffn_all.items() if k in ('classifier_w', 'e_score_correction_bias', 'gate_w', 'up_w', 'down_w')}
    del _L0_ffn_all
    return {'x': x, 'ctx_2048': ctx_2048, 'pos_BxS2': pos_BxS2, 'itok_BxS_4096_4607': itok_BxS_4096_4607, 'L0_attn_q_proj_w': _L0_attn_in['q_proj_w'], 'L0_attn_kv_a_proj_w': _L0_attn_in['kv_a_proj_w'], 'L0_attn_kv_a_ln_w': _L0_attn_in['kv_a_ln_w'], 'L0_attn_kv_b_proj_w': _L0_attn_in['kv_b_proj_w'], 'L0_attn_o_proj_w': _L0_attn_in['o_proj_w'], 'L0_xattn_Wq': _L0_xattn_in['Wq'], 'L0_xattn_Wk': _L0_xattn_in['Wk'], 'L0_xattn_Wv': _L0_xattn_in['Wv'], 'L0_xattn_Wo': _L0_xattn_in['Wo'], 'L0_xattn_q_norm_w': _L0_xattn_in['q_norm_w'], 'L0_xattn_k_norm_w': _L0_xattn_in['k_norm_w'], 'L0_ffn_classifier_w': _L0_ffn_in['classifier_w'], 'L0_ffn_e_score_correction_bias': _L0_ffn_in['e_score_correction_bias'], 'L0_ffn_gate_w': _L0_ffn_in['gate_w'], 'L0_ffn_up_w': _L0_ffn_in['up_w'], 'L0_ffn_down_w': _L0_ffn_in['down_w']}

def reference(x, ctx_2048, pos_BxS2, itok_BxS_4096_4607, L0_attn_q_proj_w, L0_attn_kv_a_proj_w, L0_attn_kv_a_ln_w, L0_attn_kv_b_proj_w, L0_attn_o_proj_w, L0_xattn_Wq, L0_xattn_Wk, L0_xattn_Wv, L0_xattn_Wo, L0_xattn_q_norm_w, L0_xattn_k_norm_w, L0_ffn_classifier_w, L0_ffn_e_score_correction_bias, L0_ffn_gate_w, L0_ffn_up_w, L0_ffn_down_w):
    import jax
    import jax.numpy as jnp

    def _L0_attn_ref(hidden_states, q_proj_w, kv_a_proj_w, kv_a_ln_w, kv_b_proj_w, o_proj_w):
        import jax, jax.numpy as jnp
        import numpy as np
        B, S, HID = (2, 512, 512)
        H = 16
        NOPE, ROPE, V_DIM, KV_RANK = (128, 64, 128, 128)
        Q_DIM = NOPE + ROPE
        EPS = 1e-06
        NEG = -1000000000.0

        def _rmsnorm(x, w):
            xf = x.astype(jnp.float32)
            var = jnp.mean(xf * xf, axis=-1, keepdims=True)
            return w * (xf * jax.lax.rsqrt(var + EPS)).astype(x.dtype)
        b, s, _ = hidden_states.shape
        scaling = Q_DIM ** (-0.5)
        q = (hidden_states @ q_proj_w.T).reshape(b, s, H, Q_DIM).transpose(0, 2, 1, 3)
        compressed = hidden_states @ kv_a_proj_w.T
        k_pass_lat = compressed[..., :KV_RANK]
        k_rot = compressed[..., KV_RANK:]
        kv = _rmsnorm(k_pass_lat, kv_a_ln_w) @ kv_b_proj_w.T
        kv = kv.reshape(b, s, H, NOPE + V_DIM).transpose(0, 2, 1, 3)
        k_pass = kv[..., :NOPE]
        v = kv[..., NOPE:]
        k_rot = jnp.broadcast_to(k_rot[:, None, :, :], (b, H, s, ROPE))
        k = jnp.concatenate([k_pass, k_rot], axis=-1)
        scores = jnp.einsum('bhqd,bhkd->bhqk', q, k) * scaling
        causal = jnp.tril(jnp.ones((s, s), bool))
        scores = jnp.where(causal[None, None], scores, NEG)
        probs = jax.nn.softmax(scores.astype(jnp.float32), axis=-1).astype(q.dtype)
        out = jnp.einsum('bhqk,bhkd->bhqd', probs, v)
        out = out.transpose(0, 2, 1, 3).reshape(b, s, H * V_DIM)
        return out @ o_proj_w.T

    def _L0_xattn_ref(draft_hidden, context_hidden, Wq, Wk, Wv, Wo, q_norm_w, k_norm_w, context_position_ids, draft_position_ids):
        import jax, jax.numpy as jnp
        import numpy as np
        B, CTX, DRAFT, D = (2, 1024, 128, 512)
        H, KVH, HD = (16, 4, 128)
        N_REP = H // KVH
        EPS = 1e-06
        THETA = 10000.0
        SCALE = 1.0 / np.sqrt(HD).astype(np.float32)

        def _rms_norm(x, w):
            v = jnp.mean(jnp.square(x.astype(jnp.float32)), axis=-1, keepdims=True)
            return (w * (x.astype(jnp.float32) * jax.lax.rsqrt(v + EPS))).astype(x.dtype)

        def _rotate_half(x):
            x1, x2 = jnp.split(x, 2, axis=-1)
            return jnp.concatenate((-x2, x1), axis=-1)

        def _rope(x, pos):
            inv_freq = 1.0 / THETA ** (jnp.arange(0, HD, 2, dtype=jnp.float32) / HD)
            freqs = pos.astype(jnp.float32)[:, None, :, None] * inv_freq
            emb = jnp.concatenate((freqs, freqs), axis=-1)
            return x * jnp.cos(emb) + _rotate_half(x) * jnp.sin(emb)
        bsz, draft_len, _ = draft_hidden.shape
        ctx_len = context_hidden.shape[1]
        total_len = ctx_len + draft_len
        q = (draft_hidden @ Wq.T).reshape(bsz, draft_len, H, HD)
        q = _rms_norm(q, q_norm_w).transpose(0, 2, 1, 3)
        kv_in = jnp.concatenate([context_hidden, draft_hidden], axis=1)
        k = (kv_in @ Wk.T).reshape(bsz, total_len, KVH, HD)
        v = (kv_in @ Wv.T).reshape(bsz, total_len, KVH, HD).transpose(0, 2, 1, 3)
        k = _rms_norm(k, k_norm_w).transpose(0, 2, 1, 3)
        full_position_ids = jnp.concatenate([context_position_ids, draft_position_ids], axis=1)
        q = _rope(q, draft_position_ids)
        k = _rope(k, full_position_ids)
        k = jnp.repeat(k, N_REP, axis=1)
        v = jnp.repeat(v, N_REP, axis=1)
        scores = jnp.einsum('bhqd,bhkd->bhqk', q, k) * SCALE
        probs = jax.nn.softmax(scores, axis=-1)
        attn = jnp.einsum('bhqk,bhkd->bhqd', probs, v)
        attn = attn.transpose(0, 2, 1, 3).reshape(bsz, draft_len, H * HD)
        return attn @ Wo.T

    def _L0_ffn_ref(hidden_states, classifier_w, e_score_correction_bias, gate_w, up_w, down_w):
        import jax, jax.numpy as jnp
        import numpy as np
        B, S, H = (2, 512, 512)
        INTER = 256
        N_ROUTED = 8
        ZERO = 4
        TOTAL = N_ROUTED + ZERO
        TOP_K = 2
        SCALE = 1.5
        x = hidden_states
        total = classifier_w.shape[0]
        n_routed = gate_w.shape[0]
        logits = jnp.einsum('bsh,eh->bse', x, classifier_w)
        probs = jax.nn.softmax(logits, axis=-1)
        biased = probs + e_score_correction_bias
        _, idx = jax.lax.top_k(biased, TOP_K)
        rw = jnp.take_along_axis(probs, idx, axis=-1) * SCALE
        w_full = jnp.sum(jax.nn.one_hot(idx, total, dtype=x.dtype) * rw[..., None], axis=-2)
        g = jnp.einsum('bsh,eih->bsei', x, gate_w)
        u = jnp.einsum('bsh,eih->bsei', x, up_w)
        act = jax.nn.silu(g) * u
        expert_out = jnp.einsum('bsei,ehi->bseh', act, down_w)
        out = jnp.einsum('bse,bseh->bsh', w_full[..., :n_routed], expert_out)
        out = out + x * jnp.sum(w_full[..., n_routed:], axis=-1, keepdims=True)
        return out
    x = x + _L0_attn_ref(_layernorm(x, axis=-1), L0_attn_q_proj_w, L0_attn_kv_a_proj_w, L0_attn_kv_a_ln_w, L0_attn_kv_b_proj_w, L0_attn_o_proj_w)
    x = x + _L0_xattn_ref(_layernorm(x, axis=-1), ctx_2048, L0_xattn_Wq, L0_xattn_Wk, L0_xattn_Wv, L0_xattn_Wo, L0_xattn_q_norm_w, L0_xattn_k_norm_w, pos_BxS2, itok_BxS_4096_4607)
    x = x + _L0_ffn_ref(_layernorm(x, axis=-1), L0_ffn_classifier_w, L0_ffn_e_score_correction_bias, L0_ffn_gate_w, L0_ffn_up_w, L0_ffn_down_w)
    return x

_drawn_inputs = setup_inputs


def setup_inputs(seed=0):
    import zlib

    import numpy as np

    out = dict(_drawn_inputs(seed))
    spreads = {'L0_attn_kv_a_ln_w': (1.0, 0.2),
     'L0_xattn_q_norm_w': (1.0, 0.6),
     'L0_xattn_k_norm_w': (1.0, 0.6)}
    factors = {'L0_ffn_gate_w': 7.262, 'L0_ffn_up_w': 7.212, 'L0_ffn_down_w': 7.224}
    for name, (base, spread) in spreads.items():
        noise = np.random.default_rng([zlib.crc32(name.encode()), seed]).standard_normal(out[name].shape)
        drawn = base * np.exp(spread * noise) if base else spread * noise
        out[name] = jnp.asarray(drawn.astype(out[name].dtype))
    for name, factor in factors.items():
        out[name] = (out[name] * factor).astype(out[name].dtype)
    return out
```

```python
from contextlib import ExitStack

import numpy as np

import concourse.bass as bass
from concourse import mybir

F32 = mybir.dt.float32
F32R = mybir.dt.float32r
I32 = mybir.dt.int32
U32 = mybir.dt.uint32
ALU = mybir.AluOpType
ACT = mybir.ActivationFunctionType
AX = mybir.AxisListType

B, S, D = 16, 112, 512
T = B * S
C = 375
KV = C + S
P = 128
KD = D // P
H = 16
HQ = 4
NQ = H // HQ
NOPE, ROPE, RANK = 128, 64, 128
HD, KVH = 128, 4
CT = C // 3
E, TOTAL, INTER = 8, 12, 256
TT = T // P
G = 4
GT = G * S
LN_EPS, RMS_EPS = 1e-5, 1e-6
MLA_SCALE = float((NOPE + ROPE) ** -0.5)
X_SCALE = float(HD ** -0.5)
ROUTE_SCALE = 1.5
MASKED = -3.0e9
PI2 = (6.28125, float(2 * np.pi) - 6.28125)


class Event:

    def __init__(self, sem, per, ahead, step):
        self.sem = sem
        self.per, self.ahead, self.step = per, ahead, step

    def at(self, item, n=0):
        return (item * self.per + (n + 1 + self.ahead)) * self.step

    def open(self, eng):
        eng.sem_inc(self.sem, self.ahead * self.step)


def wait(eng, event, item, n=0):
    eng.wait_ge(event.sem, event.at(item, n))


def carry(eng, item, ticks):
    if not isinstance(item, int):
        eng.sem_inc(ticks, 1)


def mm3(pe, out, a_hi, a_lo, b_hi, b_lo, start, stop):
    pe.matmul(out, a_hi, b_hi, start=start, stop=False)
    pe.matmul(out, a_hi, b_lo, start=False, stop=False)
    return pe.matmul(out, a_lo, b_hi, start=False, stop=stop)


def over_heads(ap, n):
    return ap.unsqueeze(1).broadcast_to((ap.shape[0], n, ap.shape[1]))


def along(ap, n):
    return ap.unsqueeze(2).broadcast_to((ap.shape[0], ap.shape[1], n))


class Phase(ExitStack):

    def __init__(self, nc, name):
        super().__init__()
        self.nc, self.name = nc, name
        self.sems = []

    def sb(self, name, shape, dt=F32):
        return self.enter_context(self.nc.sbuf_tensor(f"{self.name}_{name}", shape, dt))

    def sem(self, name):
        self.sems.append(self.nc.alloc_semaphore(name=f"{self.name}_{name}"))
        return self.sems[-1]

    def __exit__(self, *exc):
        done = super().__exit__(*exc)
        self.nc.clear_and_free_semaphores(self.sems)
        self.nc.all_engine_barrier()
        return done

    def ev(self, name, per, ahead=0, step=1):
        return Event(self.sem(name), per, ahead, step)

    def bank(self, name, *shape):
        flat = self.enter_context(self.nc.psum_tensor(f"{self.name}_{name}", [P, 512], F32))
        if len(shape) == 2:
            return flat[0:shape[0], 0:shape[1]]
        return flat[0:shape[0], 0:shape[1] * shape[2]].rearrange("p (a b) -> p a b", a=shape[1])


def identity(pool, tile, sem):
    pool.memset(tile, 0.0).then_inc(sem, 1)
    pool.wait_ge(sem, 1)
    pool.affine_select(out=tile, in_=tile, compare_op=ALU.not_equal, fill=1.0, base=0,
                       pattern=[[-1, tile.shape[1]]], channel_multiplier=1).then_inc(sem, 1)


def fold_weights(nc, wq_nope, wkb, wvb, woT, wq_rotT, wkvaT, qf_hi, qf_lo, qr_hi, qr_lo, kva_hi, kva_lo, scratch, vo):
    ctx = Phase(nc, "fold")
    with ctx:
        sb = ctx.sb
        sem = ctx.sem
        wq = sb("wq_nat", [P, 2, HQ, D])
        kb = sb("kb_nat", [P, H, RANK])
        vb = sb("vb_nat", [P, H, RANK])
        wo = sb("wo_nat", [P, 2, HQ, D])
        rot = scratch[:, 0:KD * H * ROPE].rearrange("p (k n) -> p k n", k=KD)
        kva = sb("kva_raw", [P, KD, RANK + ROPE])
        vos = sb("vos", [P, 2, HQ, D])
        psq = [ctx.bank(f"psq{i}", P, 512) for i in range(4)]
        psv = [ctx.bank(f"psv{i}", P, 512) for i in range(4)]
        small, wq_in = sem("small_loaded"), [sem("wq_loaded0"), sem("wq_loaded1")]
        wo_in = [sem("wo_loaded0"), sem("wo_loaded1")]
        split_in, vb_in = sem("split_loaded"), sem("vb_loaded")
        stored = [sem("vo_stored0"), sem("vo_stored1")]
        q_mm, v_mm, q_hi, q_lo, v_out, plain_hi, plain_lo = (sem(n) for n in (
            "q_products", "v_products", "q_hi", "q_lo", "v_copied", "plain_hi", "plain_lo"))
        block = ctx.enter_context(nc.Block())
        nope = wq_nope.rearrange("(h d) i -> d h i", h=H)

        @block.sync
        def _(sp):
            sp.dma_start(kb[:, :, :], wkb).then_inc(small, 16)
            for c in range(NQ):
                if c >= 2:
                    sp.wait_ge(q_mm, KD * (c - 1))
                sp.dma_start(wq[:, c % 2], nope[0:NOPE, c * HQ:(c + 1) * HQ, :]).then_inc(wq_in[c % 2], 16)
            for c in range(NQ):
                sp.wait_ge(v_out, HQ * (c + 1))
                sp.dma_start(vo[:, c * HQ:(c + 1) * HQ, :], vos[:, c % 2]).then_inc(stored[c % 2], 16)
            for i in range(2):
                sp.wait_ge(stored[i], 16 * NQ // 2)

        @block.gpsimd
        def _(pool):
            pool.wait_ge(plain_hi, 1)
            pool.tensor_tensor(kva_lo[:, :, :], kva[:, :, :], kva_hi[:, :, :], ALU.subtract).then_inc(plain_lo, 1)
            pool.wait_ge(plain_hi, 2)
            pool.tensor_tensor(qr_lo[:, :, :], rot[:, :, :], qr_hi[:, :, :], ALU.subtract).then_inc(plain_lo, 1)

        @block.tensor
        def _(pe):
            pe.wait_ge(small, 16)
            for c in range(NQ):
                pe.wait_ge(wq_in[c % 2], 16 * (c // 2 + 1))
                for k in range(KD):
                    n = c * KD + k
                    if n >= 4:
                        pe.wait_ge(q_lo, n - 3)
                    for j in range(HQ):
                        mm = pe.matmul(psq[n % 4][:, j * RANK:(j + 1) * RANK], wq[:, c % 2, j, k * P:(k + 1) * P],
                                       kb[:, c * HQ + j, :], start=True, stop=True)
                    mm.then_inc(q_mm, 1)
            pe.wait_ge(vb_in, 16)
            for c in range(NQ):
                pe.wait_ge(wo_in[c % 2], 16 * (c // 2 + 1))
                for j in range(HQ):
                    n = c * HQ + j
                    if n >= 4:
                        pe.wait_ge(v_out, n - 3)
                    pe.matmul(psv[n % 4][:, :], vb[:, n, :], wo[:, c % 2, j, :], start=True, stop=True).then_inc(v_mm, 1)

        @block.scalar
        def _(act):
            act.dma_start(kva[:, :, :], wkvaT).then_inc(split_in, 16)
            act.dma_start(rot[:, :, :], wq_rotT).then_inc(split_in, 16)
            act.dma_start(vb[:, :, :], wvb).then_inc(vb_in, 16)
            for c in range(2):
                act.dma_start(wo[:, c], woT[:, c * HQ:(c + 1) * HQ, :]).then_inc(wo_in[c], 16)
            act.wait_ge(split_in, 32)
            act.activation(kva_hi[:, :, :], kva[:, :, :], ACT.Copy).then_inc(plain_hi, 1)
            act.activation(qr_hi[:, :, :], rot[:, :, :], ACT.Copy).then_inc(plain_hi, 1)
            for n in range(NQ * KD):
                c, k = n // KD, n % KD
                act.wait_ge(q_mm, n + 1)
                act.activation(qf_hi[:, k, c * HQ:(c + 1) * HQ, :], psq[n % 4][:, :], ACT.Copy).then_inc(q_hi, 1)
            for c in range(2, NQ):
                act.wait_ge(v_mm, HQ * (c - 1))
                act.dma_start(wo[:, c % 2], woT[:, c * HQ:(c + 1) * HQ, :]).then_inc(wo_in[c % 2], 16)

        @block.vector
        def _(dve):
            for n in range(NQ * KD):
                c, k = n // KD, n % KD
                dve.wait_ge(q_hi, n + 1)
                dve.tensor_tensor(qf_lo[:, k, c * HQ:(c + 1) * HQ, :], psq[n % 4][:, :].rearrange("p (j r) -> p j r", j=HQ),
                                  qf_hi[:, k, c * HQ:(c + 1) * HQ, :], ALU.subtract).then_inc(q_lo, 1)
            for n in range(H):
                c = n // HQ
                if c >= 2 and n % HQ == 0:
                    dve.wait_ge(stored[c % 2], 16 * (c // 2))
                dve.wait_ge(v_mm, n + 1)
                dve.tensor_copy(vos[:, c % 2, n % HQ, :], psv[n % 4][:, :]).then_inc(v_out, 1)


class LayerNorm:

    def __init__(self, ctx, rows):
        self.stats, self.mv = ctx.sb("stats", [rows, 6]), ctx.sb("mean_var", [rows, 2])
        self.counted, self.varied = ctx.ev("ln_stats", 1), ctx.ev("ln_var", 1)
        self.ticks = ctx.sem("ln_ticks")
        self.shifted, self.rooted = ctx.ev("ln_var_eps", 1), ctx.ev("ln_rstd", 1)

    def vector(self, dve, item, dst, src):
        dve.bn_stats(self.stats[:, :], src).then_inc(self.counted.sem, 1)
        wait(dve, self.counted, item)
        carry(dve, item, self.ticks)
        dve.bn_aggr(self.mv[:, :], self.stats[:, :]).then_inc(self.varied.sem, 1)
        wait(dve, self.rooted, item)
        return dve.tensor_scalar(dst, src, self.mv[:, 0:1], self.mv[:, 1:2], ALU.subtract, ALU.mult)

    def root(self, pool, item, minus_half):
        var = self.mv[:, 1:2]
        wait(pool, self.varied, item)
        carry(pool, item, self.ticks)
        pool.tensor_scalar(var, var, LN_EPS, None, ALU.add).then_inc(self.shifted.sem, 1)
        wait(pool, self.shifted, item)
        pool.tensor_tensor(var, var, minus_half[0:var.shape[0], 0:1], ALU.pow).then_inc(self.rooted.sem, 1)


def exponent(pool, tile, sem):
    pool.memset(tile, -0.5).then_inc(sem, 1)
    pool.wait_ge(sem, 1)


def latents(nc, x, lnw, kva_hi, kva_lo, lat_kT, lat_v, xT_hi, xT_lo):
    W = RANK + ROPE
    ctx = Phase(nc, "lat")
    with ctx:
        sb = ctx.sb
        ev = ctx.ev
        ident = sb("ident", [S, S])
        w_ln = sb("w_ln", [S, RANK])
        xs = [sb(f"xs{i}", [S, D]) for i in range(2)]
        xn = [sb(f"xn{i}", [S, D]) for i in range(2)]
        norm = LayerNorm(ctx, S)
        minus_half = sb("minus_half", [S, 1])
        half_ready = ctx.sem("minus_half_ready")
        xh = [sb(f"xh{i}", [P, KD, S], F32R) for i in range(2)]
        xl = [sb(f"xl{i}", [P, KD, S], F32R) for i in range(2)]
        sq = sb("sq", [S, RANK])
        ms = sb("ms", [S, 2])
        rstd = sb("rstd", [S, 1])
        ln = [sb(f"ln{i}", [S, RANK]) for i in range(2)]
        kr = [sb(f"kr{i}", [S, 3, ROPE]) for i in range(2)]
        ps_x = [ctx.bank(f"ps_x{i}", P, KD, S) for i in range(2)]
        ps_l = [ctx.bank(f"ps_l{i}", S, W) for i in range(2)]
        ps_t = [ctx.bank(f"ps_t{i}", P, 3, S) for i in range(2)]
        id_ready = ctx.sem("id_ready")
        ticks = ctx.sem("ticks")
        w_in = ctx.sem("lnw_loaded")
        zeros = ctx.sem("kr_zeros")
        x_in = [ctx.ev(f"x_loaded{i}", 1, step=16) for i in range(2)]
        normed = ev("x_normed", 1, 2)
        x_turned = ev("x_turned", 1)
        hi, lo = ev("x_hi", 1), ev("x_lo", 1)
        put = [ctx.ev(f"xT_stored{i}", 2, 2, 16) for i in range(2)]
        lat_mm = ev("lat_products", 1)
        squared = ev("lat_squared", 1)
        rms_in = ev("lat_mean_square", 1)
        rms = ev("lat_rstd", 1, 1)
        lat_ready = ev("lat_normed", 1)
        kr_ready = ev("kr_copied", 1)
        v_kept = ev("lat_v_kept", 1, 2)
        turned = ev("lat_turned", 1)
        kept = ev("lat_kept", 1, 2)
        block = ctx.enter_context(nc.Block())

        @block.sync
        def _(sp):
            sp.dma_start(w_ln[:, :], lnw).then_inc(w_in, 16)
            for i in range(2):
                put[i].open(sp)

            def body(b, par):
                wait(sp, normed, b, -2)
                sp.dma_start(xs[par][:, :], x[b]).then_inc(x_in[par].sem, 16)

            def store(b, h, par):
                cols = bass.ds(b * S, S)
                wait(sp, lo, b)
                sp.dma_start(xT_hi[:, :, cols], xh[par][:, :, :].bitcast(F32)).then_inc(put[par].sem, 16)
                sp.dma_start(xT_lo[:, :, cols], xl[par][:, :, :].bitcast(F32)).then_inc(put[par].sem, 16)

            body(0, 0)
            body(1, 1)
            with sp.Fori(0, B // 2 - 1) as h:
                for par in range(2):
                    body(h * 2 + 2 + par, par)
                    store(h * 2 + par, h, par)
            for par in range(2):
                store(B - 2 + par, B // 2 - 1, par)
            for par in range(2):
                sp.wait_ge(put[par].sem, put[par].at(B // 2 - 1, 1))

        @block.gpsimd
        def _(pool):
            identity(pool, ident[:, :], id_ready)
            for i in range(2):
                pool.memset(kr[i][:, :, :], 0.0).then_inc(zeros, 1)
            exponent(pool, minus_half[:, :], half_ready)
            v_kept.open(pool)
            rms.open(pool)

            def body(b, par, last=False):
                if not last:
                    norm.root(pool, b + 1, minus_half)
                wait(pool, rms_in, b)
                pool.tensor_tensor(rstd[:, :], ms[:, 1:2], minus_half[:, :], ALU.pow).then_inc(rms.sem, 1)
                wait(pool, lat_ready, b)
                carry(pool, b, ticks)
                pool.tensor_copy(lat_v[:, b, :], ln[par][:, :]).then_inc(v_kept.sem, 1)

            norm.root(pool, 0, minus_half)
            with pool.Fori(0, B // 2 - 1) as h:
                body(h * 2, 0)
                body(h * 2 + 1, 1)
            body(B - 2, 0)
            body(B - 1, 1, last=True)

        @block.vector
        def _(dve):
            normed.open(dve)
            dve.wait_ge(w_in, 16)
            dve.wait_ge(zeros, 2)

            def layer_norm(b, h, par):
                wait(dve, x_in[par], h)
                norm.vector(dve, b, xn[par][:, :], xs[par][:, :]).then_inc(normed.sem, 1)

            def low(b, h, par):
                wait(dve, hi, b)
                wait(dve, put[par], h, -1)
                dve.tensor_tensor(xl[par][:, :, :], ps_x[par][:, :, :], xh[par][:, :, :], ALU.subtract).then_inc(lo.sem, 1)

            def latent(b, par):
                wait(dve, squared, b)
                dve.tensor_scalar(ms[:, 1:2], ms[:, 0:1], 1.0 / RANK, RMS_EPS, ALU.mult, ALU.add).then_inc(rms_in.sem, 1)
                wait(dve, rms, b)
                wait(dve, v_kept, b, -2)
                wait(dve, kept, b, -2)
                dve.scalar_tensor_tensor(ln[par][:, :], ps_l[par][:, 0:RANK], rstd[:, 0:1], w_ln[:, :],
                                         ALU.mult, ALU.mult).then_inc(lat_ready.sem, 1)
                dve.tensor_copy(kr[par][:, 1, :], ps_l[par][:, RANK:W]).then_inc(kr_ready.sem, 1)

            def body(b, h, par, last=False):
                if not last:
                    layer_norm(b + 1, h + par, 1 - par)
                latent(b, par)
                if not last:
                    low(b + 1, h + par, 1 - par)

            layer_norm(0, 0, 0)
            low(0, 0, 0)
            with dve.Fori(0, B // 2 - 1) as h:
                body(h * 2, h, 0)
                body(h * 2 + 1, h, 1)
            body(B - 2, B // 2 - 1, 0)
            body(B - 1, B // 2 - 1, 1, last=True)

        @block.scalar
        def _(act):
            kept.open(act)

            def high(b, h, par):
                wait(act, x_turned, b)
                wait(act, put[par], h, -1)
                act.activation(xh[par][:, :, :], ps_x[par][:, :, :], ACT.Copy).then_inc(hi.sem, 1)

            def body(b, h, par, last=False):
                wait(act, lat_mm, b)
                wait(act, rms, b, -1)
                act.activation(sq[:, :], ps_l[par][:, 0:RANK], ACT.Square, accum_out=ms[:, 0:1]).then_inc(squared.sem, 1)
                if not last:
                    high(b + 1, h + par, 1 - par)
                wait(act, turned, b)
                act.activation(lat_kT[:, :, bass.ds(b * S, S)], ps_t[par][:, :, :], ACT.Copy).then_inc(kept.sem, 1)

            high(0, 0, 0)
            with act.Fori(0, B // 2 - 1) as h:
                body(h * 2, h, 0)
                body(h * 2 + 1, h, 1)
            body(B - 2, B // 2 - 1, 0)
            body(B - 1, B // 2 - 1, 1, last=True)

        @block.tensor
        def _(pe):
            pe.wait_ge(id_ready, 2)

            def turn_x(b, par):
                wait(pe, normed, b)
                if not (isinstance(b, int) and b < 2):
                    wait(pe, lo, b, -2)
                for k in range(KD):
                    mm = pe.transpose(ps_x[par][:, k, :], xn[par][:, k * P:(k + 1) * P], ident[:, :])
                mm.then_inc(x_turned.sem, 1)

            def body(b, par, last=False):
                wait(pe, lo, b)
                if not (isinstance(b, int) and b < 2):
                    wait(pe, kr_ready, b, -2)
                for k in range(KD):
                    mm = mm3(pe, ps_l[par][:, :], xh[par][:, k, :], xl[par][:, k, :], kva_hi[:, k, :], kva_lo[:, k, :],
                             k == 0, k == KD - 1)
                mm.then_inc(lat_mm.sem, 1)
                if not last:
                    turn_x(b + 1, 1 - par)
                wait(pe, kr_ready, b)
                wait(pe, kept, b, -2)
                pe.transpose(ps_t[par][:, 0, :], ln[par][:, :], ident[:, :])
                pe.transpose(ps_t[par][:, 1, :], kr[par][:, 1:3, :], ident[:, :])
                pe.transpose(ps_t[par][:, 2, :], kr[par][:, 0:2, :], ident[:, :]).then_inc(turned.sem, 1)

            turn_x(0, 0)
            body(0, 0)
            body(1, 1)
            with pe.Fori(1, B // 2 - 1) as h:
                body(h * 2, 0)
                body(h * 2 + 1, 1)
            body(B - 2, 0)
            body(B - 1, 1, last=True)


def self_attention(nc, xT_hi, xT_lo, qf_hi, qf_lo, qr_hi, qr_lo, lat_kT, lat_v, oT):
    NU = NQ * G
    ctx = Phase(nc, "sa")
    with ctx:
        sb = ctx.sb
        ev = ctx.ev
        ident = sb("ident", [S, S])
        mask = sb("mask", [S, S])
        xh = sb("xh", [P, 2, KD, GT], F32R)
        xl = sb("xl", [P, 2, KD, GT], F32R)
        qn = [sb(f"qn{i}", [P, HQ, GT]) for i in range(2)]
        qr = [sb(f"qr{i}", [P, HQ // 2, GT]) for i in range(2)]
        prob = [sb(f"prob{i}", [S, HQ, S]) for i in range(2)]
        top = [sb(f"top{i}", [S, HQ]) for i in range(2)]
        total = [sb(f"total{i}", [S, HQ]) for i in range(2)]
        pT = [sb(f"pT{i}", [S, HQ, S]) for i in range(2)]
        val = [sb(f"val{i}", [S, RANK]) for i in range(2)]
        ov = [sb(f"ov{i}", [P, HQ, S]) for i in range(2)]
        ps_q = [ctx.bank(f"ps_q{i}", P, GT) for i in range(2)]
        ps_s = [ctx.bank(f"ps_s{i}", S, HQ, S) for i in range(2)]
        ps_t = [ctx.bank(f"ps_t{i}", S, HQ, S) for i in range(2)]
        ps_o = [ctx.bank(f"ps_o{i}", P, HQ, S) for i in range(2)]
        consts = ctx.sem("consts")
        ticks = ctx.sem("ticks")
        x_in = ev("xT_loaded", 2, step=16)
        q_mm = ev("q_projected", 6 * NQ, 1)
        qn_ready = ev("q_nope_copied", 4 * NQ)
        qr_ready = ev("q_rot_copied", 2 * NQ)
        scored = ev("scored", NU)
        masked = ev("masked", NU, 2)
        maxed = ev("maxed", NU)
        shifted = ev("shifted", NU)
        exped = ev("exped", NU)
        summed = ev("summed", 2 * NU)
        probs = ev("probs", NU)
        p_turned = ev("p_turned", NU, 2)
        pT_ready = ev("pT_ready", NU, 2)
        val_ready = ev("values_ready", NU)
        pv = ev("weighted", NU, 2)
        o_ready = ev("o_ready", NU, 2)
        o_put = [ev(f"o_stored{i}", NU // 2, 1, 16) for i in range(2)]
        block = ctx.enter_context(nc.Block())
        NG = B // G

        def groups(eng, body):
            with eng.Fori(0, NG - 1) as g:
                body(g, True)
            body(NG - 1, False)

        @block.sync
        def _(sp):
            def load(g, n_free):
                for src, dst in ((xT_hi, xh), (xT_lo, xl)):
                    sp.dma_start(dst[:, bass.ds(n_free, 1), :, :].bitcast(F32),
                                 src[:, :, bass.ds(g * GT, GT)]).then_inc(x_in.sem, 16)

            for i in range(2):
                o_put[i].open(sp)
            load(0, 0)

            def body(g, more):
                for n in range(NU):
                    if n == 0 and more:
                        wait(sp, q_mm, g, -1)
                        wait(sp, x_in, g, 1)
                        load(g + 1, (g + 1) % 2)
                    hq, s = n // G, n % G
                    wait(sp, o_ready, g, n)
                    sp.dma_start(oT[:, hq * HQ:(hq + 1) * HQ, bass.ds(g * GT + s * S, S)], ov[n % 2][:, :, :])\
                        .then_inc(o_put[n % 2].sem, 16)

            groups(sp, body)
            for i in range(2):
                sp.wait_ge(o_put[i].sem, o_put[i].at(NG - 1, NU // 2 - 1))

        @block.gpsimd
        def _(pool):
            identity(pool, ident[:, :], consts)
            pool.memset(mask[:, :], 0.0).then_inc(consts, 1)
            pool.wait_ge(consts, 3)
            pool.affine_select(out=mask[:, :], in_=mask[:, :], compare_op=ALU.is_ge, fill=MASKED, base=0,
                               pattern=[[-1, S]], channel_multiplier=1).then_inc(consts, 1)

            def body(g, more):
                for n in range(NU):
                    wait(pool, pv, g, n - 2)
                    carry(pool, g, ticks)
                    pool.tensor_copy(val[n % 2][:, :], lat_v[:, g * G + n % G, :]).then_inc(val_ready.sem, 1)

            groups(pool, body)

        @block.tensor
        def _(pe):
            pe.wait_ge(consts, 4)
            p_turned.open(pe)
            pv.open(pe)
            q_mm.open(pe)

            def project(g, hq, j, rot):
                u = (0, 2, 3, 5)[j] if not rot else (1, 4)[j]
                first = isinstance(g, int) and g == 0 and hq == 0
                if u == 3 or (u == 0 and not first):
                    wait(pe, qr_ready, g, 2 * hq + (0 if u else -1))
                elif u != 0 and not (u == 1 and first):
                    wait(pe, qn_ready, g, 4 * hq + {1: -1, 2: 0, 4: 1, 5: 2}[u])
                if u == 0 and hq == 0:
                    wait(pe, x_in, g, 1)
                w_hi, w_lo, w = (qr_hi, qr_lo, P) if rot else (qf_hi, qf_lo, RANK)
                for k in range(KD):
                    c0 = (2 * hq + j) * P if rot else 0
                    a_hi = w_hi[:, k, c0:c0 + P] if rot else w_hi[:, k, hq * HQ + j, :]
                    a_lo = w_lo[:, k, c0:c0 + P] if rot else w_lo[:, k, hq * HQ + j, :]
                    slot = g % 2
                    mm = mm3(pe, ps_q[u % 2][:, :], a_hi, a_lo, xh[:, slot, k, :], xl[:, slot, k, :],
                             k == 0, k == KD - 1)
                mm.then_inc(q_mm.sem, 1)

            def score(g, n):
                hq, s = n // G, n % G
                if s == 0:
                    wait(pe, qn_ready, g, 4 * hq + 3)
                    wait(pe, qr_ready, g, 2 * hq + 1)
                wait(pe, masked, g, n - 2)
                for j in range(HQ):
                    cols = slice(s * S, (s + 1) * S)
                    keys = lambda c: lat_kT[:, c, bass.ds(g * GT + s * S, S)]
                    pe.matmul(ps_s[n % 2][:, j, :], qn[hq % 2][:, j, cols], keys(0), start=True, stop=False)
                    mm = pe.matmul(ps_s[n % 2][:, j, :], qr[hq % 2][:, j // 2, cols], keys(1 + j % 2),
                                   start=False, stop=True)
                mm.then_inc(scored.sem, 1)

            def turn(g, n):
                wait(pe, probs, g, n)
                wait(pe, pT_ready, g, n - 2)
                for j in range(HQ):
                    mm = pe.transpose(ps_t[n % 2][:, j, :], prob[n % 2][:, j, :], ident[:, :])
                mm.then_inc(p_turned.sem, 1)

            def weigh(g, n):
                wait(pe, pT_ready, g, n)
                wait(pe, val_ready, g, n)
                wait(pe, o_ready, g, n - 2)
                pe.matmul(ps_o[n % 2][:, :, :], val[n % 2][:, :], pT[n % 2][:, :, :], start=True, stop=True)\
                    .then_inc(pv.sem, 1)

            def queries(g):
                for j in range(HQ):
                    project(g, 0, j, False)
                    if j % 2 == 0:
                        project(g, 0, j // 2, True)

            def body(g, more):
                for n in range(NU):
                    hq, s = n // G, n % G
                    score(g, n)
                    if n:
                        turn(g, n - 1)
                    if hq + 1 < NQ:
                        project(g, hq + 1, s, False)
                    if n:
                        weigh(g, n - 1)
                    if hq + 1 < NQ and s % 2 == 0:
                        project(g, hq + 1, s // 2, True)
                if more:
                    queries(g + 1)
                turn(g, NU - 1)
                weigh(g, NU - 1)

            queries(0)
            groups(pe, body)

        @block.scalar
        def _(act):
            pT_ready.open(act)
            o_ready.open(act)

            def query(g, hq, j):
                wait(act, q_mm, g, 6 * hq + (0, 2, 3, 5)[j])
                act.activation(qn[hq % 2][:, j, :], ps_q[(0, 2, 3, 5)[j] % 2][:, :], ACT.Copy).then_inc(qn_ready.sem, 1)

            def exp(g, n):
                wait(act, shifted, g, n)
                act.activation(prob[n % 2][:, :, :], prob[n % 2][:, :, :], ACT.Exp, scale=MLA_SCALE).then_inc(exped.sem, 1)

            def copy_pT(g, n):
                wait(act, p_turned, g, n)
                wait(act, pv, g, n - 2)
                act.activation(pT[n % 2][:, :, :], ps_t[n % 2][:, :, :], ACT.Copy).then_inc(pT_ready.sem, 1)

            def copy_o(g, n):
                wait(act, pv, g, n)
                wait(act, o_put[n % 2], g, n // 2 - 1)
                act.activation(ov[n % 2][:, :, :], ps_o[n % 2][:, :, :], ACT.Copy).then_inc(o_ready.sem, 1)

            def body(g, more):
                for n in range(NU):
                    hq, s = n // G, n % G
                    if n:
                        copy_pT(g, n - 1)
                    if hq + 1 < NQ:
                        query(g, hq + 1, s)
                    exp(g, n)
                    if n:
                        copy_o(g, n - 1)
                if more:
                    for j in range(HQ):
                        query(g + 1, 0, j)
                copy_pT(g, NU - 1)
                copy_o(g, NU - 1)

            for j in range(HQ):
                query(0, 0, j)
            groups(act, body)

        @block.vector
        def _(dve):
            masked.open(dve)
            dve.wait_ge(consts, 4)

            def query(g, hq, j):
                wait(dve, q_mm, g, 6 * hq + (1, 4)[j])
                dve.tensor_copy(qr[hq % 2][:, j, :], ps_q[(1, 4)[j] % 2][:, :]).then_inc(qr_ready.sem, 1)

            def softmax(g, n):
                p, mx, sm = prob[n % 2], top[n % 2], total[n % 2]
                wait(dve, scored, g, n)
                wait(dve, p_turned, g, n - 2)
                dve.tensor_tensor(p[:, :, :], ps_s[n % 2][:, :, :], over_heads(mask[:, :], HQ), ALU.add).then_inc(masked.sem, 1)
                wait(dve, masked, g, n)
                dve.tensor_reduce(mx[:, :], p[:, :, :], AX.X, ALU.max).then_inc(maxed.sem, 1)
                wait(dve, maxed, g, n)
                dve.tensor_tensor(p[:, :, :], p[:, :, :], along(mx[:, :], S), ALU.subtract).then_inc(shifted.sem, 1)

            def divide(g, n):
                p, sm = prob[n % 2], total[n % 2]
                wait(dve, exped, g, n)
                dve.tensor_reduce(sm[:, :], p[:, :, :], AX.X, ALU.add).then_inc(summed.sem, 1)
                wait(dve, summed, g, 2 * n)
                dve.reciprocal(sm[:, :], sm[:, :]).then_inc(summed.sem, 1)
                wait(dve, summed, g, 2 * n + 1)
                dve.tensor_tensor(p[:, :, :], p[:, :, :], along(sm[:, :], S), ALU.mult).then_inc(probs.sem, 1)

            def body(g, more):
                for n in range(NU):
                    hq, s = n // G, n % G
                    softmax(g, n)
                    divide(g, n)
                    if hq + 1 < NQ and s % 2 == 0:
                        query(g, hq + 1, s // 2)
                if more:
                    query(g + 1, 0, 0)
                    query(g + 1, 0, 1)

            query(0, 0, 0)
            query(0, 0, 1)
            groups(dve, body)


class RopeTables:

    HF = HD // 2
    ROUND = 1.5 * 2.0 ** 23
    STEPS = 7

    def __init__(self, ctx, pos_ctx, pos_x, inv_freq, k_norm_w, q_norm_w, tables):
        sb, HF = ctx.sb, self.HF
        self.src = pos_ctx, pos_x, inv_freq, k_norm_w, q_norm_w
        self.tables = tables
        self.pos_i = sb("pos_i", [P, 4, B], I32)
        self.pos = sb("pos", [P, B, 4])
        self.freq = sb("freq", [P, HF])
        self.w = [sb(f"{n}_norm_w", [P, HD]) for n in "kq"]
        self.w_rot = [sb(f"{n}_norm_w_rot", [P, HD]) for n in "kq"]
        self.turns = sb("turns", [P, 4, HF])
        self.ang = [sb(f"ang{i}", [P, 4, HF]) for i in range(2)]
        self.sin = [sb(f"sin{i}", [P, 4, HF]) for i in range(2)]
        self.cos = [sb(f"cos{i}", [P, 4, HF]) for i in range(2)]
        self.tab = [sb(f"tab{i}", [P, 5, 2, HD]) for i in range(2)]
        self.loaded, self.zeroed, self.ready = (ctx.sem(n) for n in ("rope_loaded", "rope_zeroed", "rope_ready"))
        self.reduced = ctx.ev("angle_steps", self.STEPS)
        self.sines = ctx.ev("sines", 2)
        self.cosine = ctx.ev("cosine_steps", 2)
        self.made = ctx.ev("tables_made", 1)
        self.put = [ctx.ev(f"tables_stored{i}", 1, 1, 16) for i in range(2)]
        self.ticks = ctx.sem("rope_ticks")

    def load(self, sp):
        pos_ctx, pos_x, inv_freq, k_norm_w, q_norm_w = self.src
        for i in range(2):
            self.put[i].open(sp)
        sp.wait_ge(self.zeroed, 1)
        sp.dma_start(self.pos_i[0:CT, 0:3, :], pos_ctx).then_inc(self.loaded, 16)
        sp.dma_start(self.pos_i[0:S, 3, :], pos_x).then_inc(self.loaded, 16)
        sp.dma_start(self.freq[:, :], inv_freq).then_inc(self.loaded, 16)
        sp.dma_start(self.w[0][:, :], k_norm_w).then_inc(self.loaded, 16)
        sp.dma_start(self.w[1][:, :], q_norm_w).then_inc(self.loaded, 16)

    def store(self, sp, b, par):
        wait(sp, self.made, b)
        carry(sp, b, self.ticks)
        sp.dma_start(self.tables[b], self.tab[par][:, :, :, :]).then_inc(self.put[par].sem, 16)

    def prepare(self, dve):
        HF = self.HF
        dve.memset(self.pos_i[:, :, :], 0).then_inc(self.zeroed, 1)
        dve.wait_ge(self.loaded, 80)
        dve.tensor_copy(self.pos[:, :, :], self.pos_i[:, :, :].rearrange("p t b -> p b t")).then_inc(self.ready, 1)
        for w, rot in zip(self.w, self.w_rot):
            dve.tensor_scalar(rot[:, 0:HF], w[:, HF:HD], -1.0, None, ALU.mult).then_inc(self.ready, 1)
            dve.tensor_copy(rot[:, HF:HD], w[:, 0:HF]).then_inc(self.ready, 1)
        dve.wait_ge(self.ready, 5)

    def angles(self, dve, b, par):
        HF, step = self.HF, [0]
        ang, turns = self.ang[par][:, :, :], self.turns[:, :, :]

        def then(ins):
            ins.then_inc(self.reduced.sem, 1)
            wait(dve, self.reduced, b, step[0])
            step[0] += 1

        if not isinstance(b, int) or b > 1:
            wait(dve, self.sines, b, -3)
        pos = self.pos[:, bass.ds(b, 1), :].rearrange("p o t -> p (o t)")
        then(dve.tensor_tensor(ang, along(pos, HF), over_heads(self.freq[:, :], 4), ALU.mult))
        then(dve.tensor_scalar(turns, ang, float(1 / (2 * np.pi)), self.ROUND, ALU.mult, ALU.add))
        then(dve.tensor_scalar(turns, turns, self.ROUND, -PI2[0], ALU.subtract, ALU.mult))
        then(dve.tensor_tensor(ang, ang, turns, ALU.add))
        then(dve.scalar_tensor_tensor(ang, turns, PI2[1] / PI2[0], ang, ALU.mult, ALU.add))
        then(dve.tensor_scalar(ang, ang, 3.1415925, None, ALU.min))
        then(dve.tensor_scalar(ang, ang, -3.1415925, None, ALU.max))

    def sine(self, act, b, par):
        wait(act, self.reduced, b, self.STEPS - 1)
        if not isinstance(b, int) or b > 1:
            wait(act, self.made, b, -2)
        ang = self.ang[par][:, :, :]
        act.activation(self.sin[par][:, :, :], ang, ACT.Sin).then_inc(self.sines.sem, 1)
        act.activation(self.cos[par][:, :, :], ang, ACT.Sin, scale=0.5).then_inc(self.sines.sem, 1)

    def make(self, pool, b, h, par):
        sin, cos = self.sin[par], self.cos[par]
        if isinstance(b, int) and b == 0:
            pool.wait_ge(self.ready, 5)
        wait(pool, self.sines, b, 1)
        pool.tensor_tensor(cos[:, :, :], cos[:, :, :], cos[:, :, :], ALU.mult).then_inc(self.cosine.sem, 1)
        wait(pool, self.cosine, b, 0)
        carry(pool, b, self.ticks)
        pool.tensor_scalar(cos[:, :, :], cos[:, :, :], -2.0, 1.0, ALU.mult, ALU.add).then_inc(self.cosine.sem, 1)
        wait(pool, self.cosine, b, 1)
        wait(pool, self.put[par], h, -1)
        for tiles, src, i in ((slice(0, 4), slice(0, 4), 0), (slice(4, 5), slice(3, 4), 1)):
            n = tiles.stop - tiles.start
            for c, part, w in ((0, cos, self.w[i]), (1, sin, self.w_rot[i])):
                angles = part[:, src, :].unsqueeze(2).broadcast_to((P, n, 2, self.HF))
                weights = w[:, :].rearrange("p (h f) -> p h f", h=2).unsqueeze(1).broadcast_to((P, n, 2, self.HF))
                out = self.tab[par][:, tiles, c, :].rearrange("p t (h f) -> p t h f", h=2)
                ins = pool.tensor_tensor(out, angles, weights, ALU.mult)
        ins.then_inc(self.made.sem, 1)


def project_out(nc, oT, w_src, res, store_x, store_xT, rope=None, router=None, keep=None):
    CH = HQ * P
    ctx = Phase(nc, "out2" if router is not None else "out1")
    with ctx:
        sb = ctx.sb
        ev = ctx.ev
        ident = sb("ident", [P, P])
        w_raw = sb("w_raw", [P, 4, D])
        w_hi = sb("w_hi", [P, H, D], F32R)
        w_lo = sb("w_lo", [P, H, D], F32R)
        o_raw = sb("o_raw", [P, NQ, HQ, P])
        o_hi = sb("o_hi", [P, NQ, HQ, P], F32R)
        o_lo = sb("o_lo", [P, NQ, HQ, P], F32R)
        r_in = [sb(f"r_in{i}", [P, D]) for i in range(2)]
        y = [sb(f"y{i}", [P, D]) for i in range(2)]
        yn = [sb(f"yn{i}", [P, D]) for i in range(2)]
        layer = LayerNorm(ctx, P)
        minus_half = sb("minus_half", [P, 1])
        half_ready = ctx.sem("minus_half_ready")
        xh = [sb(f"xh{i}", [P, KD, P], F32R) for i in range(2)]
        xl = [sb(f"xl{i}", [P, KD, P], F32R) for i in range(2)]
        ps_y = [ctx.bank(f"ps_y{i}", P, D) for i in range(2)]
        ps_x = [ctx.bank(f"ps_x{i}", P, KD, P) for i in range(2)]
        ps_r = ctx.bank("ps_r", P, TOTAL)
        id_ready = ctx.sem("id_ready")
        w_in = [ctx.sem(f"w_loaded{i}") for i in range(4)]
        w_hi_ready = ctx.sem("w_hi_ready")
        w_lo_ready = ctx.sem("w_lo_ready")
        o_in = [ev(f"o_loaded{c}", 1, step=16) for c in range(NQ)]
        o_hi_ready, o_lo_ready = ev("o_hi_ready", NQ), ev("o_lo_ready", NQ)
        used = ev("o_used", NQ, NQ)
        r_loaded = [ev(f"r_loaded{i}", 1, step=16) for i in range(2)]
        added = ev("y_added", 1, 2)
        normed = ev("y_normed", 1)
        turned = ev("y_turned", 1, 2)
        hi, lo = ev("x_hi", 1), ev("x_lo", 1)
        y_put = [ev(f"y_stored{i}", 1, 1, 16) for i in range(2)]
        x_put = [ev(f"xT_stored{i}", 2, 2, 16) for i in range(2)]
        ticks = ctx.sem("ticks")
        if rope is not None:
            guest = RopeTables(ctx, *rope)
        if router is not None:
            cls_src, bias_src = router
            acc, shares = keep
            cls = sb("cls", [P, KD, TOTAL])
            cls_hi = sb("cls_hi", [P, KD, TOTAL], F32R)
            cls_lo = sb("cls_lo", [P, KD, TOTAL], F32R)
            bias = sb("bias", [P, TOTAL])
            iota = sb("iota", [P, TOTAL])
            iota_i = sb("iota_i", [P, TOTAL], I32)
            small = sb("small", [P, 4])
            prob = sb("prob", [P, TOTAL])
            biased = sb("biased", [P, TOTAL])
            best = sb("best", [P, 8])
            best_i = sb("best_i", [P, 8], U32)
            best_f = sb("best_f", [P, 8])
            first = sb("first", [P, TOTAL])
            chosen = sb("chosen", [P, TOTAL])
            weight = sb("weight", [P, TOTAL])
            r_src = ctx.sem("router_loaded")
            r_split = ctx.sem("router_split")
            logits = ev("logits", 1)
            r_step = ev("route_step", 12)
            r_exp = ev("route_exp", 1)
            r_done = ev("routed", 1)
        block = ctx.enter_context(nc.Block())

        @block.sync
        def _(sp):
            for i in range(2):
                y_put[i].open(sp)
                x_put[i].open(sp)
            if rope is not None:
                guest.load(sp)
            if router is not None:
                sp.dma_start(cls[:, :, :], cls_src).then_inc(r_src, 16)
                sp.dma_start(bias[:, :], bias_src).then_inc(r_src, 16)

            def load(t, h, par):
                cols = bass.ds(t * P, P)
                for c in range(NQ):
                    if not isinstance(t, int) or t:
                        wait(sp, o_lo_ready, t, c - NQ)
                    sp.dma_start(o_raw[:, c, :, :], oT[:, c * HQ:(c + 1) * HQ, cols]).then_inc(o_in[c].sem, 16)
                wait(sp, added, t, -2)
                sp.dma_start(r_in[par][:, :], res[cols, :]).then_inc(r_loaded[par].sem, 16)

            def store(t, h, par):
                cols = bass.ds(t * P, P)
                if store_x is not None:
                    wait(sp, added, t)
                    sp.dma_start(store_x[cols, :], y[par][:, :]).then_inc(y_put[par].sem, 16)
                wait(sp, lo, t)
                carry(sp, t, ticks)
                dst_hi, dst_lo = store_xT
                sp.dma_start(dst_hi[:, :, cols], xh[par][:, :, :].bitcast(F32)).then_inc(x_put[par].sem, 16)
                sp.dma_start(dst_lo[:, :, cols], xl[par][:, :, :].bitcast(F32)).then_inc(x_put[par].sem, 16)

            for h in range(H):
                if h >= 4:
                    sp.wait_ge(w_lo_ready, h - 3)
                sp.dma_start(w_raw[:, h % 4, :], w_src[:, h, :]).then_inc(w_in[h % 4], 16)
                if h % 4 == 3 and h < 4:
                    load(0, 0, 0)
            load(1, 0, 1)
            with sp.Fori(0, TT // 2 - 1) as h:
                for par in range(2):
                    load(h * 2 + 2 + par, h + 1, par)
                    store(h * 2 + par, h, par)
                    if rope is not None:
                        guest.store(sp, h * 2 + par, par)
            for par in range(2):
                store(TT - 2 + par, TT // 2 - 1, par)
                if rope is not None:
                    guest.store(sp, TT - 2 + par, par)
            if rope is not None:
                for par in range(2):
                    guest.store(sp, TT + par, par)
            for par in range(2):
                if rope is not None:
                    sp.wait_ge(guest.put[par].sem, guest.put[par].at(B // 2 - 1))
                if store_x is not None:
                    sp.wait_ge(y_put[par].sem, y_put[par].at(TT // 2 - 1))
                sp.wait_ge(x_put[par].sem, x_put[par].at(TT // 2 - 1, 1))

        @block.gpsimd
        def _(pool):
            identity(pool, ident[:, :], id_ready)
            if router is not None:
                pool.iota(iota_i[:, :], pattern=[[1, TOTAL]], base=0, channel_multiplier=0).then_inc(id_ready, 1)
                pool.wait_ge(id_ready, 3)
                pool.tensor_copy(iota[:, :], iota_i[:, :]).then_inc(id_ready, 1)
                pool.wait_ge(r_src, 32)
                pool.tensor_copy(cls_hi[:, :, :], cls[:, :, :]).then_inc(r_split, 1)
                pool.wait_ge(r_split, 1)
                pool.tensor_tensor(cls_lo[:, :, :], cls[:, :, :], cls_hi[:, :, :], ALU.subtract).then_inc(r_split, 1)
            exponent(pool, minus_half[:, :], half_ready)
            if rope is not None:
                guest.make(pool, 0, 0, 0)
            with pool.Fori(0, TT // 2) as h:
                for par in range(2):
                    layer.root(pool, h * 2 + par, minus_half)
                    if rope is not None:
                        guest.make(pool, h * 2 + par + 1, h + par, 1 - par)
            if rope is not None:
                guest.make(pool, B - 1, B // 2 - 1, 1)

        @block.scalar
        def _(act):
            def high(t, c):
                wait(act, o_in[c], t)
                wait(act, used, t, c - NQ)
                act.activation(o_hi[:, c, :, :], o_raw[:, c, :, :], ACT.Copy).then_inc(o_hi_ready.sem, 1)

            def turn(t, h, par):
                wait(act, turned, t)
                wait(act, x_put[par], h, -1)
                act.activation(xh[par][:, :, :], ps_x[par][:, :, :], ACT.Copy).then_inc(hi.sem, 1)

            def route(t):
                wait(act, r_step, t, 0)
                act.activation(prob[:, :], ps_r[:, :], ACT.Exp, bias=small[:, 0:1],
                               accum_out=small[:, 1:2]).then_inc(r_exp.sem, 1)

            def body(t, h, par, ahead=True):
                if ahead:
                    high(t + 2, 0)
                    high(t + 2, 1)
                if router is not None and not (isinstance(t, int) and t == 0):
                    route(t - 1)
                turn(t, h, par)
                if ahead:
                    high(t + 2, 2)
                if rope is not None:
                    guest.sine(act, t + 2, par)
                if ahead:
                    high(t + 2, 3)

            if rope is not None:
                guest.sine(act, 0, 0)
                guest.sine(act, 1, 1)
            for h in range(H):
                act.wait_ge(w_in[h % 4], 16 * (h // 4 + 1))
                act.activation(w_hi[:, h, :], w_raw[:, h % 4, :], ACT.Copy).then_inc(w_hi_ready, 1)
                if h % 4 == 3:
                    high(0, h // 4)
            for c in range(NQ):
                high(1, c)
            for par in range(2):
                body(par, 0, par)
            with act.Fori(1, TT // 2 - 1) as h:
                body(h * 2, h, 0)
                body(h * 2 + 1, h, 1)
            for par in range(2):
                body(TT - 2 + par, TT // 2 - 1, par, ahead=False)
            if router is not None:
                route(TT - 1)

        @block.vector
        def _(dve):
            added.open(dve)

            def low(t, c):
                wait(dve, o_hi_ready, t, c)
                dve.tensor_tensor(o_lo[:, c, :, :], o_raw[:, c, :, :], o_hi[:, c, :, :], ALU.subtract).then_inc(o_lo_ready.sem, 1)

            def norm(t, h, par):
                wait(dve, r_loaded[par], h)
                wait(dve, used, t, NQ - 1)
                if store_x is not None:
                    wait(dve, y_put[par], h, -1)
                if router is not None and not (isinstance(t, int) and t < 2):
                    wait(dve, r_done, t, -2)
                dve.tensor_tensor(y[par][:, :], ps_y[par][:, :], r_in[par][:, :], ALU.add).then_inc(added.sem, 1)
                wait(dve, added, t)
                wait(dve, turned, t, -2)
                layer.vector(dve, t, yn[par][:, :], y[par][:, :]).then_inc(normed.sem, 1)

            def turn(t, h, par):
                wait(dve, hi, t)
                dve.tensor_tensor(xl[par][:, :, :], ps_x[par][:, :, :], xh[par][:, :, :], ALU.subtract).then_inc(lo.sem, 1)

            def route(t, par):
                m, total, inv, back = (small[:, i:i + 1] for i in range(4))

                def then(n, ins):
                    ins.then_inc(r_step.sem, 1)
                    wait(dve, r_step, t, n)

                wait(dve, logits, t)
                then(0, dve.tensor_reduce(m, ps_r[:, :], AX.X, ALU.max, negate=True))
                wait(dve, r_exp, t)
                then(1, dve.reciprocal(inv, total))
                then(2, dve.tensor_scalar(prob[:, :], prob[:, :], inv, None, ALU.mult))
                then(3, dve.tensor_tensor(biased[:, :], prob[:, :], bias[:, :], ALU.add))
                carry(dve, t, ticks)
                then(4, dve.max(best[:, :], biased[:, :]))
                carry(dve, t, ticks)
                then(5, dve.max_index(best_i[:, :], best[:, :], biased[:, :]))
                then(6, dve.tensor_copy(best_f[:, :], best_i[:, :]))
                then(7, dve.tensor_scalar(first[:, :], iota[:, :], best_f[:, 0:1], None, ALU.is_equal))
                then(8, dve.scalar_tensor_tensor(chosen[:, :], iota[:, :], best_f[:, 1:2], first[:, :],
                                                 ALU.is_equal, ALU.add))
                then(9, dve.scalar_tensor_tensor(weight[:, :], chosen[:, :], ROUTE_SCALE, prob[:, :],
                                                 ALU.mult, ALU.mult))
                then(10, dve.tensor_reduce(back, weight[:, E:TOTAL], AX.X, ALU.add))
                then(11, dve.tensor_copy(shares[:, t, :], weight[:, 0:E]))
                dve.scalar_tensor_tensor(acc[:, t, :], yn[par][:, :], back, y[par][:, :], ALU.mult, ALU.add)\
                    .then_inc(r_done.sem, 1)

            def body(t, h, par, ahead=True):
                norm(t, h, par)
                if ahead:
                    low(t + 2, 0)
                    low(t + 2, 1)
                if router is not None and not (isinstance(t, int) and t == 0):
                    route(t - 1, 1 - par)
                turn(t, h, par)
                if rope is not None:
                    guest.angles(dve, t + 2, par)
                if ahead:
                    low(t + 2, 2)
                    low(t + 2, 3)

            if rope is not None:
                guest.prepare(dve)
                guest.angles(dve, 0, 0)
                guest.angles(dve, 1, 1)
            if router is not None:
                dve.wait_ge(r_src, 32)
                dve.wait_ge(id_ready, 4)
            for h in range(H):
                dve.wait_ge(w_hi_ready, h + 1)
                dve.tensor_tensor(w_lo[:, h, :], w_raw[:, h % 4, :], w_hi[:, h, :], ALU.subtract).then_inc(w_lo_ready, 1)
                if h % 4 == 3:
                    low(0, h // 4)
            for c in range(NQ):
                low(1, c)
            for par in range(2):
                body(par, 0, par)
            with dve.Fori(1, TT // 2 - 1) as h:
                body(h * 2, h, 0)
                body(h * 2 + 1, h, 1)
            for par in range(2):
                body(TT - 2 + par, TT // 2 - 1, par, ahead=False)
            if router is not None:
                route(TT - 1, 1)

        @block.tensor
        def _(pe):
            used.open(pe)
            turned.open(pe)
            pe.wait_ge(id_ready, 2)

            def project(t, par, chunks):
                for c in chunks:
                    wait(pe, o_lo_ready, t, c)
                    if c == 0 and (not isinstance(t, int) or t > 1):
                        wait(pe, added, t, -2)
                    for j in range(HQ):
                        h = c * HQ + j
                        if isinstance(t, int) and t == 0:
                            pe.wait_ge(w_lo_ready, h + 1)
                        mm = mm3(pe, ps_y[par][:, :], o_hi[:, c, j, :], o_lo[:, c, j, :], w_hi[:, h, :], w_lo[:, h, :],
                                 h == 0, h == H - 1)
                    mm.then_inc(used.sem, 1)

            def turn(t, par):
                wait(pe, normed, t)
                if not isinstance(t, int) or t > 1:
                    wait(pe, lo, t, -2)
                for k in range(KD):
                    mm = pe.transpose(ps_x[par][:, k, :], yn[par][:, k * P:(k + 1) * P], ident[:, :])
                mm.then_inc(turned.sem, 1)

            def route(t, par):
                wait(pe, lo, t)
                if isinstance(t, int) and t == 0:
                    pe.wait_ge(r_split, 2)
                else:
                    wait(pe, r_done, t, -1)
                for k in range(KD):
                    mm = mm3(pe, ps_r[:, :], xh[par][:, k, :], xl[par][:, k, :], cls_hi[:, k, :], cls_lo[:, k, :],
                             k == 0, k == KD - 1)
                mm.then_inc(logits.sem, 1)

            def body(t, par, last=False):
                if not last:
                    project(t + 1, 1 - par, (0, 1))
                turn(t, par)
                if not last:
                    project(t + 1, 1 - par, (2, 3))
                if router is not None:
                    route(t, par)

            project(0, 0, range(NQ))
            body(0, 0)
            body(1, 1)
            with pe.Fori(1, TT // 2 - 1) as h:
                body(h * 2, 0)
                body(h * 2 + 1, 1)
            body(TT - 2, 0)
            body(TT - 1, 1, last=True)


def cross_attention(nc, ctxT, xT_hi, xT_lo, wqT, wkT, wvT, tables, oT):
    M = (CT, CT, CT, S)
    HF = HD // 2
    ctx = Phase(nc, "ca")
    with ctx:
        sb = ctx.sb
        ev = ctx.ev
        ident = sb("ident", [P, P])
        NW = (H * HD + 2 * D) // D
        w_hi = sb("w_hi", [P, NW, KD, D], F32R)
        w_lo = sb("w_lo", [P, NW, KD, D], F32R)
        w_src = [wqT[:, :, i * D:(i + 1) * D] for i in range(4)] + [wkT, wvT]
        W_ORDER = (0, 4, 5, 1, 2, 3)
        WK, WV = 4, 5
        c_raw = sb("c_raw", [P, KD, C])
        c_hi = [sb(f"c_hi{i}", [P, KD, CT], F32R) for i in range(2)]
        c_lo = [sb(f"c_lo{i}", [P, KD, CT], F32R) for i in range(2)]
        xh = [sb(f"xh{i}", [P, KD, S], F32R) for i in range(2)]
        xl = [sb(f"xl{i}", [P, KD, S], F32R) for i in range(2)]
        tab = [sb(f"tab{i}", [P, 5, 2, HD]) for i in range(2)]
        qT = sb("qT", [P, KVH, HQ, S])
        kT = [sb(f"kT{i}", [P, KVH, KV]) for i in range(2)]
        v = [sb(f"v{i}", [P, 4, KVH * HD]) for i in range(2)]
        prob = [sb(f"prob{j}", [S, 4 * CT]) for j in range(HQ)]
        top = sb("top", [S, HQ])
        down = sb("down", [S, HQ])
        total = sb("total", [S, HQ])
        inv = sb("inv", [S, HQ])
        pT = [sb(f"pT{i}", [P, 4, HQ, S]) for i in range(2)]
        ov = [sb(f"ov{i}", [P, HQ, S]) for i in range(2)]
        sq = sb("sq", [P, D])
        q1, q2, k1, k2 = (sb(n, [P, D]) for n in ("q1", "q2", "k1", "k2"))
        ssum = sb("ssum", [P, 2, HQ])
        k_rstd = sb("k_rstd", [P, HQ])
        minus_half = sb("minus_half", [P, HQ])
        half_ready = ctx.sem("minus_half_ready")
        q_scale = [sb(f"q_scale{i}", [S, KVH, HQ]) for i in range(2)]
        ps_p = [ctx.bank(f"ps_p{i}", P, D) for i in range(2)]
        ps_s = [ctx.bank(f"ps_s{i}", S, KV) for i in range(2)]
        ps_t = [ctx.bank(f"ps_t{i}", P, 4, S) for i in range(2)]
        ps_r = ctx.bank("ps_r", P, HQ * P)
        ps_o = ctx.bank("ps_o", P, HQ, S)
        id_ready = ctx.sem("id_ready")
        padded = ctx.sem("prob_padded")
        w_in = [ctx.sem(f"w_loaded{i}") for i in range(2)]
        w_hi_ready = ctx.sem("w_hi_ready")
        w_lo_ready = ctx.sem("w_lo_ready")
        c_in = ev("ctx_loaded", 1, step=16)
        c_hi_ready, c_lo_ready = ev("ctx_hi", 3), ev("ctx_lo", 3)
        x_in = [ctx.sem(f"x_loaded{i}") for i in range(2)]
        q_mm, k_mm, v_mm = ev("q_projected", 4), ev("k_projected", 4), ev("v_projected", 4)
        q_sq, k_sq = ev("q_squared", 4), ev("k_squared", 4)
        q_rot, k_rot = ev("q_products", 4), ev("k_products", 4)
        q_sum, k_sum = ev("q_squares_summed", 8, 1), ev("k_squares_summed", 8, 1)
        q_scaled, k_scaled = ev("q_scale_ready", 4), ev("k_rstd_ready", 4)
        q_added, k_added = ev("q_rotated", 4), ev("k_added", 4)
        k_normed = ev("k_rotated", 4)
        q_turned, k_turned = ev("q_turned", 4), ev("k_turned", 4)
        qT_ready, kT_ready = ev("qT_ready", 4), ev("kT_ready", 4)
        v_ready = ev("v_ready", 4)
        N = KVH * HQ
        scored = ev("scored", N)
        maxed, shifted = ev("maxed", N), ev("shift_ready", N)
        exped = ev("exped", N, 2)
        inverted = ev("inverted", N)
        probs = ev("probs", N)
        p_turned = ev("p_turned", N, HQ)
        pT_ready = ev("pT_ready", N, 2)
        pv = ev("weighted", 4, 8)
        o_ready = ev("o_ready", 4, 1)
        o_put = [ev(f"o_stored{i}", 2, 1, 16) for i in range(2)]
        block = ctx.enter_context(nc.Block())

        def inputs(eng, b, par):
            eng.wait_ge(x_in[par], b * 24 + 48 - 24 * par)

        def batches(eng, project, step):
            for i in range(4):
                project(0, i, 0)
            with eng.Fori(0, B // 2 - 1) as h:
                for par in range(2):
                    for i in range(4):
                        step(h * 2 + par, i, par, True)
            for i in range(4):
                step(B - 2, i, 0, True)
            for i in range(4):
                step(B - 1, i, 1, False)

        @block.sync
        def _(sp):
            for i in range(2):
                o_put[i].open(sp)

            def load(b, h, par):
                cols = bass.ds(b * S, S)
                if not isinstance(b, int) or b:
                    wait(sp, c_lo_ready, b, -1)
                sp.dma_start(c_raw[:, :, :], ctxT[b]).then_inc(c_in.sem, 16)
                if not isinstance(b, int) or b > 1:
                    wait(sp, v_mm, b, -5)
                    wait(sp, q_mm, b, -5)
                    wait(sp, q_rot, b, -5)
                    wait(sp, k_rot, b, -5)
                sp.dma_start(xh[par][:, :, :].bitcast(F32), xT_hi[:, :, cols]).then_inc(x_in[par], 16)
                sp.dma_start(xl[par][:, :, :].bitcast(F32), xT_lo[:, :, cols]).then_inc(x_in[par], 16)
                sp.dma_start(tab[par][:, :, :, :], tables[b]).then_inc(x_in[par], 16)

            def store(b, i):
                wait(sp, o_ready, b, i)
                sp.dma_start(oT[:, i * HQ:(i + 1) * HQ, bass.ds(b * S, S)], ov[i % 2][:, :, :])\
                    .then_inc(o_put[i % 2].sem, 16)

            load(0, 0, 0)
            for n in range(NW):
                if n >= 2:
                    sp.wait_ge(w_lo_ready, n - 1)
                sp.dma_start(v[n % 2][:, :, :], w_src[W_ORDER[n]]).then_inc(w_in[n % 2], 16)
            load(1, 0, 1)
            with sp.Fori(0, B // 2 - 1) as h:
                for par in range(2):
                    store(h * 2 + par, 0)
                    store(h * 2 + par, 1)
                    load(h * 2 + par + 2, h + 1, par)
                    store(h * 2 + par, 2)
                    store(h * 2 + par, 3)
            for b in (B - 2, B - 1):
                for i in range(4):
                    store(b, i)
            for i in range(2):
                sp.wait_ge(o_put[i].sem, o_put[i].at(B - 1, 1))

        @block.gpsimd
        def _(pool):
            identity(pool, ident[:, :], id_ready)
            exponent(pool, minus_half[:, :], half_ready)
            for j in range(HQ):
                pool.memset(prob[j][:, KV:4 * CT], 0.0).then_inc(padded, 1)

            def low(b, t, par):
                wait(pool, c_hi_ready, b, t)
                slot = (par + t) % 2
                pool.tensor_tensor(c_lo[slot][:, :, :], c_raw[:, :, t * CT:(t + 1) * CT], c_hi[slot][:, :, :],
                                   ALU.subtract).then_inc(c_lo_ready.sem, 1)

            def project(b, i, par):
                m = M[i]
                wait(pool, q_sum, b, 2 * i + 1)
                pool.tensor_tensor(q_scale[par][:, i, :], ssum[0:S, 0, :], minus_half[0:S, :], ALU.pow).then_inc(q_scaled.sem, 1)
                wait(pool, q_rot, b, i)
                pool.tensor_tensor(q1[0:S, :], q1[0:S, :], q2[0:S, :], ALU.add).then_inc(q_added.sem, 1)
                wait(pool, k_rot, b, i)
                pool.tensor_tensor(k1[0:m, :], k1[0:m, :], k2[0:m, :], ALU.add).then_inc(k_added.sem, 1)
                wait(pool, k_sum, b, 2 * i + 1)
                pool.tensor_tensor(k_rstd[0:m, :], ssum[0:m, 1, :], minus_half[0:m, :], ALU.pow).then_inc(k_scaled.sem, 1)
                wait(pool, k_scaled, b, i)
                wait(pool, k_added, b, i)
                heads = k1[0:m, :].rearrange("p (h d) -> p h d", h=KVH)
                pool.tensor_tensor(heads, heads, along(k_rstd[0:m, :], HD), ALU.mult).then_inc(k_normed.sem, 1)
                if i in (0, 1):
                    low(b, i + 1, par)
                elif i == 3 and not (isinstance(b, int) and b == B - 1):
                    low(b + 1, 0, 1 - par)

            def step(b, i, par, more):
                if more:
                    project(b + 1, i, 1 - par)

            low(0, 0, 0)
            batches(pool, project, step)

        @block.tensor
        def _(pe):
            pe.wait_ge(id_ready, 2)
            pe.wait_ge(padded, HQ)
            p_turned.open(pe)
            pv.open(pe)
            first = lambda b: isinstance(b, int) and b == 0

            def weights(b, c):
                if first(b):
                    pe.wait_ge(w_lo_ready, W_ORDER.index(c) + 1)

            def project(b, i, unit, par):
                out = ps_p[(3 * i + unit) % 2]
                done = (q_mm, k_mm, v_mm)[unit]
                c = (i, WK, WV)[unit]
                weights(b, c)
                if i == 0 and unit == 0:
                    inputs(pe, b, par)
                if unit == 0 or i == 3:
                    m, a_hi, a_lo = S, xh[par], xl[par]
                else:
                    slot = (par + i) % 2
                    m, a_hi, a_lo = CT, c_hi[slot], c_lo[slot]
                    wait(pe, c_lo_ready, b, i)
                if unit == 2:
                    wait(pe, q_rot, b, i)
                    wait(pe, q_sq, b, i)
                elif unit == 0 and not (first(b) and i == 0):
                    wait(pe, k_rot, b, i - 1)
                    wait(pe, k_sq, b, i - 1)
                elif unit == 1 and not (first(b) and i == 0):
                    wait(pe, v_ready, b, i - 1)
                for k in range(KD):
                    mm = mm3(pe, out[0:m, :], a_hi[:, k, :], a_lo[:, k, :], w_hi[:, c, k, :], w_lo[:, c, k, :],
                             k == 0, k == KD - 1)
                mm.then_inc(done.sem, 1)

            def turn_q(b, i):
                wait(pe, q_added, b, i)
                if not (first(b) and i == 0):
                    wait(pe, kT_ready, b, i - 1)
                for j in range(HQ):
                    mm = pe.transpose(ps_r[:, j * S:(j + 1) * S], q1[0:S, j * HD:(j + 1) * HD], ident[0:S, 0:S])
                mm.then_inc(q_turned.sem, 1)

            def turn_k(b, i):
                m = M[i]
                wait(pe, k_normed, b, i)
                wait(pe, qT_ready, b, i)
                for j in range(KVH):
                    mm = pe.transpose(ps_r[:, j * m:(j + 1) * m], k1[0:m, j * HD:(j + 1) * HD], ident[0:m, 0:m])
                mm.then_inc(k_turned.sem, 1)

            def score(b, i, j, par):
                if j == 0:
                    wait(pe, qT_ready, b, i)
                    if i == 0:
                        wait(pe, kT_ready, b, 3)
                wait(pe, exped, b, i * HQ + j - 2)
                pe.matmul(ps_s[j % 2][:, :], qT[:, i, j, :], kT[par][:, i, :], start=True, stop=True).then_inc(scored.sem, 1)

            def turn(b, i, j):
                n = i * HQ + j
                wait(pe, probs, b, n)
                wait(pe, pT_ready, b, n - 2)
                for t in range(4):
                    mm = pe.transpose(ps_t[j % 2][0:CT, t, :], prob[j][:, t * CT:(t + 1) * CT], ident[0:S, 0:S])
                mm.then_inc(p_turned.sem, 1)

            def weigh(b, i, par):
                wait(pe, pT_ready, b, i * HQ + HQ - 1)
                if i == 0:
                    wait(pe, v_ready, b, 3)
                if not (first(b) and i == 0):
                    wait(pe, o_ready, b, i - 1)
                for t in range(4):
                    mm = pe.matmul(ps_o[:, :, :], v[par][0:M[t], t, i * HD:(i + 1) * HD], pT[i % 2][0:M[t], t, :, :],
                                   start=(t == 0), stop=(t == 3))
                mm.then_inc(pv.sem, 1)

            def start(b, i, par):
                project(b, i, 0, par)
                project(b, i, 1, par)
                turn_q(b, i)
                project(b, i, 2, par)
                turn_k(b, i)

            def step(b, i, par, more):
                score(b, i, 0, par)
                score(b, i, 1, par)
                if more:
                    project(b + 1, i, 0, 1 - par)
                turn(b, i, 0)
                score(b, i, 2, par)
                turn(b, i, 1)
                score(b, i, 3, par)
                if more:
                    project(b + 1, i, 1, 1 - par)
                turn(b, i, 2)
                turn(b, i, 3)
                if more:
                    turn_q(b + 1, i)
                    project(b + 1, i, 2, 1 - par)
                weigh(b, i, par)
                if more:
                    turn_k(b + 1, i)

            batches(pe, start, step)

        @block.scalar
        def _(act):
            def high(b, t, par):
                wait(act, c_in, b)
                if not (isinstance(b, int) and b == 0 and t < 2):
                    wait(act, v_mm, b, (-3, -2, 0)[t])
                act.activation(c_hi[(par + t) % 2][:, :, :], c_raw[:, :, t * CT:(t + 1) * CT], ACT.Copy)\
                    .then_inc(c_hi_ready.sem, 1)

            def square(b, i, unit, par):
                m = (S, M[i])[unit]
                wait(act, (q_mm, k_mm)[unit], b, i)
                if unit == 0:
                    if not (isinstance(b, int) and b == 0 and i == 0):
                        wait(act, k_sum, b, 2 * i - 2)
                else:
                    wait(act, q_sum, b, 2 * i)
                act.activation(sq[0:m, :], ps_p[(3 * i + unit) % 2][0:m, :], ACT.Square)\
                    .then_inc((q_sq, k_sq)[unit].sem, 1)

            def keep_q(b, i):
                wait(act, q_turned, b, i)
                act.activation(qT[:, i, :, :], ps_r[:, 0:HQ * S].rearrange("p (j q) -> p j q", j=HQ), ACT.Copy)\
                    .then_inc(qT_ready.sem, 1)

            def keep_k(b, i, par):
                m = M[i]
                wait(act, k_turned, b, i)
                act.activation(kT[par][:, :, i * CT:i * CT + m],
                               ps_r[:, 0:KVH * m].rearrange("p (h t) -> p h t", h=KVH), ACT.Copy)\
                    .then_inc(kT_ready.sem, 1)

            def keep_v(b, i, par):
                m = M[i]
                wait(act, v_mm, b, i)
                wait(act, pv, b, -5)
                act.activation(v[par][0:m, i, :], ps_p[(3 * i + 2) % 2][0:m, :], ACT.Copy).then_inc(v_ready.sem, 1)

            def exp(b, i, j, par):
                n = i * HQ + j
                wait(act, shifted, b, n)
                wait(act, p_turned, b, n - HQ)
                act.activation(prob[j][:, 0:KV], ps_s[j % 2][:, :], ACT.Exp, bias=down[:, j:j + 1],
                               scale=q_scale[par][:, i, j:j + 1], accum_out=total[:, j:j + 1]).then_inc(exped.sem, 1)

            def copy_pT(b, i, j):
                wait(act, p_turned, b, i * HQ + j)
                if j == 0:
                    wait(act, pv, b, i - 2)
                act.activation(pT[i % 2][0:CT, :, j, :], ps_t[j % 2][0:CT, :, :], ACT.Copy).then_inc(pT_ready.sem, 1)

            def copy_o(b, i):
                wait(act, pv, b, i)
                wait(act, o_put[i % 2], b, i // 2 - 1)
                act.activation(ov[i % 2][:, :, :], ps_o[:, :, :], ACT.Copy).then_inc(o_ready.sem, 1)

            def next_high(b, i, par):
                if i in (0, 1):
                    high(b, i + 1, par)
                elif i == 3 and not (isinstance(b, int) and b == B - 1):
                    high(b + 1, 0, 1 - par)

            def project(b, i, par):
                square(b, i, 0, par)
                square(b, i, 1, par)
                keep_q(b, i)
                next_high(b, i, par)
                keep_v(b, i, par)
                keep_k(b, i, par)

            def step(b, i, par, more):
                nb, npar = b + 1, 1 - par
                exp(b, i, 0, par)
                exp(b, i, 1, par)
                if more:
                    square(nb, i, 0, npar)
                copy_pT(b, i, 0)
                copy_pT(b, i, 1)
                exp(b, i, 2, par)
                exp(b, i, 3, par)
                if more:
                    square(nb, i, 1, npar)
                copy_pT(b, i, 2)
                copy_pT(b, i, 3)
                if more:
                    keep_q(nb, i)
                    next_high(nb, i, npar)
                    keep_v(nb, i, npar)
                copy_o(b, i)
                if more:
                    keep_k(nb, i, npar)

            exped.open(act)
            o_ready.open(act)
            pT_ready.open(act)
            high(0, 0, 0)
            for n in range(NW):
                act.wait_ge(w_in[n % 2], 16 * (n // 2 + 1))
                act.activation(w_hi[:, W_ORDER[n], :, :], v[n % 2][:, :, :], ACT.Copy).then_inc(w_hi_ready, 1)
            act.wait_ge(w_lo_ready, NW)
            batches(act, project, step)

        @block.vector
        def _(dve):
            q_sum.open(dve)
            k_sum.open(dve)

            def rotate(b, i, unit, par):
                m = (S, M[i])[unit]
                ps = ps_p[(3 * i + unit) % 2][0:m, :]
                r1, r2 = ((q1, q2), (k1, k2))[unit]
                t = (4, i)[unit]
                turned, rot = ((q_turned, q_rot), (k_turned, k_rot))[unit]
                sq_done, summed, scaled = ((q_sq, q_sum, q_scaled), (k_sq, k_sum, k_scaled))[unit]
                wait(dve, sq_done, b, i)
                if i == 0:
                    inputs(dve, b, par)
                if not (isinstance(b, int) and b == 0 and i == 0):
                    wait(dve, turned, b, i - 1)
                h4 = lambda ap: ap.rearrange("p (h d) -> p h d", h=HQ)
                dve.tensor_tensor(h4(r1[0:m, :]), h4(ps), over_heads(tab[par][0:m, t, 0, :], HQ), ALU.mult)
                for half in range(2):
                    this, other = slice(half * HF, (half + 1) * HF), slice((1 - half) * HF, (2 - half) * HF)
                    ins = dve.tensor_tensor(h4(r2[0:m, :])[:, :, this], h4(ps)[:, :, other],
                                            over_heads(tab[par][0:m, t, 1, this], HQ), ALU.mult)
                ins.then_inc(rot.sem, 1)
                if not (isinstance(b, int) and b == 0 and i == 0):
                    wait(dve, scaled, b, i - 1)
                dve.tensor_reduce(ssum[0:m, unit, :], h4(sq[0:m, :]), AX.X, ALU.add).then_inc(summed.sem, 1)
                wait(dve, summed, b, 2 * i)
                if unit == 0:
                    f = 1.0 / X_SCALE ** 2
                    dve.tensor_scalar(ssum[0:m, unit, :], ssum[0:m, unit, :], f / HD, RMS_EPS * f,
                                      ALU.mult, ALU.add).then_inc(summed.sem, 1)
                else:
                    dve.tensor_scalar(ssum[0:m, unit, :], ssum[0:m, unit, :], 1.0 / HD, RMS_EPS,
                                      ALU.mult, ALU.add).then_inc(summed.sem, 1)

            def maximum(b, i, j, par):
                n = i * HQ + j
                if i == 0 and j == 0:
                    wait(dve, q_scaled, b, 3)
                wait(dve, scored, b, n)
                dve.tensor_reduce(top[:, j:j + 1], ps_s[j % 2][:, :], AX.X, ALU.max, negate=True).then_inc(maxed.sem, 1)
                wait(dve, maxed, b, n)
                dve.tensor_tensor(down[:, j:j + 1], top[:, j:j + 1], q_scale[par][:, i, j:j + 1], ALU.mult).then_inc(shifted.sem, 1)

            def divide(b, i, j):
                n = i * HQ + j
                wait(dve, exped, b, n)
                dve.reciprocal(inv[:, j:j + 1], total[:, j:j + 1]).then_inc(inverted.sem, 1)
                wait(dve, inverted, b, n)
                dve.tensor_scalar(prob[j][:, 0:KV], prob[j][:, 0:KV], inv[:, j:j + 1], None, ALU.mult).then_inc(probs.sem, 1)

            def project(b, i, par):
                rotate(b, i, 0, par)
                rotate(b, i, 1, par)

            def step(b, i, par, more):
                maximum(b, i, 0, par)
                maximum(b, i, 1, par)
                divide(b, i, 0)
                divide(b, i, 1)
                if more:
                    rotate(b + 1, i, 0, 1 - par)
                maximum(b, i, 2, par)
                maximum(b, i, 3, par)
                divide(b, i, 2)
                divide(b, i, 3)
                if more:
                    rotate(b + 1, i, 1, 1 - par)

            for n in range(NW):
                dve.wait_ge(w_hi_ready, n + 1)
                dve.tensor_tensor(w_lo[:, W_ORDER[n], :, :], v[n % 2][:, :, :], w_hi[:, W_ORDER[n], :, :], ALU.subtract)\
                    .then_inc(w_lo_ready, 1)
            batches(dve, project, step)


def experts(nc, gate_up, down, acc, shares, xT_hi, xT_lo, out):
    KI = INTER // P
    NU = 2 * TT
    ctx = Phase(nc, "ffn")
    with ctx:
        sb = ctx.sb
        ev = ctx.ev
        ident = sb("ident", [P, P])
        raw_g = sb("raw_g", [P, KD, 2 * INTER])
        raw_d = sb("raw_d", [P, KI, D])
        g_hi = [sb(f"g_hi{i}", [P, KD, 2 * INTER], F32R) for i in range(2)]
        g_lo = [sb(f"g_lo{i}", [P, KD, 2 * INTER], F32R) for i in range(2)]
        d_hi = [sb(f"d_hi{i}", [P, KI, D], F32R) for i in range(2)]
        d_lo = [sb(f"d_lo{i}", [P, KI, D], F32R) for i in range(2)]
        den = [sb(f"den{i}", [P, INTER]) for i in range(2)]
        a = [sb(f"a{i}", [P, INTER]) for i in range(2)]
        aT_hi = [sb(f"aT_hi{i}", [P, KI, P], F32R) for i in range(2)]
        aT_lo = [sb(f"aT_lo{i}", [P, KI, P], F32R) for i in range(2)]
        ps_g = [ctx.bank(f"ps_g{i}", P, 2 * INTER) for i in range(2)]
        ps_a = [ctx.bank(f"ps_a{i}", P, KI, P) for i in range(2)]
        ps_y = [ctx.bank(f"ps_y{i}", P, D) for i in range(2)]
        id_ready = ctx.sem("id_ready")
        ticks = ctx.sem("ticks")
        raw_in = ev("raw_loaded", 2, step=16)
        w_hi, w_lo = ev("w_hi", 2), ev("w_lo", 2)
        gu = ev("gate_up", NU)
        expd = ev("exped", NU)
        plus1 = ev("plus_one", NU)
        inverse = ev("inverse", NU)
        silu = ev("silu", NU)
        gated = ev("gated", NU)
        turned = ev("a_turned", NU, 2)
        a_hi, a_lo = ev("aT_hi", NU), ev("aT_lo", NU)
        down_mm = ev("down", NU, TT + 1)
        summed = ev("summed", NU, 1)
        stored = ctx.sem("stored")
        block = ctx.enter_context(nc.Block())
        NP = E // 2

        @block.sync
        def _(sp):
            def load(e):
                if not isinstance(e, int):
                    wait(sp, w_lo, e, -1)
                sp.dma_start(raw_g[:, :, :], gate_up[e]).then_inc(raw_in.sem, 16)
                sp.dma_start(raw_d[:, :, :], down[e]).then_inc(raw_in.sem, 16)

            load(0)
            with sp.Fori(1, E) as e:
                load(e)
            for t in range(TT):
                wait(sp, summed, NP - 1, TT + t)
                sp.dma_start(out[t * P:(t + 1) * P, :], acc[:, t, :]).then_inc(stored, 16)
            sp.wait_ge(stored, 16 * TT)

        @block.gpsimd
        def _(pool):
            identity(pool, ident[:, :], id_ready)

            def split(p, par):
                e = p * 2 + par
                wait(pool, raw_in, e, 1)
                wait(pool, down_mm, p, (par - 1) * TT - 1)
                carry(pool, p, ticks)
                pool.tensor_copy(g_hi[par][:, :, :], raw_g[:, :, :]).then_inc(w_hi.sem, 1)
                pool.tensor_copy(d_hi[par][:, :, :], raw_d[:, :, :]).then_inc(w_hi.sem, 1)
                wait(pool, w_hi, e, 0)
                pool.tensor_tensor(g_lo[par][:, :, :], raw_g[:, :, :], g_hi[par][:, :, :], ALU.subtract).then_inc(w_lo.sem, 1)
                wait(pool, w_hi, e, 1)
                pool.tensor_tensor(d_lo[par][:, :, :], raw_d[:, :, :], d_hi[par][:, :, :], ALU.subtract).then_inc(w_lo.sem, 1)

            with pool.Fori(0, NP) as p:
                split(p, 0)
                split(p, 1)

        @block.tensor
        def _(pe):
            pe.wait_ge(id_ready, 2)
            turned.open(pe)
            down_mm.open(pe)

            def project(p, n):
                par, t = n // TT, n % TT
                if t == 0:
                    wait(pe, w_lo, p * 2 + par, 1)
                if n >= 2:
                    wait(pe, gated, p, n - 2)
                for k in range(KD):
                    cols = slice(t * P, (t + 1) * P)
                    mm = mm3(pe, ps_g[n % 2][:, :], xT_hi[:, k, cols], xT_lo[:, k, cols], g_hi[par][:, k, :],
                             g_lo[par][:, k, :], k == 0, k == KD - 1)
                mm.then_inc(gu.sem, 1)

            def turn(p, n):
                wait(pe, gated, p, n)
                if n >= 2:
                    wait(pe, a_lo, p, n - 2)
                for k in range(KI):
                    mm = pe.transpose(ps_a[n % 2][:, k, :], a[n % 2][:, k * P:(k + 1) * P], ident[:, :])
                mm.then_inc(turned.sem, 1)

            def project_down(p, n):
                par = n // TT
                wait(pe, a_lo, p, n)
                if n >= 2:
                    wait(pe, summed, p, n - 2)
                for k in range(KI):
                    mm = mm3(pe, ps_y[n % 2][:, :], aT_hi[n % 2][:, k, :], aT_lo[n % 2][:, k, :], d_hi[par][:, k, :],
                             d_lo[par][:, k, :], k == 0, k == KI - 1)
                mm.then_inc(down_mm.sem, 1)

            with pe.Fori(0, NP) as p:
                wait(pe, summed, p, -1)
                for n in range(NU + 2):
                    if n < NU:
                        project(p, n)
                    if n >= 2:
                        project_down(p, n - 2)
                    if 1 <= n <= NU:
                        turn(p, n - 1)

        @block.scalar
        def _(act):
            def exp(p, n):
                wait(act, gu, p, n)
                wait(act, turned, p, n - 2)
                act.activation(den[n % 2][:, :], ps_g[n % 2][:, 0:INTER], ACT.Exp, scale=-1.0).then_inc(expd.sem, 1)

            def high(p, n):
                wait(act, turned, p, n)
                wait(act, down_mm, p, n - 2)
                act.activation(aT_hi[n % 2][:, :, :], ps_a[n % 2][:, :, :], ACT.Copy).then_inc(a_hi.sem, 1)

            with act.Fori(0, NP) as p:
                for n in range(NU + 1):
                    if n < NU:
                        exp(p, n)
                    if n:
                        high(p, n - 1)

        @block.vector
        def _(dve):
            def gate(p, n):
                d, g = den[n % 2], ps_g[n % 2]
                wait(dve, expd, p, n)
                dve.tensor_scalar(d[:, :], d[:, :], 1.0, None, ALU.add).then_inc(plus1.sem, 1)
                wait(dve, plus1, p, n)
                dve.reciprocal(d[:, :], d[:, :]).then_inc(inverse.sem, 1)
                wait(dve, inverse, p, n)
                dve.tensor_tensor(d[:, :], g[:, 0:INTER], d[:, :], ALU.mult).then_inc(silu.sem, 1)
                wait(dve, silu, p, n)
                wait(dve, turned, p, n - 2)
                dve.tensor_tensor(a[n % 2][:, :], g[:, INTER:2 * INTER], d[:, :], ALU.mult).then_inc(gated.sem, 1)

            def low(p, n):
                wait(dve, a_hi, p, n)
                dve.tensor_tensor(aT_lo[n % 2][:, :, :], ps_a[n % 2][:, :, :], aT_hi[n % 2][:, :, :], ALU.subtract)\
                    .then_inc(a_lo.sem, 1)

            def add(p, n):
                par, t = n // TT, n % TT
                wait(dve, down_mm, p, n)
                dve.scalar_tensor_tensor(acc[:, t, :], ps_y[n % 2][:, :], shares[:, t, bass.ds(p * 2 + par, 1)],
                                         acc[:, t, :], ALU.mult, ALU.add).then_inc(summed.sem, 1)

            summed.open(dve)
            with dve.Fori(0, NP) as p:
                for n in range(NU + 2):
                    if n < NU:
                        gate(p, n)
                    if n >= 2:
                        add(p, n - 2)
                    if 1 <= n <= NU:
                        low(p, n - 1)


def build(nc, x, ctxT, pos_ctx, pos_x, inv_freq, q_proj, wq_rotT, wkvaT, kv_ln, kv_b, woT, xwqT, xwkT, xwvT,
          xwoT, q_norm, k_norm, clsT, bias, gate_up, down, out):
    dram = lambda name, shape: nc.dram_tensor(name, shape, F32).ap()
    tables = dram("rope_tables", (B, P, 5, 2, HD))
    vo = dram("value_output_weights", (P, H, D))
    x0T = dram("x0T_hi", (P, KD, T)), dram("x0T_lo", (P, KD, T))
    x1T = dram("x1T_hi", (P, KD, T)), dram("x1T_lo", (P, KD, T))
    o1T, o2T = dram("self_outT", (P, H, T)), dram("cross_outT", (P, H, T))
    x1 = dram("x1", (T, D))
    x_rows = x.rearrange("b s d -> (b s) d")
    out_rows = out.rearrange("b s d -> (b s) d")
    kv_heads = kv_b.rearrange("(h c d) r -> c d h r", h=H, c=2)

    with ExitStack() as ctx:
        sb = lambda name, shape, dt=F32: ctx.enter_context(nc.sbuf_tensor(name, shape, dt))
        qf = sb("qf_hi", [P, KD, H, RANK], F32R), sb("qf_lo", [P, KD, H, RANK], F32R)
        qr = sb("qr_hi", [P, KD, H * ROPE], F32R), sb("qr_lo", [P, KD, H * ROPE], F32R)
        lat_kT = sb("lat_kT", [P, 3, T])
        lat_v = sb("lat_v", [S, B, RANK])
        with ExitStack() as early:
            esb = lambda name, shape, dt: early.enter_context(nc.sbuf_tensor(name, shape, dt))
            kva = esb("kva_hi", [P, KD, RANK + ROPE], F32R), esb("kva_lo", [P, KD, RANK + ROPE], F32R)
            fold_weights(nc, q_proj, kv_heads[0], kv_heads[1], woT, wq_rotT, wkvaT, *qf, *qr, *kva,
                         lat_kT[:, :, :].rearrange("p c t -> p (c t)"), vo)
            latents(nc, x, kv_ln, *kva, lat_kT, lat_v, *x0T)
        self_attention(nc, *x0T, *qf, *qr, lat_kT, lat_v, o1T)
    project_out(nc, o1T, vo, x_rows, x1, x1T, rope=(pos_ctx, pos_x, inv_freq, k_norm, q_norm, tables))
    cross_attention(nc, ctxT, *x1T, xwqT, xwkT, xwvT, tables, o2T)
    with ExitStack() as ctx:
        sb = lambda name, shape, dt=F32: ctx.enter_context(nc.sbuf_tensor(name, shape, dt))
        acc = sb("acc", [P, TT, D])
        shares = sb("shares", [P, TT, E])
        x2T = sb("x2T_hi", [P, KD, T], F32R), sb("x2T_lo", [P, KD, T], F32R)
        project_out(nc, o2T, xwoT, x1, None, [t[:, :, :].bitcast(F32) for t in x2T],
                    router=(clsT, bias), keep=(acc, shares))
        experts(nc, gate_up, down, acc, shares, *x2T, out_rows)


def layouts(x, ctx_2048, pos_BxS2, itok_BxS_4096_4607, L0_attn_q_proj_w, L0_attn_kv_a_proj_w, L0_attn_kv_a_ln_w,
            L0_attn_kv_b_proj_w, L0_attn_o_proj_w, L0_xattn_Wq, L0_xattn_Wk, L0_xattn_Wv, L0_xattn_Wo,
            L0_xattn_q_norm_w, L0_xattn_k_norm_w, L0_ffn_classifier_w, L0_ffn_e_score_correction_bias,
            L0_ffn_gate_w, L0_ffn_up_w, L0_ffn_down_w):
    kT = lambda w: w.T.reshape(KD, P, -1).transpose(1, 0, 2)
    rows = lambda w, n: np.broadcast_to(w, (n, w.shape[0]))
    heads = lambda w: w.reshape(D, H, P).transpose(2, 1, 0)
    rot = L0_attn_q_proj_w.reshape(H, NOPE + ROPE, D)[:, NOPE:].reshape(H * ROPE, D)
    gu = np.concatenate([L0_ffn_gate_w, L0_ffn_up_w], axis=1)
    freq = 1.0 / np.float32(10000.0) ** (np.arange(0, HD, 2, dtype=np.float32) / np.float32(HD))
    return {
        "x": x,
        "ctxT": ctx_2048.reshape(B, C, KD, P).transpose(0, 3, 2, 1),
        "pos_ctx": pos_BxS2.reshape(B, 3, CT).transpose(2, 1, 0),
        "pos_x": itok_BxS_4096_4607.T,
        "inv_freq": rows(freq.astype(np.float32), P),
        "q_proj": L0_attn_q_proj_w,
        "wq_rotT": kT(rot),
        "wkvaT": kT(L0_attn_kv_a_proj_w),
        "kv_ln": rows(L0_attn_kv_a_ln_w, S),
        "kv_b": L0_attn_kv_b_proj_w,
        "woT": heads(L0_attn_o_proj_w),
        "xwqT": kT(L0_xattn_Wq),
        "xwkT": kT(L0_xattn_Wk),
        "xwvT": kT(L0_xattn_Wv),
        "xwoT": heads(L0_xattn_Wo),
        "q_norm": rows(L0_xattn_q_norm_w, P),
        "k_norm": rows(L0_xattn_k_norm_w, P),
        "clsT": kT(L0_ffn_classifier_w),
        "bias": rows(L0_ffn_e_score_correction_bias, P),
        "gate_up": gu.transpose(0, 2, 1).reshape(E, KD, P, 2 * INTER).transpose(0, 2, 1, 3),
        "down": L0_ffn_down_w.transpose(0, 2, 1).reshape(E, INTER // P, P, D).transpose(0, 2, 1, 3),
    }


def kernel(**inputs):
    import concourse.bacc as bacc
    from concourse.bass_utils import run_bass_kernel_spmd

    nc = bacc.Bacc("TRN2", target_bir_lowering=False, num_devices=1)
    arrays, args = {}, {}
    for name, a in layouts(**{k: np.asarray(v) for k, v in inputs.items()}).items():
        a = np.ascontiguousarray(a)
        arrays[f"in_{name}"] = a
        args[name] = nc.dram_tensor(f"in_{name}", a.shape, mybir.dt.from_np(a.dtype), kind="ExternalInput").ap()
    out = nc.dram_tensor("out", (B, S, D), F32, kind="ExternalOutput").ap()
    build(nc, **args, out=out)
    r = run_bass_kernel_spmd(nc, [arrays], core_ids=[0])
    return r.results[0]["out"]
```

```python
from contextlib import ExitStack

import numpy as np

import concourse.bass as bass
from concourse import mybir

F32 = mybir.dt.float32
F32R = mybir.dt.float32r
I32 = mybir.dt.int32
U32 = mybir.dt.uint32
ALU = mybir.AluOpType
ACT = mybir.ActivationFunctionType
AX = mybir.AxisListType

B, S, D = 16, 112, 512
T = B * S
C = 375
KV = C + S
P = 128
KD = D // P
H = 16
HQ = 4
NQ = H // HQ
NOPE, ROPE, RANK = 128, 64, 128
HD, KVH = 128, 4
CT = C // 3
E, TOTAL, INTER = 8, 12, 256
TT = T // P
G = 4
GT = G * S
ST = 2 * P
NS = (2 * T - E) // ST + E
REGION = 2048
DUMP = (E - 1) * REGION + NS * ST
LN_EPS, RMS_EPS = 1e-5, 1e-6
MLA_SCALE = float((NOPE + ROPE) ** -0.5)
X_SCALE = float(HD ** -0.5)
ROUTE_SCALE = 1.5
MASKED = -3.0e9
PI2 = (6.28125, float(2 * np.pi) - 6.28125)


class Event:

    def __init__(self, sem, per, ahead, step):
        self.sem = sem
        self.per, self.ahead, self.step = per, ahead, step

    def at(self, item, n=0):
        return (item * self.per + (n + 1 + self.ahead)) * self.step

    def open(self, eng):
        eng.sem_inc(self.sem, self.ahead * self.step)


def wait(eng, event, item, n=0):
    eng.wait_ge(event.sem, event.at(item, n))


def carry(eng, item, ticks):
    if not isinstance(item, int):
        eng.sem_inc(ticks, 1)


def mm3(pe, out, a_hi, a_lo, b_hi, b_lo, start, stop):
    pe.matmul(out, a_hi, b_hi, start=start, stop=False)
    pe.matmul(out, a_hi, b_lo, start=False, stop=False)
    return pe.matmul(out, a_lo, b_hi, start=False, stop=stop)


def over_heads(ap, n):
    return ap.unsqueeze(1).broadcast_to((ap.shape[0], n, ap.shape[1]))


def along(ap, n):
    return ap.unsqueeze(2).broadcast_to((ap.shape[0], ap.shape[1], n))


class Phase(ExitStack):

    def __init__(self, nc, name):
        super().__init__()
        self.nc, self.name = nc, name
        self.sems = []

    def sb(self, name, shape, dt=F32):
        return self.enter_context(self.nc.sbuf_tensor(f"{self.name}_{name}", shape, dt))

    def sem(self, name):
        self.sems.append(self.nc.alloc_semaphore(name=f"{self.name}_{name}"))
        return self.sems[-1]

    def __exit__(self, *exc):
        done = super().__exit__(*exc)
        self.nc.clear_and_free_semaphores(self.sems)
        self.nc.all_engine_barrier()
        return done

    def ev(self, name, per, ahead=0, step=1):
        return Event(self.sem(name), per, ahead, step)

    def bank(self, name, *shape):
        flat = self.enter_context(self.nc.psum_tensor(f"{self.name}_{name}", [P, 512], F32))
        if len(shape) == 2:
            return flat[0:shape[0], 0:shape[1]]
        return flat[0:shape[0], 0:shape[1] * shape[2]].rearrange("p (a b) -> p a b", a=shape[1])


def identity(pool, tile, sem, before=0):
    pool.memset(tile, 0.0).then_inc(sem, 1)
    pool.wait_ge(sem, before + 1)
    pool.affine_select(out=tile, in_=tile, compare_op=ALU.not_equal, fill=1.0, base=0,
                       pattern=[[-1, tile.shape[1]]], channel_multiplier=1).then_inc(sem, 1)


def fold_weights(nc, wq_nope, wkb, wvb, woT, wq_rotT, wkvaT, qf_hi, qf_lo, qr_hi, qr_lo, kva_hi, kva_lo, scratch, vo):
    ctx = Phase(nc, "fold")
    with ctx:
        sb = ctx.sb
        sem = ctx.sem
        wq = sb("wq_nat", [P, 2, HQ, D])
        kb = sb("kb_nat", [P, H, RANK])
        vb = sb("vb_nat", [P, H, RANK])
        wo = sb("wo_nat", [P, 2, HQ, D])
        rot = scratch[:, 0:KD * H * ROPE].rearrange("p (k n) -> p k n", k=KD)
        kva = sb("kva_raw", [P, KD, RANK + ROPE])
        vos = sb("vos", [P, 2, HQ, D])
        psq = [ctx.bank(f"psq{i}", P, 512) for i in range(4)]
        psv = [ctx.bank(f"psv{i}", P, 512) for i in range(4)]
        small, wq_in = sem("small_loaded"), [sem("wq_loaded0"), sem("wq_loaded1")]
        wo_in = [sem("wo_loaded0"), sem("wo_loaded1")]
        split_in, vb_in = sem("split_loaded"), sem("vb_loaded")
        stored = [sem("vo_stored0"), sem("vo_stored1")]
        q_mm, v_mm, q_hi, q_lo, v_out, plain_hi, plain_lo = (sem(n) for n in (
            "q_products", "v_products", "q_hi", "q_lo", "v_copied", "plain_hi", "plain_lo"))
        block = ctx.enter_context(nc.Block())
        nope = wq_nope.rearrange("(h d) i -> d h i", h=H)

        @block.sync
        def _(sp):
            sp.dma_start(kb[:, :, :], wkb).then_inc(small, 16)
            for c in range(NQ):
                if c >= 2:
                    sp.wait_ge(q_mm, KD * (c - 1))
                sp.dma_start(wq[:, c % 2], nope[0:NOPE, c * HQ:(c + 1) * HQ, :]).then_inc(wq_in[c % 2], 16)
            for c in range(NQ):
                sp.wait_ge(v_out, HQ * (c + 1))
                sp.dma_start(vo[:, c * HQ:(c + 1) * HQ, :], vos[:, c % 2]).then_inc(stored[c % 2], 16)
            for i in range(2):
                sp.wait_ge(stored[i], 16 * NQ // 2)

        @block.gpsimd
        def _(pool):
            pool.wait_ge(plain_hi, 1)
            pool.tensor_tensor(kva_lo[:, :, :], kva[:, :, :], kva_hi[:, :, :], ALU.subtract).then_inc(plain_lo, 1)
            pool.wait_ge(plain_hi, 2)
            pool.tensor_tensor(qr_lo[:, :, :], rot[:, :, :], qr_hi[:, :, :], ALU.subtract).then_inc(plain_lo, 1)

        @block.tensor
        def _(pe):
            pe.wait_ge(small, 16)
            for c in range(NQ):
                pe.wait_ge(wq_in[c % 2], 16 * (c // 2 + 1))
                for k in range(KD):
                    n = c * KD + k
                    if n >= 4:
                        pe.wait_ge(q_lo, n - 3)
                    for j in range(HQ):
                        mm = pe.matmul(psq[n % 4][:, j * RANK:(j + 1) * RANK], wq[:, c % 2, j, k * P:(k + 1) * P],
                                       kb[:, c * HQ + j, :], start=True, stop=True)
                    mm.then_inc(q_mm, 1)
            pe.wait_ge(vb_in, 16)
            for c in range(NQ):
                pe.wait_ge(wo_in[c % 2], 16 * (c // 2 + 1))
                for j in range(HQ):
                    n = c * HQ + j
                    if n >= 4:
                        pe.wait_ge(v_out, n - 3)
                    pe.matmul(psv[n % 4][:, :], vb[:, n, :], wo[:, c % 2, j, :], start=True, stop=True).then_inc(v_mm, 1)

        @block.scalar
        def _(act):
            act.dma_start(kva[:, :, :], wkvaT).then_inc(split_in, 16)
            act.dma_start(rot[:, :, :], wq_rotT).then_inc(split_in, 16)
            act.dma_start(vb[:, :, :], wvb).then_inc(vb_in, 16)
            for c in range(2):
                act.dma_start(wo[:, c], woT[:, c * HQ:(c + 1) * HQ, :]).then_inc(wo_in[c], 16)
            act.wait_ge(split_in, 32)
            act.activation(kva_hi[:, :, :], kva[:, :, :], ACT.Copy).then_inc(plain_hi, 1)
            act.activation(qr_hi[:, :, :], rot[:, :, :], ACT.Copy).then_inc(plain_hi, 1)
            for n in range(NQ * KD):
                c, k = n // KD, n % KD
                act.wait_ge(q_mm, n + 1)
                act.activation(qf_hi[:, k, c * HQ:(c + 1) * HQ, :], psq[n % 4][:, :], ACT.Copy).then_inc(q_hi, 1)
            for c in range(2, NQ):
                act.wait_ge(v_mm, HQ * (c - 1))
                act.dma_start(wo[:, c % 2], woT[:, c * HQ:(c + 1) * HQ, :]).then_inc(wo_in[c % 2], 16)

        @block.vector
        def _(dve):
            for n in range(NQ * KD):
                c, k = n // KD, n % KD
                dve.wait_ge(q_hi, n + 1)
                dve.tensor_tensor(qf_lo[:, k, c * HQ:(c + 1) * HQ, :], psq[n % 4][:, :].rearrange("p (j r) -> p j r", j=HQ),
                                  qf_hi[:, k, c * HQ:(c + 1) * HQ, :], ALU.subtract).then_inc(q_lo, 1)
            for n in range(H):
                c = n // HQ
                if c >= 2 and n % HQ == 0:
                    dve.wait_ge(stored[c % 2], 16 * (c // 2))
                dve.wait_ge(v_mm, n + 1)
                dve.tensor_copy(vos[:, c % 2, n % HQ, :], psv[n % 4][:, :]).then_inc(v_out, 1)


class LayerNorm:

    def __init__(self, ctx, rows):
        self.stats, self.mv = ctx.sb("stats", [rows, 6]), ctx.sb("mean_var", [rows, 2])
        self.counted, self.varied = ctx.ev("ln_stats", 1), ctx.ev("ln_var", 1)
        self.ticks = ctx.sem("ln_ticks")
        self.shifted, self.rooted = ctx.ev("ln_var_eps", 1), ctx.ev("ln_rstd", 1)

    def vector(self, dve, item, dst, src):
        dve.bn_stats(self.stats[:, :], src).then_inc(self.counted.sem, 1)
        wait(dve, self.counted, item)
        carry(dve, item, self.ticks)
        dve.bn_aggr(self.mv[:, :], self.stats[:, :]).then_inc(self.varied.sem, 1)
        wait(dve, self.rooted, item)
        return dve.tensor_scalar(dst, src, self.mv[:, 0:1], self.mv[:, 1:2], ALU.subtract, ALU.mult)

    def root(self, pool, item, minus_half):
        var = self.mv[:, 1:2]
        wait(pool, self.varied, item)
        carry(pool, item, self.ticks)
        pool.tensor_scalar(var, var, LN_EPS, None, ALU.add).then_inc(self.shifted.sem, 1)
        wait(pool, self.shifted, item)
        pool.tensor_tensor(var, var, minus_half[0:var.shape[0], 0:1], ALU.pow).then_inc(self.rooted.sem, 1)


def exponent(pool, tile, sem):
    pool.memset(tile, -0.5).then_inc(sem, 1)
    pool.wait_ge(sem, 1)


def latents(nc, x, lnw, kva_hi, kva_lo, lat_kT, lat_v, xT_hi, xT_lo):
    W = RANK + ROPE
    ctx = Phase(nc, "lat")
    with ctx:
        sb = ctx.sb
        ev = ctx.ev
        ident = sb("ident", [S, S])
        w_ln = sb("w_ln", [S, RANK])
        xs = [sb(f"xs{i}", [S, D]) for i in range(2)]
        xn = [sb(f"xn{i}", [S, D]) for i in range(2)]
        norm = LayerNorm(ctx, S)
        minus_half = sb("minus_half", [S, 1])
        half_ready = ctx.sem("minus_half_ready")
        xh = [sb(f"xh{i}", [P, KD, S], F32R) for i in range(2)]
        xl = [sb(f"xl{i}", [P, KD, S], F32R) for i in range(2)]
        sq = sb("sq", [S, RANK])
        ms = sb("ms", [S, 2])
        rstd = sb("rstd", [S, 1])
        ln = [sb(f"ln{i}", [S, RANK]) for i in range(2)]
        kr = [sb(f"kr{i}", [S, 3, ROPE]) for i in range(2)]
        ps_x = [ctx.bank(f"ps_x{i}", P, KD, S) for i in range(2)]
        ps_l = [ctx.bank(f"ps_l{i}", S, W) for i in range(2)]
        ps_t = [ctx.bank(f"ps_t{i}", P, 3, S) for i in range(2)]
        id_ready = ctx.sem("id_ready")
        ticks = ctx.sem("ticks")
        w_in = ctx.sem("lnw_loaded")
        zeros = ctx.sem("kr_zeros")
        x_in = [ctx.ev(f"x_loaded{i}", 1, step=16) for i in range(2)]
        normed = ev("x_normed", 1, 2)
        x_turned = ev("x_turned", 1)
        hi, lo = ev("x_hi", 1), ev("x_lo", 1)
        put = [ctx.ev(f"xT_stored{i}", 2, 2, 16) for i in range(2)]
        lat_mm = ev("lat_products", 1)
        squared = ev("lat_squared", 1)
        rms_in = ev("lat_mean_square", 1)
        rms = ev("lat_rstd", 1, 1)
        lat_ready = ev("lat_normed", 1)
        kr_ready = ev("kr_copied", 1)
        v_kept = ev("lat_v_kept", 1, 2)
        turned = ev("lat_turned", 1)
        kept = ev("lat_kept", 1, 2)
        block = ctx.enter_context(nc.Block())

        @block.sync
        def _(sp):
            sp.dma_start(w_ln[:, :], lnw).then_inc(w_in, 16)
            for i in range(2):
                put[i].open(sp)

            def body(b, par):
                wait(sp, normed, b, -2)
                sp.dma_start(xs[par][:, :], x[b]).then_inc(x_in[par].sem, 16)

            def store(b, h, par):
                cols = bass.ds(b * S, S)
                wait(sp, lo, b)
                sp.dma_start(xT_hi[:, :, cols], xh[par][:, :, :].bitcast(F32)).then_inc(put[par].sem, 16)
                sp.dma_start(xT_lo[:, :, cols], xl[par][:, :, :].bitcast(F32)).then_inc(put[par].sem, 16)

            body(0, 0)
            body(1, 1)
            with sp.Fori(0, B // 2 - 1) as h:
                for par in range(2):
                    body(h * 2 + 2 + par, par)
                    store(h * 2 + par, h, par)
            for par in range(2):
                store(B - 2 + par, B // 2 - 1, par)
            for par in range(2):
                sp.wait_ge(put[par].sem, put[par].at(B // 2 - 1, 1))

        @block.gpsimd
        def _(pool):
            identity(pool, ident[:, :], id_ready)
            for i in range(2):
                pool.memset(kr[i][:, :, :], 0.0).then_inc(zeros, 1)
            exponent(pool, minus_half[:, :], half_ready)
            v_kept.open(pool)
            rms.open(pool)

            def body(b, par, last=False):
                if not last:
                    norm.root(pool, b + 1, minus_half)
                wait(pool, rms_in, b)
                pool.tensor_tensor(rstd[:, :], ms[:, 1:2], minus_half[:, :], ALU.pow).then_inc(rms.sem, 1)
                wait(pool, lat_ready, b)
                carry(pool, b, ticks)
                pool.tensor_copy(lat_v[:, b, :], ln[par][:, :]).then_inc(v_kept.sem, 1)

            norm.root(pool, 0, minus_half)
            with pool.Fori(0, B // 2 - 1) as h:
                body(h * 2, 0)
                body(h * 2 + 1, 1)
            body(B - 2, 0)
            body(B - 1, 1, last=True)

        @block.vector
        def _(dve):
            normed.open(dve)
            dve.wait_ge(w_in, 16)
            dve.wait_ge(zeros, 2)

            def layer_norm(b, h, par):
                wait(dve, x_in[par], h)
                norm.vector(dve, b, xn[par][:, :], xs[par][:, :]).then_inc(normed.sem, 1)

            def low(b, h, par):
                wait(dve, hi, b)
                wait(dve, put[par], h, -1)
                dve.tensor_tensor(xl[par][:, :, :], ps_x[par][:, :, :], xh[par][:, :, :], ALU.subtract).then_inc(lo.sem, 1)

            def latent(b, par):
                wait(dve, squared, b)
                dve.tensor_scalar(ms[:, 1:2], ms[:, 0:1], 1.0 / RANK, RMS_EPS, ALU.mult, ALU.add).then_inc(rms_in.sem, 1)
                wait(dve, rms, b)
                wait(dve, v_kept, b, -2)
                wait(dve, kept, b, -2)
                dve.scalar_tensor_tensor(ln[par][:, :], ps_l[par][:, 0:RANK], rstd[:, 0:1], w_ln[:, :],
                                         ALU.mult, ALU.mult).then_inc(lat_ready.sem, 1)
                dve.tensor_copy(kr[par][:, 1, :], ps_l[par][:, RANK:W]).then_inc(kr_ready.sem, 1)

            def body(b, h, par, last=False):
                if not last:
                    layer_norm(b + 1, h + par, 1 - par)
                latent(b, par)
                if not last:
                    low(b + 1, h + par, 1 - par)

            layer_norm(0, 0, 0)
            low(0, 0, 0)
            with dve.Fori(0, B // 2 - 1) as h:
                body(h * 2, h, 0)
                body(h * 2 + 1, h, 1)
            body(B - 2, B // 2 - 1, 0)
            body(B - 1, B // 2 - 1, 1, last=True)

        @block.scalar
        def _(act):
            kept.open(act)

            def high(b, h, par):
                wait(act, x_turned, b)
                wait(act, put[par], h, -1)
                act.activation(xh[par][:, :, :], ps_x[par][:, :, :], ACT.Copy).then_inc(hi.sem, 1)

            def body(b, h, par, last=False):
                wait(act, lat_mm, b)
                wait(act, rms, b, -1)
                act.activation(sq[:, :], ps_l[par][:, 0:RANK], ACT.Square, accum_out=ms[:, 0:1]).then_inc(squared.sem, 1)
                if not last:
                    high(b + 1, h + par, 1 - par)
                wait(act, turned, b)
                act.activation(lat_kT[:, :, bass.ds(b * S, S)], ps_t[par][:, :, :], ACT.Copy).then_inc(kept.sem, 1)

            high(0, 0, 0)
            with act.Fori(0, B // 2 - 1) as h:
                body(h * 2, h, 0)
                body(h * 2 + 1, h, 1)
            body(B - 2, B // 2 - 1, 0)
            body(B - 1, B // 2 - 1, 1, last=True)

        @block.tensor
        def _(pe):
            pe.wait_ge(id_ready, 2)

            def turn_x(b, par):
                wait(pe, normed, b)
                if not (isinstance(b, int) and b < 2):
                    wait(pe, lo, b, -2)
                for k in range(KD):
                    mm = pe.transpose(ps_x[par][:, k, :], xn[par][:, k * P:(k + 1) * P], ident[:, :])
                mm.then_inc(x_turned.sem, 1)

            def body(b, par, last=False):
                wait(pe, lo, b)
                if not (isinstance(b, int) and b < 2):
                    wait(pe, kr_ready, b, -2)
                for k in range(KD):
                    mm = mm3(pe, ps_l[par][:, :], xh[par][:, k, :], xl[par][:, k, :], kva_hi[:, k, :], kva_lo[:, k, :],
                             k == 0, k == KD - 1)
                mm.then_inc(lat_mm.sem, 1)
                if not last:
                    turn_x(b + 1, 1 - par)
                wait(pe, kr_ready, b)
                wait(pe, kept, b, -2)
                pe.transpose(ps_t[par][:, 0, :], ln[par][:, :], ident[:, :])
                pe.transpose(ps_t[par][:, 1, :], kr[par][:, 1:3, :], ident[:, :])
                pe.transpose(ps_t[par][:, 2, :], kr[par][:, 0:2, :], ident[:, :]).then_inc(turned.sem, 1)

            turn_x(0, 0)
            body(0, 0)
            body(1, 1)
            with pe.Fori(1, B // 2 - 1) as h:
                body(h * 2, 0)
                body(h * 2 + 1, 1)
            body(B - 2, 0)
            body(B - 1, 1, last=True)


def self_attention(nc, xT_hi, xT_lo, qf_hi, qf_lo, qr_hi, qr_lo, lat_kT, lat_v, oT):
    NU = NQ * G
    ctx = Phase(nc, "sa")
    with ctx:
        sb = ctx.sb
        ev = ctx.ev
        ident = sb("ident", [S, S])
        mask = sb("mask", [S, S])
        xh = sb("xh", [P, 2, KD, GT], F32R)
        xl = sb("xl", [P, 2, KD, GT], F32R)
        qn = [sb(f"qn{i}", [P, HQ, GT]) for i in range(2)]
        qr = [sb(f"qr{i}", [P, HQ // 2, GT]) for i in range(2)]
        prob = [sb(f"prob{i}", [S, HQ, S]) for i in range(2)]
        top = [sb(f"top{i}", [S, HQ]) for i in range(2)]
        total = [sb(f"total{i}", [S, HQ]) for i in range(2)]
        pT = [sb(f"pT{i}", [S, HQ, S]) for i in range(2)]
        val = [sb(f"val{i}", [S, RANK]) for i in range(2)]
        ov = [sb(f"ov{i}", [P, HQ, S]) for i in range(2)]
        ps_q = [ctx.bank(f"ps_q{i}", P, GT) for i in range(2)]
        ps_s = [ctx.bank(f"ps_s{i}", S, HQ, S) for i in range(2)]
        ps_t = [ctx.bank(f"ps_t{i}", S, HQ, S) for i in range(2)]
        ps_o = [ctx.bank(f"ps_o{i}", P, HQ, S) for i in range(2)]
        consts = ctx.sem("consts")
        ticks = ctx.sem("ticks")
        x_in = ev("xT_loaded", 2, step=16)
        q_mm = ev("q_projected", 6 * NQ, 1)
        qn_ready = ev("q_nope_copied", 4 * NQ)
        qr_ready = ev("q_rot_copied", 2 * NQ)
        scored = ev("scored", NU)
        masked = ev("masked", NU, 2)
        maxed = ev("maxed", NU)
        shifted = ev("shifted", NU)
        exped = ev("exped", NU)
        summed = ev("summed", 2 * NU)
        probs = ev("probs", NU)
        p_turned = ev("p_turned", NU, 2)
        pT_ready = ev("pT_ready", NU, 2)
        val_ready = ev("values_ready", NU)
        pv = ev("weighted", NU, 2)
        o_ready = ev("o_ready", NU, 2)
        o_put = [ev(f"o_stored{i}", NU // 2, 1, 16) for i in range(2)]
        block = ctx.enter_context(nc.Block())
        NG = B // G

        def groups(eng, body):
            with eng.Fori(0, NG - 1) as g:
                body(g, True)
            body(NG - 1, False)

        @block.sync
        def _(sp):
            def load(g, n_free):
                for src, dst in ((xT_hi, xh), (xT_lo, xl)):
                    sp.dma_start(dst[:, bass.ds(n_free, 1), :, :].bitcast(F32),
                                 src[:, :, bass.ds(g * GT, GT)]).then_inc(x_in.sem, 16)

            for i in range(2):
                o_put[i].open(sp)
            load(0, 0)

            def body(g, more):
                for n in range(NU):
                    if n == 0 and more:
                        wait(sp, q_mm, g, -1)
                        wait(sp, x_in, g, 1)
                        load(g + 1, (g + 1) % 2)
                    hq, s = n // G, n % G
                    wait(sp, o_ready, g, n)
                    sp.dma_start(oT[:, hq * HQ:(hq + 1) * HQ, bass.ds(g * GT + s * S, S)], ov[n % 2][:, :, :])\
                        .then_inc(o_put[n % 2].sem, 16)

            groups(sp, body)
            for i in range(2):
                sp.wait_ge(o_put[i].sem, o_put[i].at(NG - 1, NU // 2 - 1))

        @block.gpsimd
        def _(pool):
            identity(pool, ident[:, :], consts)
            pool.memset(mask[:, :], 0.0).then_inc(consts, 1)
            pool.wait_ge(consts, 3)
            pool.affine_select(out=mask[:, :], in_=mask[:, :], compare_op=ALU.is_ge, fill=MASKED, base=0,
                               pattern=[[-1, S]], channel_multiplier=1).then_inc(consts, 1)

            def body(g, more):
                for n in range(NU):
                    wait(pool, pv, g, n - 2)
                    carry(pool, g, ticks)
                    pool.tensor_copy(val[n % 2][:, :], lat_v[:, g * G + n % G, :]).then_inc(val_ready.sem, 1)

            groups(pool, body)

        @block.tensor
        def _(pe):
            pe.wait_ge(consts, 4)
            p_turned.open(pe)
            pv.open(pe)
            q_mm.open(pe)

            def project(g, hq, j, rot):
                u = (0, 2, 3, 5)[j] if not rot else (1, 4)[j]
                first = isinstance(g, int) and g == 0 and hq == 0
                if u == 3 or (u == 0 and not first):
                    wait(pe, qr_ready, g, 2 * hq + (0 if u else -1))
                elif u != 0 and not (u == 1 and first):
                    wait(pe, qn_ready, g, 4 * hq + {1: -1, 2: 0, 4: 1, 5: 2}[u])
                if u == 0 and hq == 0:
                    wait(pe, x_in, g, 1)
                w_hi, w_lo, w = (qr_hi, qr_lo, P) if rot else (qf_hi, qf_lo, RANK)
                for k in range(KD):
                    c0 = (2 * hq + j) * P if rot else 0
                    a_hi = w_hi[:, k, c0:c0 + P] if rot else w_hi[:, k, hq * HQ + j, :]
                    a_lo = w_lo[:, k, c0:c0 + P] if rot else w_lo[:, k, hq * HQ + j, :]
                    slot = g % 2
                    mm = mm3(pe, ps_q[u % 2][:, :], a_hi, a_lo, xh[:, slot, k, :], xl[:, slot, k, :],
                             k == 0, k == KD - 1)
                mm.then_inc(q_mm.sem, 1)

            def score(g, n):
                hq, s = n // G, n % G
                if s == 0:
                    wait(pe, qn_ready, g, 4 * hq + 3)
                    wait(pe, qr_ready, g, 2 * hq + 1)
                wait(pe, masked, g, n - 2)
                for j in range(HQ):
                    cols = slice(s * S, (s + 1) * S)
                    keys = lambda c: lat_kT[:, c, bass.ds(g * GT + s * S, S)]
                    pe.matmul(ps_s[n % 2][:, j, :], qn[hq % 2][:, j, cols], keys(0), start=True, stop=False)
                    mm = pe.matmul(ps_s[n % 2][:, j, :], qr[hq % 2][:, j // 2, cols], keys(1 + j % 2),
                                   start=False, stop=True)
                mm.then_inc(scored.sem, 1)

            def turn(g, n):
                wait(pe, probs, g, n)
                wait(pe, pT_ready, g, n - 2)
                for j in range(HQ):
                    mm = pe.transpose(ps_t[n % 2][:, j, :], prob[n % 2][:, j, :], ident[:, :])
                mm.then_inc(p_turned.sem, 1)

            def weigh(g, n):
                wait(pe, pT_ready, g, n)
                wait(pe, val_ready, g, n)
                wait(pe, o_ready, g, n - 2)
                pe.matmul(ps_o[n % 2][:, :, :], val[n % 2][:, :], pT[n % 2][:, :, :], start=True, stop=True)\
                    .then_inc(pv.sem, 1)

            def queries(g):
                for j in range(HQ):
                    project(g, 0, j, False)
                    if j % 2 == 0:
                        project(g, 0, j // 2, True)

            def body(g, more):
                for n in range(NU):
                    hq, s = n // G, n % G
                    score(g, n)
                    if n:
                        turn(g, n - 1)
                    if hq + 1 < NQ:
                        project(g, hq + 1, s, False)
                    if n:
                        weigh(g, n - 1)
                    if hq + 1 < NQ and s % 2 == 0:
                        project(g, hq + 1, s // 2, True)
                if more:
                    queries(g + 1)
                turn(g, NU - 1)
                weigh(g, NU - 1)

            queries(0)
            groups(pe, body)

        @block.scalar
        def _(act):
            pT_ready.open(act)
            o_ready.open(act)

            def query(g, hq, j):
                wait(act, q_mm, g, 6 * hq + (0, 2, 3, 5)[j])
                act.activation(qn[hq % 2][:, j, :], ps_q[(0, 2, 3, 5)[j] % 2][:, :], ACT.Copy).then_inc(qn_ready.sem, 1)

            def exp(g, n):
                wait(act, shifted, g, n)
                act.activation(prob[n % 2][:, :, :], prob[n % 2][:, :, :], ACT.Exp, scale=MLA_SCALE).then_inc(exped.sem, 1)

            def copy_pT(g, n):
                wait(act, p_turned, g, n)
                wait(act, pv, g, n - 2)
                act.activation(pT[n % 2][:, :, :], ps_t[n % 2][:, :, :], ACT.Copy).then_inc(pT_ready.sem, 1)

            def copy_o(g, n):
                wait(act, pv, g, n)
                wait(act, o_put[n % 2], g, n // 2 - 1)
                act.activation(ov[n % 2][:, :, :], ps_o[n % 2][:, :, :], ACT.Copy).then_inc(o_ready.sem, 1)

            def body(g, more):
                for n in range(NU):
                    hq, s = n // G, n % G
                    if n:
                        copy_pT(g, n - 1)
                    if hq + 1 < NQ:
                        query(g, hq + 1, s)
                    exp(g, n)
                    if n:
                        copy_o(g, n - 1)
                if more:
                    for j in range(HQ):
                        query(g + 1, 0, j)
                copy_pT(g, NU - 1)
                copy_o(g, NU - 1)

            for j in range(HQ):
                query(0, 0, j)
            groups(act, body)

        @block.vector
        def _(dve):
            masked.open(dve)
            dve.wait_ge(consts, 4)

            def query(g, hq, j):
                wait(dve, q_mm, g, 6 * hq + (1, 4)[j])
                dve.tensor_copy(qr[hq % 2][:, j, :], ps_q[(1, 4)[j] % 2][:, :]).then_inc(qr_ready.sem, 1)

            def softmax(g, n):
                p, mx, sm = prob[n % 2], top[n % 2], total[n % 2]
                wait(dve, scored, g, n)
                wait(dve, p_turned, g, n - 2)
                dve.tensor_tensor(p[:, :, :], ps_s[n % 2][:, :, :], over_heads(mask[:, :], HQ), ALU.add).then_inc(masked.sem, 1)
                wait(dve, masked, g, n)
                dve.tensor_reduce(mx[:, :], p[:, :, :], AX.X, ALU.max).then_inc(maxed.sem, 1)
                wait(dve, maxed, g, n)
                dve.tensor_tensor(p[:, :, :], p[:, :, :], along(mx[:, :], S), ALU.subtract).then_inc(shifted.sem, 1)

            def divide(g, n):
                p, sm = prob[n % 2], total[n % 2]
                wait(dve, exped, g, n)
                dve.tensor_reduce(sm[:, :], p[:, :, :], AX.X, ALU.add).then_inc(summed.sem, 1)
                wait(dve, summed, g, 2 * n)
                dve.reciprocal(sm[:, :], sm[:, :]).then_inc(summed.sem, 1)
                wait(dve, summed, g, 2 * n + 1)
                dve.tensor_tensor(p[:, :, :], p[:, :, :], along(sm[:, :], S), ALU.mult).then_inc(probs.sem, 1)

            def body(g, more):
                for n in range(NU):
                    hq, s = n // G, n % G
                    softmax(g, n)
                    divide(g, n)
                    if hq + 1 < NQ and s % 2 == 0:
                        query(g, hq + 1, s // 2)
                if more:
                    query(g + 1, 0, 0)
                    query(g + 1, 0, 1)

            query(0, 0, 0)
            query(0, 0, 1)
            groups(dve, body)


class RopeTables:

    HF = HD // 2
    ROUND = 1.5 * 2.0 ** 23
    STEPS = 7

    def __init__(self, ctx, pos_ctx, pos_x, inv_freq, k_norm_w, q_norm_w, tables):
        sb, HF = ctx.sb, self.HF
        self.src = pos_ctx, pos_x, inv_freq, k_norm_w, q_norm_w
        self.tables = tables
        self.pos_i = sb("pos_i", [P, 4, B], I32)
        self.pos = sb("pos", [P, B, 4])
        self.freq = sb("freq", [P, HF])
        self.w = [sb(f"{n}_norm_w", [P, HD]) for n in "kq"]
        self.w_rot = [sb(f"{n}_norm_w_rot", [P, HD]) for n in "kq"]
        self.turns = sb("turns", [P, 4, HF])
        self.ang = [sb(f"ang{i}", [P, 4, HF]) for i in range(2)]
        self.sin = [sb(f"sin{i}", [P, 4, HF]) for i in range(2)]
        self.cos = [sb(f"cos{i}", [P, 4, HF]) for i in range(2)]
        self.tab = [sb(f"tab{i}", [P, 5, 2, HD]) for i in range(2)]
        self.loaded, self.zeroed, self.ready = (ctx.sem(n) for n in ("rope_loaded", "rope_zeroed", "rope_ready"))
        self.reduced = ctx.ev("angle_steps", self.STEPS)
        self.sines = ctx.ev("sines", 2)
        self.cosine = ctx.ev("cosine_steps", 2)
        self.made = ctx.ev("tables_made", 1)
        self.put = [ctx.ev(f"tables_stored{i}", 1, 1, 16) for i in range(2)]
        self.ticks = ctx.sem("rope_ticks")

    def load(self, sp):
        pos_ctx, pos_x, inv_freq, k_norm_w, q_norm_w = self.src
        for i in range(2):
            self.put[i].open(sp)
        sp.wait_ge(self.zeroed, 1)
        sp.dma_start(self.pos_i[0:CT, 0:3, :], pos_ctx).then_inc(self.loaded, 16)
        sp.dma_start(self.pos_i[0:S, 3, :], pos_x).then_inc(self.loaded, 16)
        sp.dma_start(self.freq[:, :], inv_freq).then_inc(self.loaded, 16)
        sp.dma_start(self.w[0][:, :], k_norm_w).then_inc(self.loaded, 16)
        sp.dma_start(self.w[1][:, :], q_norm_w).then_inc(self.loaded, 16)

    def store(self, sp, b, par):
        wait(sp, self.made, b)
        carry(sp, b, self.ticks)
        sp.dma_start(self.tables[b], self.tab[par][:, :, :, :]).then_inc(self.put[par].sem, 16)

    def prepare(self, dve):
        HF = self.HF
        dve.memset(self.pos_i[:, :, :], 0).then_inc(self.zeroed, 1)
        dve.wait_ge(self.loaded, 80)
        dve.tensor_copy(self.pos[:, :, :], self.pos_i[:, :, :].rearrange("p t b -> p b t")).then_inc(self.ready, 1)
        for w, rot in zip(self.w, self.w_rot):
            dve.tensor_scalar(rot[:, 0:HF], w[:, HF:HD], -1.0, None, ALU.mult).then_inc(self.ready, 1)
            dve.tensor_copy(rot[:, HF:HD], w[:, 0:HF]).then_inc(self.ready, 1)
        dve.wait_ge(self.ready, 5)

    def angles(self, dve, b, par):
        HF, step = self.HF, [0]
        ang, turns = self.ang[par][:, :, :], self.turns[:, :, :]

        def then(ins):
            ins.then_inc(self.reduced.sem, 1)
            wait(dve, self.reduced, b, step[0])
            step[0] += 1

        if not isinstance(b, int) or b > 1:
            wait(dve, self.sines, b, -3)
        pos = self.pos[:, bass.ds(b, 1), :].rearrange("p o t -> p (o t)")
        then(dve.tensor_tensor(ang, along(pos, HF), over_heads(self.freq[:, :], 4), ALU.mult))
        then(dve.tensor_scalar(turns, ang, float(1 / (2 * np.pi)), self.ROUND, ALU.mult, ALU.add))
        then(dve.tensor_scalar(turns, turns, self.ROUND, -PI2[0], ALU.subtract, ALU.mult))
        then(dve.tensor_tensor(ang, ang, turns, ALU.add))
        then(dve.scalar_tensor_tensor(ang, turns, PI2[1] / PI2[0], ang, ALU.mult, ALU.add))
        then(dve.tensor_scalar(ang, ang, 3.1415925, None, ALU.min))
        then(dve.tensor_scalar(ang, ang, -3.1415925, None, ALU.max))

    def sine(self, act, b, par):
        wait(act, self.reduced, b, self.STEPS - 1)
        if not isinstance(b, int) or b > 1:
            wait(act, self.made, b, -2)
        ang = self.ang[par][:, :, :]
        act.activation(self.sin[par][:, :, :], ang, ACT.Sin).then_inc(self.sines.sem, 1)
        act.activation(self.cos[par][:, :, :], ang, ACT.Sin, scale=0.5).then_inc(self.sines.sem, 1)

    def make(self, pool, b, h, par):
        sin, cos = self.sin[par], self.cos[par]
        if isinstance(b, int) and b == 0:
            pool.wait_ge(self.ready, 5)
        wait(pool, self.sines, b, 1)
        pool.tensor_tensor(cos[:, :, :], cos[:, :, :], cos[:, :, :], ALU.mult).then_inc(self.cosine.sem, 1)
        wait(pool, self.cosine, b, 0)
        carry(pool, b, self.ticks)
        pool.tensor_scalar(cos[:, :, :], cos[:, :, :], -2.0, 1.0, ALU.mult, ALU.add).then_inc(self.cosine.sem, 1)
        wait(pool, self.cosine, b, 1)
        wait(pool, self.put[par], h, -1)
        for tiles, src, i in ((slice(0, 4), slice(0, 4), 0), (slice(4, 5), slice(3, 4), 1)):
            n = tiles.stop - tiles.start
            for c, part, w in ((0, cos, self.w[i]), (1, sin, self.w_rot[i])):
                angles = part[:, src, :].unsqueeze(2).broadcast_to((P, n, 2, self.HF))
                weights = w[:, :].rearrange("p (h f) -> p h f", h=2).unsqueeze(1).broadcast_to((P, n, 2, self.HF))
                out = self.tab[par][:, tiles, c, :].rearrange("p t (h f) -> p t h f", h=2)
                ins = pool.tensor_tensor(out, angles, weights, ALU.mult)
        ins.then_inc(self.made.sem, 1)


def project_out(nc, oT, w_src, res, store_x, store_xT, rope=None, router=None, keep=None):
    CH = HQ * P
    ctx = Phase(nc, "out2" if router is not None else "out1")
    with ctx:
        sb = ctx.sb
        ev = ctx.ev
        ident = sb("ident", [P, P])
        w_raw = sb("w_raw", [P, 4, D])
        w_hi = sb("w_hi", [P, H, D], F32R)
        w_lo = sb("w_lo", [P, H, D], F32R)
        o_raw = sb("o_raw", [P, NQ, HQ, P])
        o_hi = sb("o_hi", [P, NQ, HQ, P], F32R)
        o_lo = sb("o_lo", [P, NQ, HQ, P], F32R)
        r_in = [sb(f"r_in{i}", [P, D]) for i in range(2)]
        y = [sb(f"y{i}", [P, D]) for i in range(2)]
        yn = [sb(f"yn{i}", [P, D]) for i in range(2)]
        layer = LayerNorm(ctx, P)
        minus_half = sb("minus_half", [P, 1])
        half_ready = ctx.sem("minus_half_ready")
        xh = [sb(f"xh{i}", [P, KD, P], F32R) for i in range(2)]
        xl = [sb(f"xl{i}", [P, KD, P], F32R) for i in range(2)]
        ps_y = [ctx.bank(f"ps_y{i}", P, D) for i in range(2)]
        ps_x = [ctx.bank(f"ps_x{i}", P, KD, P) for i in range(2)]
        ps_r = ctx.bank("ps_r", P, TOTAL)
        id_ready = ctx.sem("id_ready")
        w_in = [ctx.sem(f"w_loaded{i}") for i in range(4)]
        w_hi_ready = ctx.sem("w_hi_ready")
        w_lo_ready = ctx.sem("w_lo_ready")
        o_in = [ev(f"o_loaded{c}", 1, step=16) for c in range(NQ)]
        o_hi_ready, o_lo_ready = ev("o_hi_ready", NQ), ev("o_lo_ready", NQ)
        used = ev("o_used", NQ, NQ)
        r_loaded = [ev(f"r_loaded{i}", 1, step=16) for i in range(2)]
        added = ev("y_added", 1, 2)
        normed = ev("y_normed", 1)
        turned = ev("y_turned", 1, 2)
        hi, lo = ev("x_hi", 1), ev("x_lo", 1)
        y_put = [ev(f"y_stored{i}", 1, 1, 16) for i in range(2)]
        x_put = [ev(f"xT_stored{i}", 2, 2, 16) for i in range(2)]
        ticks = ctx.sem("ticks")
        if rope is not None:
            guest = RopeTables(ctx, *rope)
        if router is not None:
            cls_src, bias_src = router
            acc, oh, place, weight, run, rows_n, tokens = keep
            cls = sb("cls", [P, KD, TOTAL])
            cls_hi = sb("cls_hi", [P, KD, TOTAL], F32R)
            cls_lo = sb("cls_lo", [P, KD, TOTAL], F32R)
            bias = sb("bias", [P, TOTAL])
            iota = sb("iota", [P, TOTAL])
            iota_i = sb("iota_i", [P, TOTAL], I32)
            small = sb("small", [P, 4])
            prob = sb("prob", [P, TOTAL])
            biased = sb("biased", [P, TOTAL])
            best = sb("best", [P, 8])
            best_i = sb("best_i", [P, 8], U32)
            best_f = sb("best_f", [P, 8])
            share = sb("share", [P, TOTAL])
            hot = sb("hot", [P, 2, TOTAL])
            chosen = sb("chosen", [P, TOTAL])
            below = sb("below", [P, P])
            ones = sb("ones", [P, P])
            spot = sb("spot", [P, TOTAL])
            spots = sb("spots", [P, 2, TOTAL])
            dest = sb("dest", [P, 2])
            dest_i = [sb(f"dest_i{i}", [P, 2], U32) for i in range(2)]
            base = sb("base", [P, TOTAL])
            base_i = sb("base_i", [P, TOTAL], I32)
            ids_i = sb("ids_i", [P, TT], I32)
            ids_f = sb("ids_f", [P, TT])
            id_i = [sb(f"id_i{i}", [P, 1], I32) for i in range(2)]
            fill = sb("fill", [P, (DUMP + P) // P], I32)
            ps_c = ctx.bank("ps_c", P, 2, E)
            list_ready = ctx.sem("list_filled")
            zeroed = ctx.sem("list_zeros")
            tables_ready = ctx.sem("place_tables")
            counted = ev("choices_counted", 1)
            p_step = ev("place_step", 5)
            scattered = ev("tokens_listed", 2, 0, 16)
            r_src = ctx.sem("router_loaded")
            r_split = ctx.sem("router_split")
            logits = ev("logits", 1)
            r_step = ev("route_step", 11)
            r_exp = ev("route_exp", 1)
            r_done = ev("routed", 1)
        block = ctx.enter_context(nc.Block())

        @block.sync
        def _(sp):
            for i in range(2):
                y_put[i].open(sp)
                x_put[i].open(sp)
            if rope is not None:
                guest.load(sp)
            if router is not None:
                sp.dma_start(cls[:, :, :], cls_src).then_inc(r_src, 16)
                sp.dma_start(bias[:, :], bias_src).then_inc(r_src, 16)
                sp.wait_ge(zeroed, 1)
                sp.dma_start(tokens.rearrange("(p n) o -> p (n o)", p=P), fill[:, :]).then_inc(list_ready, 16)

            def load(t, h, par):
                cols = bass.ds(t * P, P)
                for c in range(NQ):
                    if not isinstance(t, int) or t:
                        wait(sp, o_lo_ready, t, c - NQ)
                    sp.dma_start(o_raw[:, c, :, :], oT[:, c * HQ:(c + 1) * HQ, cols]).then_inc(o_in[c].sem, 16)
                wait(sp, added, t, -2)
                sp.dma_start(r_in[par][:, :], res[cols, :]).then_inc(r_loaded[par].sem, 16)

            def store(t, h, par):
                cols = bass.ds(t * P, P)
                if store_x is not None:
                    wait(sp, added, t)
                    sp.dma_start(store_x[cols, :], y[par][:, :]).then_inc(y_put[par].sem, 16)
                else:
                    wait(sp, normed, t)
                    sp.dma_start(rows_n[cols, :], yn[par][:, :]).then_inc(y_put[par].sem, 16)
                    return
                wait(sp, lo, t)
                carry(sp, t, ticks)
                dst_hi, dst_lo = store_xT
                sp.dma_start(dst_hi[:, :, cols], xh[par][:, :, :].bitcast(F32)).then_inc(x_put[par].sem, 16)
                sp.dma_start(dst_lo[:, :, cols], xl[par][:, :, :].bitcast(F32)).then_inc(x_put[par].sem, 16)

            for h in range(H):
                if h >= 4:
                    sp.wait_ge(w_lo_ready, h - 3)
                sp.dma_start(w_raw[:, h % 4, :], w_src[:, h, :]).then_inc(w_in[h % 4], 16)
                if h % 4 == 3 and h < 4:
                    load(0, 0, 0)
            load(1, 0, 1)
            with sp.Fori(0, TT // 2 - 1) as h:
                for par in range(2):
                    load(h * 2 + 2 + par, h + 1, par)
                    store(h * 2 + par, h, par)
                    if rope is not None:
                        guest.store(sp, h * 2 + par, par)
            for par in range(2):
                store(TT - 2 + par, TT // 2 - 1, par)
                if rope is not None:
                    guest.store(sp, TT - 2 + par, par)
            if rope is not None:
                for par in range(2):
                    guest.store(sp, TT + par, par)
            for par in range(2):
                if rope is not None:
                    sp.wait_ge(guest.put[par].sem, guest.put[par].at(B // 2 - 1))
                sp.wait_ge(y_put[par].sem, y_put[par].at(TT // 2 - 1))
                if store_xT is not None:
                    sp.wait_ge(x_put[par].sem, x_put[par].at(TT // 2 - 1, 1))

        @block.gpsimd
        def _(pool):
            identity(pool, ident[:, :], id_ready)
            if router is not None:
                pool.iota(iota_i[:, :], pattern=[[1, TOTAL]], base=0, channel_multiplier=0).then_inc(id_ready, 1)
                pool.wait_ge(id_ready, 3)
                pool.tensor_copy(iota[:, :], iota_i[:, :]).then_inc(id_ready, 1)
                pool.memset(fill[:, :], 0).then_inc(zeroed, 1)
                pool.iota(ids_i[:, :], pattern=[[P, TT]], base=0, channel_multiplier=1).then_inc(tables_ready, 1)
                pool.iota(base_i[:, 0:E], pattern=[[REGION, E]], base=0, channel_multiplier=0).then_inc(tables_ready, 1)
                pool.iota(base_i[:, E:TOTAL], pattern=[[0, TOTAL - E]], base=DUMP, channel_multiplier=1)\
                    .then_inc(tables_ready, 1)
                pool.memset(ones[:, :], 1.0).then_inc(tables_ready, 1)
                pool.wait_ge(tables_ready, 4)
                pool.tensor_copy(ids_f[:, :], ids_i[:, :]).then_inc(tables_ready, 1)
                pool.tensor_copy(base[:, :], base_i[:, :]).then_inc(tables_ready, 1)
                pool.affine_select(out=below[:, :], in_=ones[:, :], compare_op=ALU.is_ge, fill=0.0, base=-1,
                                   pattern=[[1, P]], channel_multiplier=-1).then_inc(tables_ready, 1)
                pool.wait_ge(r_src, 32)
                pool.tensor_copy(cls_hi[:, :, :], cls[:, :, :]).then_inc(r_split, 1)
                pool.wait_ge(r_split, 1)
                pool.tensor_tensor(cls_lo[:, :, :], cls[:, :, :], cls_hi[:, :, :], ALU.subtract).then_inc(r_split, 1)
            exponent(pool, minus_half[:, :], half_ready)
            if rope is not None:
                guest.make(pool, 0, 0, 0)

            def scatter(t, par):
                for c in range(2):
                    if c == 0:
                        wait(pool, p_step, t, 4)
                    if c or not isinstance(t, int) or t:
                        wait(pool, scattered, t, c - 1)
                    carry(pool, t, ticks)
                    pool.indirect_dma_start(tokens, bass.IndirectOffsetOnAxis(ap=dest_i[par][:, c:c + 1], axis=0),
                                            id_i[par][:, :], None).then_inc(scattered.sem, 16)

            if router is not None:
                pool.wait_ge(list_ready, 16)
            for par in range(2):
                layer.root(pool, par, minus_half)
                if rope is not None:
                    guest.make(pool, par + 1, par, 1 - par)

            def pair(h):
                for par in range(2):
                    layer.root(pool, h * 2 + par, minus_half)
                    if rope is not None:
                        guest.make(pool, h * 2 + par + 1, h + par, 1 - par)
                    if router is not None:
                        scatter(h * 2 + par - 2, par)

            pair(1)
            with pool.Fori(2, TT // 2) as h:
                pair(h)
            if rope is not None:
                guest.make(pool, B - 1, B // 2 - 1, 1)
            if router is not None:
                scatter(TT - 2, 0)
                scatter(TT - 1, 1)
                pool.wait_ge(scattered.sem, scattered.at(TT - 1, 1))

        @block.scalar
        def _(act):
            def high(t, c):
                wait(act, o_in[c], t)
                wait(act, used, t, c - NQ)
                act.activation(o_hi[:, c, :, :], o_raw[:, c, :, :], ACT.Copy).then_inc(o_hi_ready.sem, 1)

            def turn(t, h, par):
                wait(act, turned, t)
                if store_xT is not None:
                    wait(act, x_put[par], h, -1)
                elif not (isinstance(t, int) and t < 2):
                    wait(act, logits, t, -2)
                act.activation(xh[par][:, :, :], ps_x[par][:, :, :], ACT.Copy).then_inc(hi.sem, 1)

            def route(t):
                wait(act, r_step, t, 0)
                act.activation(prob[:, :], ps_r[:, :], ACT.Exp, bias=small[:, 0:1],
                               accum_out=small[:, 1:2]).then_inc(r_exp.sem, 1)

            def body(t, h, par, ahead=True):
                if ahead:
                    high(t + 2, 0)
                if router is not None and not (isinstance(t, int) and t == 0):
                    route(t - 1)
                turn(t, h, par)
                if ahead:
                    high(t + 2, 1)
                    high(t + 2, 2)
                if rope is not None:
                    guest.sine(act, t + 2, par)
                if ahead:
                    high(t + 2, 3)

            if rope is not None:
                guest.sine(act, 0, 0)
                guest.sine(act, 1, 1)
            for h in range(H):
                act.wait_ge(w_in[h % 4], 16 * (h // 4 + 1))
                act.activation(w_hi[:, h, :], w_raw[:, h % 4, :], ACT.Copy).then_inc(w_hi_ready, 1)
                if h % 4 == 3:
                    high(0, h // 4)
            for c in range(NQ):
                high(1, c)
            for par in range(2):
                body(par, 0, par)
            with act.Fori(1, TT // 2 - 1) as h:
                body(h * 2, h, 0)
                body(h * 2 + 1, h, 1)
            for par in range(2):
                body(TT - 2 + par, TT // 2 - 1, par, ahead=False)
            if router is not None:
                route(TT - 1)

        @block.vector
        def _(dve):
            added.open(dve)

            def low(t, c):
                wait(dve, o_hi_ready, t, c)
                dve.tensor_tensor(o_lo[:, c, :, :], o_raw[:, c, :, :], o_hi[:, c, :, :], ALU.subtract).then_inc(o_lo_ready.sem, 1)

            def norm(t, h, par):
                wait(dve, r_loaded[par], h)
                wait(dve, used, t, NQ - 1)
                wait(dve, y_put[par], h, -1)
                if router is not None and not (isinstance(t, int) and t < 2):
                    wait(dve, r_done, t, -2)
                dve.tensor_tensor(y[par][:, :], ps_y[par][:, :], r_in[par][:, :], ALU.add).then_inc(added.sem, 1)
                wait(dve, added, t)
                wait(dve, turned, t, -2)
                layer.vector(dve, t, yn[par][:, :], y[par][:, :]).then_inc(normed.sem, 1)

            def turn(t, h, par):
                wait(dve, hi, t)
                dve.tensor_tensor(xl[par][:, :, :], ps_x[par][:, :, :], xh[par][:, :, :], ALU.subtract).then_inc(lo.sem, 1)

            def route(t, par):
                m, total, inv, back = (small[:, i:i + 1] for i in range(4))

                def then(n, ins):
                    ins.then_inc(r_step.sem, 1)
                    wait(dve, r_step, t, n)

                wait(dve, logits, t)
                then(0, dve.tensor_reduce(m, ps_r[:, :], AX.X, ALU.max, negate=True))
                wait(dve, r_exp, t)
                then(1, dve.reciprocal(inv, total))
                then(2, dve.tensor_scalar(prob[:, :], prob[:, :], inv, None, ALU.mult))
                then(3, dve.tensor_tensor(biased[:, :], prob[:, :], bias[:, :], ALU.add))
                carry(dve, t, ticks)
                then(4, dve.max(best[:, :], biased[:, :]))
                carry(dve, t, ticks)
                then(5, dve.max_index(best_i[:, :], best[:, :], biased[:, :]))
                then(6, dve.tensor_copy(best_f[:, :], best_i[:, :]))
                for c in range(2):
                    ins = dve.tensor_scalar(hot[:, c, :], iota[:, :], best_f[:, c:c + 1], None, ALU.is_equal)
                then(7, ins)
                then(8, dve.tensor_tensor(chosen[:, :], hot[:, 0, :], hot[:, 1, :], ALU.add))
                dve.tensor_tensor(oh[:, bass.ds(t, 1), :], hot[:, :, :].rearrange("p c e -> p (c e)").unsqueeze(1),
                                  hot[:, :, :].rearrange("p c e -> p (c e)").unsqueeze(1), ALU.mult)
                then(9, dve.scalar_tensor_tensor(share[:, :], chosen[:, :], ROUTE_SCALE, prob[:, :],
                                                 ALU.mult, ALU.mult))
                dve.tensor_scalar(weight[:, bass.ds(t, 1), :], share[:, :].unsqueeze(1), 1.0, None, ALU.mult)
                then(10, dve.tensor_reduce(back, share[:, E:TOTAL], AX.X, ALU.add))
                dve.scalar_tensor_tensor(acc[:, t, :], yn[par][:, :], back, y[par][:, :], ALU.mult, ALU.add)\
                    .then_inc(r_done.sem, 1)

            def locate(t, par):
                def then(n, ins):
                    ins.then_inc(p_step.sem, 1)
                    wait(dve, p_step, t, n)

                wait(dve, counted, t)
                if not isinstance(t, int) or t > 1:
                    wait(dve, scattered, t, -3)
                then(0, dve.tensor_tensor(place[:, t, :], ps_c[:, 0, :], run[:, :], ALU.add))
                dve.tensor_tensor(run[:, :], ps_c[:, 1, :], run[:, :], ALU.add)
                dve.tensor_scalar(id_i[par][:, :], ids_f[:, bass.ds(t, 1)], 0.0, None, ALU.add)
                then(1, dve.tensor_tensor(spot[:, 0:E], place[:, t, :], base[:, 0:E], ALU.add))
                then(2, dve.tensor_tensor(spots[:, :, :], oh[:, t, :].rearrange("p (c e) -> p c e", c=2),
                                          over_heads(spot[:, :], 2), ALU.mult))
                then(3, dve.tensor_reduce(dest[:, :], spots[:, :, :], AX.X, ALU.add))
                then(4, dve.tensor_copy(dest_i[par][:, :], dest[:, :]))

            def body(t, h, par, ahead=True):
                norm(t, h, par)
                if ahead:
                    low(t + 2, 0)
                if router is not None and not (isinstance(t, int) and t == 0):
                    route(t - 1, 1 - par)
                turn(t, h, par)
                if ahead:
                    low(t + 2, 1)
                if rope is not None:
                    guest.angles(dve, t + 2, par)
                if router is not None and not (isinstance(t, int) and t < 2):
                    locate(t - 2, par)
                if ahead:
                    low(t + 2, 2)
                    low(t + 2, 3)

            if rope is not None:
                guest.prepare(dve)
                guest.angles(dve, 0, 0)
                guest.angles(dve, 1, 1)
            if router is not None:
                dve.wait_ge(r_src, 32)
                dve.wait_ge(id_ready, 4)
                dve.wait_ge(tables_ready, 7)
                dve.memset(run[:, :], 0.0).then_inc(tables_ready, 1)
                dve.tensor_copy(spot[:, :], base[:, :]).then_inc(tables_ready, 1)
                dve.wait_ge(tables_ready, 9)
            for h in range(H):
                dve.wait_ge(w_hi_ready, h + 1)
                dve.tensor_tensor(w_lo[:, h, :], w_raw[:, h % 4, :], w_hi[:, h, :], ALU.subtract).then_inc(w_lo_ready, 1)
                if h % 4 == 3:
                    low(0, h // 4)
            for c in range(NQ):
                low(1, c)
            for t in range(4):
                body(t, t // 2, t % 2)
            with dve.Fori(2, TT // 2 - 1) as h:
                body(h * 2, h, 0)
                body(h * 2 + 1, h, 1)
            for par in range(2):
                body(TT - 2 + par, TT // 2 - 1, par, ahead=False)
            if router is not None:
                route(TT - 1, 1)
                locate(TT - 2, 0)
                locate(TT - 1, 1)

        @block.tensor
        def _(pe):
            used.open(pe)
            turned.open(pe)
            pe.wait_ge(id_ready, 2)

            def project(t, par, chunks):
                for c in chunks:
                    wait(pe, o_lo_ready, t, c)
                    if c == 0 and (not isinstance(t, int) or t > 1):
                        wait(pe, added, t, -2)
                    for j in range(HQ):
                        h = c * HQ + j
                        if isinstance(t, int) and t == 0:
                            pe.wait_ge(w_lo_ready, h + 1)
                        mm = mm3(pe, ps_y[par][:, :], o_hi[:, c, j, :], o_lo[:, c, j, :], w_hi[:, h, :], w_lo[:, h, :],
                                 h == 0, h == H - 1)
                    mm.then_inc(used.sem, 1)

            def turn(t, par):
                wait(pe, normed, t)
                if not isinstance(t, int) or t > 1:
                    wait(pe, lo, t, -2)
                for k in range(KD):
                    mm = pe.transpose(ps_x[par][:, k, :], yn[par][:, k * P:(k + 1) * P], ident[:, :])
                mm.then_inc(turned.sem, 1)

            def route(t, par):
                wait(pe, lo, t)
                if isinstance(t, int) and t == 0:
                    pe.wait_ge(r_split, 2)
                else:
                    wait(pe, r_done, t, -1)
                for k in range(KD):
                    mm = mm3(pe, ps_r[:, :], xh[par][:, k, :], xl[par][:, k, :], cls_hi[:, k, :], cls_lo[:, k, :],
                             k == 0, k == KD - 1)
                mm.then_inc(logits.sem, 1)

            def count(t):
                wait(pe, r_done, t)
                if isinstance(t, int) and t == 0:
                    pe.wait_ge(tables_ready, 7)
                else:
                    wait(pe, p_step, t, -1)
                pe.matmul(ps_c[:, 0, :], below[:, :], chosen[:, 0:E], start=True, stop=True)
                pe.matmul(ps_c[:, 1, :], ones[:, :], chosen[:, 0:E], start=True, stop=True).then_inc(counted.sem, 1)

            def body(t, par, last=False):
                if not last:
                    project(t + 1, 1 - par, (0, 1))
                turn(t, par)
                if not last:
                    project(t + 1, 1 - par, (2, 3))
                if router is not None:
                    if not (isinstance(t, int) and t == 0):
                        count(t - 1)
                    route(t, par)
                    if last:
                        count(t)

            project(0, 0, range(NQ))
            body(0, 0)
            body(1, 1)
            with pe.Fori(1, TT // 2 - 1) as h:
                body(h * 2, 0)
                body(h * 2 + 1, 1)
            body(TT - 2, 0)
            body(TT - 1, 1, last=True)


def cross_attention(nc, ctxT, xT_hi, xT_lo, wqT, wkT, wvT, tables, oT):
    M = (CT, CT, CT, S)
    HF = HD // 2
    ctx = Phase(nc, "ca")
    with ctx:
        sb = ctx.sb
        ev = ctx.ev
        ident = sb("ident", [P, P])
        NW = (H * HD + 2 * D) // D
        w_hi = sb("w_hi", [P, NW, KD, D], F32R)
        w_lo = sb("w_lo", [P, NW, KD, D], F32R)
        w_src = [wqT[:, :, i * D:(i + 1) * D] for i in range(4)] + [wkT, wvT]
        W_ORDER = (0, 4, 5, 1, 2, 3)
        WK, WV = 4, 5
        c_raw = sb("c_raw", [P, KD, C])
        c_hi = [sb(f"c_hi{i}", [P, KD, CT], F32R) for i in range(2)]
        c_lo = [sb(f"c_lo{i}", [P, KD, CT], F32R) for i in range(2)]
        xh = [sb(f"xh{i}", [P, KD, S], F32R) for i in range(2)]
        xl = [sb(f"xl{i}", [P, KD, S], F32R) for i in range(2)]
        tab = [sb(f"tab{i}", [P, 5, 2, HD]) for i in range(2)]
        qT = sb("qT", [P, KVH, HQ, S])
        kT = [sb(f"kT{i}", [P, KVH, KV]) for i in range(2)]
        v = [sb(f"v{i}", [P, 4, KVH * HD]) for i in range(2)]
        prob = [sb(f"prob{j}", [S, 4 * CT]) for j in range(HQ)]
        top = sb("top", [S, HQ])
        down = sb("down", [S, HQ])
        total = sb("total", [S, HQ])
        inv = sb("inv", [S, HQ])
        pT = [sb(f"pT{i}", [P, 4, HQ, S]) for i in range(2)]
        ov = [sb(f"ov{i}", [P, HQ, S]) for i in range(2)]
        sq = sb("sq", [P, D])
        q1, q2, k1, k2 = (sb(n, [P, D]) for n in ("q1", "q2", "k1", "k2"))
        ssum = sb("ssum", [P, 2, HQ])
        k_rstd = sb("k_rstd", [P, HQ])
        minus_half = sb("minus_half", [P, HQ])
        half_ready = ctx.sem("minus_half_ready")
        q_scale = [sb(f"q_scale{i}", [S, KVH, HQ]) for i in range(2)]
        ps_p = [ctx.bank(f"ps_p{i}", P, D) for i in range(2)]
        ps_s = [ctx.bank(f"ps_s{i}", S, KV) for i in range(2)]
        ps_t = [ctx.bank(f"ps_t{i}", P, 4, S) for i in range(2)]
        ps_r = ctx.bank("ps_r", P, HQ * P)
        ps_o = ctx.bank("ps_o", P, HQ, S)
        id_ready = ctx.sem("id_ready")
        padded = ctx.sem("prob_padded")
        w_in = [ctx.sem(f"w_loaded{i}") for i in range(2)]
        w_hi_ready = ctx.sem("w_hi_ready")
        w_lo_ready = ctx.sem("w_lo_ready")
        c_in = ev("ctx_loaded", 1, step=16)
        c_hi_ready, c_lo_ready = ev("ctx_hi", 3), ev("ctx_lo", 3)
        x_in = [ctx.sem(f"x_loaded{i}") for i in range(2)]
        q_mm, k_mm, v_mm = ev("q_projected", 4), ev("k_projected", 4), ev("v_projected", 4)
        q_sq, k_sq = ev("q_squared", 4), ev("k_squared", 4)
        q_rot, k_rot = ev("q_products", 4), ev("k_products", 4)
        q_sum, k_sum = ev("q_squares_summed", 8, 1), ev("k_squares_summed", 8, 1)
        q_scaled, k_scaled = ev("q_scale_ready", 4), ev("k_rstd_ready", 4)
        q_added, k_added = ev("q_rotated", 4), ev("k_added", 4)
        k_normed = ev("k_rotated", 4)
        q_turned, k_turned = ev("q_turned", 4), ev("k_turned", 4)
        qT_ready, kT_ready = ev("qT_ready", 4), ev("kT_ready", 4)
        v_ready = ev("v_ready", 4)
        N = KVH * HQ
        scored = ev("scored", N)
        maxed, shifted = ev("maxed", N), ev("shift_ready", N)
        exped = ev("exped", N, 2)
        inverted = ev("inverted", N)
        probs = ev("probs", N)
        p_turned = ev("p_turned", N, HQ)
        pT_ready = ev("pT_ready", N, 2)
        pv = ev("weighted", 4, 8)
        o_ready = ev("o_ready", 4, 1)
        o_put = [ev(f"o_stored{i}", 2, 1, 16) for i in range(2)]
        block = ctx.enter_context(nc.Block())

        def inputs(eng, b, par):
            eng.wait_ge(x_in[par], b * 24 + 48 - 24 * par)

        def batches(eng, project, step):
            for i in range(4):
                project(0, i, 0)
            with eng.Fori(0, B // 2 - 1) as h:
                for par in range(2):
                    for i in range(4):
                        step(h * 2 + par, i, par, True)
            for i in range(4):
                step(B - 2, i, 0, True)
            for i in range(4):
                step(B - 1, i, 1, False)

        @block.sync
        def _(sp):
            for i in range(2):
                o_put[i].open(sp)

            def load(b, h, par):
                cols = bass.ds(b * S, S)
                if not isinstance(b, int) or b:
                    wait(sp, c_lo_ready, b, -1)
                sp.dma_start(c_raw[:, :, :], ctxT[b]).then_inc(c_in.sem, 16)
                if not isinstance(b, int) or b > 1:
                    wait(sp, v_mm, b, -5)
                    wait(sp, q_mm, b, -5)
                    wait(sp, q_rot, b, -5)
                    wait(sp, k_rot, b, -5)
                sp.dma_start(xh[par][:, :, :].bitcast(F32), xT_hi[:, :, cols]).then_inc(x_in[par], 16)
                sp.dma_start(xl[par][:, :, :].bitcast(F32), xT_lo[:, :, cols]).then_inc(x_in[par], 16)
                sp.dma_start(tab[par][:, :, :, :], tables[b]).then_inc(x_in[par], 16)

            def store(b, i):
                wait(sp, o_ready, b, i)
                sp.dma_start(oT[:, i * HQ:(i + 1) * HQ, bass.ds(b * S, S)], ov[i % 2][:, :, :])\
                    .then_inc(o_put[i % 2].sem, 16)

            load(0, 0, 0)
            for n in range(NW):
                if n >= 2:
                    sp.wait_ge(w_lo_ready, n - 1)
                sp.dma_start(v[n % 2][:, :, :], w_src[W_ORDER[n]]).then_inc(w_in[n % 2], 16)
            load(1, 0, 1)
            with sp.Fori(0, B // 2 - 1) as h:
                for par in range(2):
                    store(h * 2 + par, 0)
                    store(h * 2 + par, 1)
                    load(h * 2 + par + 2, h + 1, par)
                    store(h * 2 + par, 2)
                    store(h * 2 + par, 3)
            for b in (B - 2, B - 1):
                for i in range(4):
                    store(b, i)
            for i in range(2):
                sp.wait_ge(o_put[i].sem, o_put[i].at(B - 1, 1))

        @block.gpsimd
        def _(pool):
            identity(pool, ident[:, :], id_ready)
            exponent(pool, minus_half[:, :], half_ready)
            for j in range(HQ):
                pool.memset(prob[j][:, KV:4 * CT], 0.0).then_inc(padded, 1)

            def low(b, t, par):
                wait(pool, c_hi_ready, b, t)
                slot = (par + t) % 2
                pool.tensor_tensor(c_lo[slot][:, :, :], c_raw[:, :, t * CT:(t + 1) * CT], c_hi[slot][:, :, :],
                                   ALU.subtract).then_inc(c_lo_ready.sem, 1)

            def project(b, i, par):
                m = M[i]
                wait(pool, q_sum, b, 2 * i + 1)
                pool.tensor_tensor(q_scale[par][:, i, :], ssum[0:S, 0, :], minus_half[0:S, :], ALU.pow).then_inc(q_scaled.sem, 1)
                wait(pool, q_rot, b, i)
                pool.tensor_tensor(q1[0:S, :], q1[0:S, :], q2[0:S, :], ALU.add).then_inc(q_added.sem, 1)
                wait(pool, k_rot, b, i)
                pool.tensor_tensor(k1[0:m, :], k1[0:m, :], k2[0:m, :], ALU.add).then_inc(k_added.sem, 1)
                wait(pool, k_sum, b, 2 * i + 1)
                pool.tensor_tensor(k_rstd[0:m, :], ssum[0:m, 1, :], minus_half[0:m, :], ALU.pow).then_inc(k_scaled.sem, 1)
                wait(pool, k_scaled, b, i)
                wait(pool, k_added, b, i)
                heads = k1[0:m, :].rearrange("p (h d) -> p h d", h=KVH)
                pool.tensor_tensor(heads, heads, along(k_rstd[0:m, :], HD), ALU.mult).then_inc(k_normed.sem, 1)
                if i in (0, 1):
                    low(b, i + 1, par)
                elif i == 3 and not (isinstance(b, int) and b == B - 1):
                    low(b + 1, 0, 1 - par)

            def step(b, i, par, more):
                if more:
                    project(b + 1, i, 1 - par)

            low(0, 0, 0)
            batches(pool, project, step)

        @block.tensor
        def _(pe):
            pe.wait_ge(id_ready, 2)
            pe.wait_ge(padded, HQ)
            p_turned.open(pe)
            pv.open(pe)
            first = lambda b: isinstance(b, int) and b == 0

            def weights(b, c):
                if first(b):
                    pe.wait_ge(w_lo_ready, W_ORDER.index(c) + 1)

            def project(b, i, unit, par):
                out = ps_p[(3 * i + unit) % 2]
                done = (q_mm, k_mm, v_mm)[unit]
                c = (i, WK, WV)[unit]
                weights(b, c)
                if i == 0 and unit == 0:
                    inputs(pe, b, par)
                if unit == 0 or i == 3:
                    m, a_hi, a_lo = S, xh[par], xl[par]
                else:
                    slot = (par + i) % 2
                    m, a_hi, a_lo = CT, c_hi[slot], c_lo[slot]
                    wait(pe, c_lo_ready, b, i)
                if unit == 2:
                    wait(pe, q_rot, b, i)
                    wait(pe, q_sq, b, i)
                elif unit == 0 and not (first(b) and i == 0):
                    wait(pe, k_rot, b, i - 1)
                    wait(pe, k_sq, b, i - 1)
                elif unit == 1 and not (first(b) and i == 0):
                    wait(pe, v_ready, b, i - 1)
                for k in range(KD):
                    mm = mm3(pe, out[0:m, :], a_hi[:, k, :], a_lo[:, k, :], w_hi[:, c, k, :], w_lo[:, c, k, :],
                             k == 0, k == KD - 1)
                mm.then_inc(done.sem, 1)

            def turn_q(b, i):
                wait(pe, q_added, b, i)
                if not (first(b) and i == 0):
                    wait(pe, kT_ready, b, i - 1)
                for j in range(HQ):
                    mm = pe.transpose(ps_r[:, j * S:(j + 1) * S], q1[0:S, j * HD:(j + 1) * HD], ident[0:S, 0:S])
                mm.then_inc(q_turned.sem, 1)

            def turn_k(b, i):
                m = M[i]
                wait(pe, k_normed, b, i)
                wait(pe, qT_ready, b, i)
                for j in range(KVH):
                    mm = pe.transpose(ps_r[:, j * m:(j + 1) * m], k1[0:m, j * HD:(j + 1) * HD], ident[0:m, 0:m])
                mm.then_inc(k_turned.sem, 1)

            def score(b, i, j, par):
                if j == 0:
                    wait(pe, qT_ready, b, i)
                    if i == 0:
                        wait(pe, kT_ready, b, 3)
                wait(pe, exped, b, i * HQ + j - 2)
                pe.matmul(ps_s[j % 2][:, :], qT[:, i, j, :], kT[par][:, i, :], start=True, stop=True).then_inc(scored.sem, 1)

            def turn(b, i, j):
                n = i * HQ + j
                wait(pe, probs, b, n)
                wait(pe, pT_ready, b, n - 2)
                for t in range(4):
                    mm = pe.transpose(ps_t[j % 2][0:CT, t, :], prob[j][:, t * CT:(t + 1) * CT], ident[0:S, 0:S])
                mm.then_inc(p_turned.sem, 1)

            def weigh(b, i, par):
                wait(pe, pT_ready, b, i * HQ + HQ - 1)
                if i == 0:
                    wait(pe, v_ready, b, 3)
                if not (first(b) and i == 0):
                    wait(pe, o_ready, b, i - 1)
                for t in range(4):
                    mm = pe.matmul(ps_o[:, :, :], v[par][0:M[t], t, i * HD:(i + 1) * HD], pT[i % 2][0:M[t], t, :, :],
                                   start=(t == 0), stop=(t == 3))
                mm.then_inc(pv.sem, 1)

            def start(b, i, par):
                project(b, i, 0, par)
                project(b, i, 1, par)
                turn_q(b, i)
                project(b, i, 2, par)
                turn_k(b, i)

            def step(b, i, par, more):
                score(b, i, 0, par)
                score(b, i, 1, par)
                if more:
                    project(b + 1, i, 0, 1 - par)
                turn(b, i, 0)
                score(b, i, 2, par)
                turn(b, i, 1)
                score(b, i, 3, par)
                if more:
                    project(b + 1, i, 1, 1 - par)
                turn(b, i, 2)
                turn(b, i, 3)
                if more:
                    turn_q(b + 1, i)
                    project(b + 1, i, 2, 1 - par)
                weigh(b, i, par)
                if more:
                    turn_k(b + 1, i)

            batches(pe, start, step)

        @block.scalar
        def _(act):
            def high(b, t, par):
                wait(act, c_in, b)
                if not (isinstance(b, int) and b == 0 and t < 2):
                    wait(act, v_mm, b, (-3, -2, 0)[t])
                act.activation(c_hi[(par + t) % 2][:, :, :], c_raw[:, :, t * CT:(t + 1) * CT], ACT.Copy)\
                    .then_inc(c_hi_ready.sem, 1)

            def square(b, i, unit, par):
                m = (S, M[i])[unit]
                wait(act, (q_mm, k_mm)[unit], b, i)
                if unit == 0:
                    if not (isinstance(b, int) and b == 0 and i == 0):
                        wait(act, k_sum, b, 2 * i - 2)
                else:
                    wait(act, q_sum, b, 2 * i)
                act.activation(sq[0:m, :], ps_p[(3 * i + unit) % 2][0:m, :], ACT.Square)\
                    .then_inc((q_sq, k_sq)[unit].sem, 1)

            def keep_q(b, i):
                wait(act, q_turned, b, i)
                act.activation(qT[:, i, :, :], ps_r[:, 0:HQ * S].rearrange("p (j q) -> p j q", j=HQ), ACT.Copy)\
                    .then_inc(qT_ready.sem, 1)

            def keep_k(b, i, par):
                m = M[i]
                wait(act, k_turned, b, i)
                act.activation(kT[par][:, :, i * CT:i * CT + m],
                               ps_r[:, 0:KVH * m].rearrange("p (h t) -> p h t", h=KVH), ACT.Copy)\
                    .then_inc(kT_ready.sem, 1)

            def keep_v(b, i, par):
                m = M[i]
                wait(act, v_mm, b, i)
                wait(act, pv, b, -5)
                act.activation(v[par][0:m, i, :], ps_p[(3 * i + 2) % 2][0:m, :], ACT.Copy).then_inc(v_ready.sem, 1)

            def exp(b, i, j, par):
                n = i * HQ + j
                wait(act, shifted, b, n)
                wait(act, p_turned, b, n - HQ)
                act.activation(prob[j][:, 0:KV], ps_s[j % 2][:, :], ACT.Exp, bias=down[:, j:j + 1],
                               scale=q_scale[par][:, i, j:j + 1], accum_out=total[:, j:j + 1]).then_inc(exped.sem, 1)

            def copy_pT(b, i, j):
                wait(act, p_turned, b, i * HQ + j)
                if j == 0:
                    wait(act, pv, b, i - 2)
                act.activation(pT[i % 2][0:CT, :, j, :], ps_t[j % 2][0:CT, :, :], ACT.Copy).then_inc(pT_ready.sem, 1)

            def copy_o(b, i):
                wait(act, pv, b, i)
                wait(act, o_put[i % 2], b, i // 2 - 1)
                act.activation(ov[i % 2][:, :, :], ps_o[:, :, :], ACT.Copy).then_inc(o_ready.sem, 1)

            def next_high(b, i, par):
                if i in (0, 1):
                    high(b, i + 1, par)
                elif i == 3 and not (isinstance(b, int) and b == B - 1):
                    high(b + 1, 0, 1 - par)

            def project(b, i, par):
                square(b, i, 0, par)
                square(b, i, 1, par)
                keep_q(b, i)
                next_high(b, i, par)
                keep_v(b, i, par)
                keep_k(b, i, par)

            def step(b, i, par, more):
                nb, npar = b + 1, 1 - par
                exp(b, i, 0, par)
                exp(b, i, 1, par)
                if more:
                    square(nb, i, 0, npar)
                copy_pT(b, i, 0)
                copy_pT(b, i, 1)
                exp(b, i, 2, par)
                exp(b, i, 3, par)
                if more:
                    square(nb, i, 1, npar)
                copy_pT(b, i, 2)
                copy_pT(b, i, 3)
                if more:
                    keep_q(nb, i)
                    next_high(nb, i, npar)
                    keep_v(nb, i, npar)
                copy_o(b, i)
                if more:
                    keep_k(nb, i, npar)

            exped.open(act)
            o_ready.open(act)
            pT_ready.open(act)
            high(0, 0, 0)
            for n in range(NW):
                act.wait_ge(w_in[n % 2], 16 * (n // 2 + 1))
                act.activation(w_hi[:, W_ORDER[n], :, :], v[n % 2][:, :, :], ACT.Copy).then_inc(w_hi_ready, 1)
            act.wait_ge(w_lo_ready, NW)
            batches(act, project, step)

        @block.vector
        def _(dve):
            q_sum.open(dve)
            k_sum.open(dve)

            def rotate(b, i, unit, par):
                m = (S, M[i])[unit]
                ps = ps_p[(3 * i + unit) % 2][0:m, :]
                r1, r2 = ((q1, q2), (k1, k2))[unit]
                t = (4, i)[unit]
                turned, rot = ((q_turned, q_rot), (k_turned, k_rot))[unit]
                sq_done, summed, scaled = ((q_sq, q_sum, q_scaled), (k_sq, k_sum, k_scaled))[unit]
                wait(dve, sq_done, b, i)
                if i == 0:
                    inputs(dve, b, par)
                if not (isinstance(b, int) and b == 0 and i == 0):
                    wait(dve, turned, b, i - 1)
                h4 = lambda ap: ap.rearrange("p (h d) -> p h d", h=HQ)
                dve.tensor_tensor(h4(r1[0:m, :]), h4(ps), over_heads(tab[par][0:m, t, 0, :], HQ), ALU.mult)
                for half in range(2):
                    this, other = slice(half * HF, (half + 1) * HF), slice((1 - half) * HF, (2 - half) * HF)
                    ins = dve.tensor_tensor(h4(r2[0:m, :])[:, :, this], h4(ps)[:, :, other],
                                            over_heads(tab[par][0:m, t, 1, this], HQ), ALU.mult)
                ins.then_inc(rot.sem, 1)
                if not (isinstance(b, int) and b == 0 and i == 0):
                    wait(dve, scaled, b, i - 1)
                dve.tensor_reduce(ssum[0:m, unit, :], h4(sq[0:m, :]), AX.X, ALU.add).then_inc(summed.sem, 1)
                wait(dve, summed, b, 2 * i)
                if unit == 0:
                    f = 1.0 / X_SCALE ** 2
                    dve.tensor_scalar(ssum[0:m, unit, :], ssum[0:m, unit, :], f / HD, RMS_EPS * f,
                                      ALU.mult, ALU.add).then_inc(summed.sem, 1)
                else:
                    dve.tensor_scalar(ssum[0:m, unit, :], ssum[0:m, unit, :], 1.0 / HD, RMS_EPS,
                                      ALU.mult, ALU.add).then_inc(summed.sem, 1)

            def maximum(b, i, j, par):
                n = i * HQ + j
                if i == 0 and j == 0:
                    wait(dve, q_scaled, b, 3)
                wait(dve, scored, b, n)
                dve.tensor_reduce(top[:, j:j + 1], ps_s[j % 2][:, :], AX.X, ALU.max, negate=True).then_inc(maxed.sem, 1)
                wait(dve, maxed, b, n)
                dve.tensor_tensor(down[:, j:j + 1], top[:, j:j + 1], q_scale[par][:, i, j:j + 1], ALU.mult).then_inc(shifted.sem, 1)

            def divide(b, i, j):
                n = i * HQ + j
                wait(dve, exped, b, n)
                dve.reciprocal(inv[:, j:j + 1], total[:, j:j + 1]).then_inc(inverted.sem, 1)
                wait(dve, inverted, b, n)
                dve.tensor_scalar(prob[j][:, 0:KV], prob[j][:, 0:KV], inv[:, j:j + 1], None, ALU.mult).then_inc(probs.sem, 1)

            def project(b, i, par):
                rotate(b, i, 0, par)
                rotate(b, i, 1, par)

            def step(b, i, par, more):
                maximum(b, i, 0, par)
                maximum(b, i, 1, par)
                divide(b, i, 0)
                divide(b, i, 1)
                if more:
                    rotate(b + 1, i, 0, 1 - par)
                maximum(b, i, 2, par)
                maximum(b, i, 3, par)
                divide(b, i, 2)
                divide(b, i, 3)
                if more:
                    rotate(b + 1, i, 1, 1 - par)

            for n in range(NW):
                dve.wait_ge(w_hi_ready, n + 1)
                dve.tensor_tensor(w_lo[:, W_ORDER[n], :, :], v[n % 2][:, :, :], w_hi[:, W_ORDER[n], :, :], ALU.subtract)\
                    .then_inc(w_lo_ready, 1)
            batches(dve, project, step)


def experts(nc, weights, acc, oh, place, weight, run, rows_n, tokens, rows_y, out):
    KI = INTER // P
    NU = 2 * NS
    GW = KD * 2 * INTER
    WW = GW + KI * D
    ctx = Phase(nc, "ffn")
    with ctx:
        sb = ctx.sb
        ev = ctx.ev
        ident = sb("ident", [P, P])
        raw = sb("raw", [P, E, WW])
        w_hi = [sb(f"w_hi{i}", [P, WW], F32R) for i in range(2)]
        w_lo = [sb(f"w_lo{i}", [P, WW], F32R) for i in range(2)]
        gu_of = lambda w: w[:, 0:GW].rearrange("p (k i) -> p k i", k=KD)
        down_of = lambda w: w[:, GW:WW].rearrange("p (k o) -> p k o", k=KI)
        xg = [sb(f"xg{i}", [P, D]) for i in range(4)]
        xh = [sb(f"xh{i}", [P, KD, P], F32R) for i in range(2)]
        xl = [sb(f"xl{i}", [P, KD, P], F32R) for i in range(2)]
        den = [sb(f"den{i}", [P, INTER]) for i in range(2)]
        a = [sb(f"a{i}", [P, INTER]) for i in range(2)]
        aT_hi = [sb(f"aT_hi{i}", [P, KI, P], F32R) for i in range(2)]
        aT_lo = [sb(f"aT_lo{i}", [P, KI, P], F32R) for i in range(2)]
        yt = [sb(f"yt{i}", [P, D]) for i in range(2)]
        slot_i = sb("slot_i", [P, NS + 1], I32)
        slot = sb("slot", [P, NS + 1])
        tiles = sb("tiles", [P, E])
        begin = sb("begin", [P, E])
        behind = sb("behind", [P, E, NS + 1])
        past = sb("past", [P, E, NS + 1])
        who = sb("who", [P, NS + 1])
        skip = sb("skip", [P, NS + 1])
        where = sb("where", [P, NS + 1])
        who_i = sb("who_i", [P, NS + 1], I32)
        where_i = sb("where_i", [P, NS + 1], I32)
        list_i = sb("list_i", [P, NS, 2], I32)
        row_i = [sb(f"row_i{i}", [P, 2], U32) for i in range(2)]
        fetch = sb("fetch", [P, TT, 2, E])
        fetch_f = sb("fetch_f", [P, TT, 2])
        fetch_i = sb("fetch_i", [P, TT, 2], U32)
        share = sb("share", [P, TT, 2])
        ps_x = [ctx.bank(f"ps_x{i}", P, KD, P) for i in range(2)]
        ps_g = [ctx.bank(f"ps_g{i}", P, 2 * INTER) for i in range(2)]
        ps_a = [ctx.bank(f"ps_a{i}", P, KI, P) for i in range(2)]
        ps_y = [ctx.bank(f"ps_y{i}", P, D) for i in range(2)]
        id_ready = ctx.sem("id_ready")
        planned = ctx.sem("slots_planned")
        plan_step = ctx.sem("plan_step")
        w_in = ctx.sem("weights_loaded")
        list_in = ctx.sem("lists_loaded")
        ticks = ctx.sem("ticks")
        row_ready = ev("row_indices", 1)
        x_in = [ev(f"x_gathered{i}", 1, step=16) for i in range(4)]
        x_turned = ev("x_turned", 1, 4)
        x_hi, x_lo = ev("x_hi", 1), ev("x_lo", 1)
        g_hi, d_hi = ev("w_gate_up_hi", 1), ev("w_down_hi", 1)
        g_lo, d_lo = ev("w_gate_up_lo", 1), ev("w_down_lo", 1)
        gu = ev("gate_up", 1, 4)
        expd = ev("exped", 1)
        plus1 = ev("plus_one", 1)
        inverse = ev("inverse", 1)
        silu = ev("silu", 1)
        gated = ev("gated", 1, 2)
        turned = ev("a_turned", 1, 2)
        a_hi, a_lo = ev("aT_hi", 1), ev("aT_lo", 1, 2)
        down_mm = ev("down", 1, 4)
        y_out = ev("y_copied", 1, 2)
        y_put = [ev(f"y_stored{i}", 1, 1, 16) for i in range(2)]
        fetched = [ctx.sem(f"y_fetched{i}") for i in range(4)]
        summed = ctx.sem("summed")
        stored = ctx.sem("stored")
        block = ctx.enter_context(nc.Block())

        LOOPS = (NU - 4) // 4

        def run_units(eng, step):
            step(0, 0)
            step(0, 1)
            with eng.Fori(0, LOOPS) as h:
                for i in range(2, 6):
                    step(h, i)
            for i in range(4 * LOOPS + 2, NU + 2):
                step(0, i)

        def has(h, i):
            return not isinstance(h, int) or 0 <= i < NU

        @block.sync
        def _(sp):
            for i in range(2):
                y_put[i].open(sp)
            sp.dma_start(raw[:, 0, :], weights[0]).then_inc(w_in, 16)
            sp.wait_ge(planned, 1)
            with sp.Fori(0, NS) as s:
                place0 = sp.value_load(where_i[0:1, bass.ds(s, 1)], min_val=0, max_val=DUMP - ST)
                sp.dma_start(list_i[:, bass.ds(s, 1), :].rearrange("p o h -> p (o h)"),
                             tokens[bass.ds(place0, ST), :].rearrange("(p h) o -> p (h o)", h=2)).then_inc(list_in, 16)
            for e in range(1, E):
                sp.wait_ge(w_in, 16 * e)
                sp.dma_start(raw[:, e, :], weights[e]).then_inc(w_in, 16)

            def store(h, i):
                n = h * 4 + i
                wait(sp, y_out, n)
                half = i % 2
                rows = rows_y[bass.ds((h * 2 + i // 2) * ST, ST), :].rearrange("(p h) d -> h p d", h=2)[half]
                sp.dma_start(rows, yt[half][:, :]).then_inc(y_put[half].sem, 16)

            with sp.Fori(0, NU // 4) as h:
                for i in range(4):
                    store(h, i)
            for i in range(NU // 4 * 4, NU):
                store(0, i)
            for t in range(TT):
                sp.wait_ge(summed, 2 * t + 2)
                sp.dma_start(out[t * P:(t + 1) * P, :], acc[:, t, :]).then_inc(stored, 16)
            sp.wait_ge(stored, 16 * TT)

        @block.gpsimd
        def _(pool):
            pool.iota(slot_i[:, :], pattern=[[1, NS + 1]], base=0, channel_multiplier=0).then_inc(id_ready, 1)
            identity(pool, ident[:, :], id_ready, 1)
            pool.wait_ge(planned, 1)
            pool.wait_ge(list_in, 16 * NS)

            def prepare(h, i):
                s = h * 2 + i
                b = i % 2
                e = pool.value_load(who_i[0:1, bass.ds(s, 1)], min_val=0, max_val=E - 1)
                wait(pool, x_turned, h * 4 + 2 * i, -3)
                carry(pool, h, ticks)
                pool.tensor_copy(row_i[b][:, :], list_i[:, bass.ds(s, 1), :].rearrange("p o h -> p (o h)"))\
                    .then_inc(row_ready.sem, 1)
                wait(pool, row_ready, s)
                carry(pool, h, ticks)
                for half in range(2):
                    pool.indirect_dma_start(xg[2 * b + half][:, :], None, rows_n,
                                            bass.IndirectOffsetOnAxis(ap=row_i[b][:, half:half + 1], axis=0))\
                        .then_inc(x_in[2 * b + half].sem, 16)
                wait(pool, g_hi, s)
                carry(pool, h, ticks)
                pool.tensor_tensor(w_lo[b][:, 0:GW], raw[:, bass.ds(e, 1), 0:GW].rearrange("p o w -> p (o w)"),
                                   w_hi[b][:, 0:GW], ALU.subtract).then_inc(g_lo.sem, 1)

            with pool.Fori(0, NS // 2) as h:
                prepare(h, 0)
                prepare(h, 1)
            for s in range(NS // 2 * 2, NS):
                prepare(0, s)
            for i in range(2):
                pool.wait_ge(y_put[i].sem, y_put[i].at(NU // 2 - 1))
            for t in range(TT):
                for c in range(2):
                    b = 2 * (t % 2) + c
                    if t >= 2:
                        pool.wait_ge(summed, 2 * (t - 2) + c + 1)
                    pool.indirect_dma_start(xg[b][:, :], None, rows_y,
                                            bass.IndirectOffsetOnAxis(ap=fetch_i[:, t, c:c + 1], axis=0))\
                        .then_inc(fetched[b], 16)

        @block.tensor
        def _(pe):
            pe.wait_ge(id_ready, 3)
            x_turned.open(pe)
            gu.open(pe)
            turned.open(pe)
            down_mm.open(pe)

            def turn_x(h, i):
                n = h * 4 + i
                pe.wait_ge(x_in[i % 4].sem, (h + i // 4) * 16 + 16)
                if not (isinstance(h, int) and i < 2):
                    wait(pe, x_lo, n, -2)
                for k in range(KD):
                    mm = pe.transpose(ps_x[i % 2][:, k, :], xg[i % 4][:, k * P:(k + 1) * P], ident[:, :])
                mm.then_inc(x_turned.sem, 1)

            def project(h, i):
                n, s, b = h * 4 + i, h * 2 + i // 2, i // 2 % 2
                if i % 2 == 0:
                    wait(pe, g_lo, s)
                wait(pe, x_lo, n)
                wait(pe, gated, n, -2)
                for k in range(KD):
                    mm = mm3(pe, ps_g[i % 2][:, :], xh[i % 2][:, k, :], xl[i % 2][:, k, :], gu_of(w_hi[b])[:, k, :],
                             gu_of(w_lo[b])[:, k, :], k == 0, k == KD - 1)
                mm.then_inc(gu.sem, 1)

            def turn(h, i):
                n = h * 4 + i
                wait(pe, gated, n)
                wait(pe, a_lo, n, -2)
                for k in range(KI):
                    mm = pe.transpose(ps_a[i % 2][:, k, :], a[i % 2][:, k * P:(k + 1) * P], ident[:, :])
                mm.then_inc(turned.sem, 1)

            def project_down(h, i):
                n, s, b = h * 4 + i, h * 2 + i // 2, i // 2 % 2
                if i % 2 == 0:
                    wait(pe, d_lo, s)
                wait(pe, a_lo, n)
                wait(pe, y_out, n, -2)
                for k in range(KI):
                    mm = mm3(pe, ps_y[i % 2][:, :], aT_hi[i % 2][:, k, :], aT_lo[i % 2][:, k, :],
                             down_of(w_hi[b])[:, k, :], down_of(w_lo[b])[:, k, :], k == 0, k == KI - 1)
                mm.then_inc(down_mm.sem, 1)

            def step(h, i):
                if has(h, i + 1):
                    turn_x(h, i + 1)
                if has(h, i):
                    project(h, i)
                if has(h, i - 1):
                    turn(h, i - 1)
                if has(h, i - 2):
                    project_down(h, i - 2)

            turn_x(0, 0)
            run_units(pe, step)

        @block.scalar
        def _(act):
            y_out.open(act)

            def split(h, i, part):
                s, b = h * 2 + i, i % 2
                e = act.value_load(who_i[0:1, bass.ds(s, 1)], min_val=0, max_val=E - 1)
                act.wait_ge(w_in, e * 16 + 16)
                wait(act, (gu, down_mm)[part], h * 4 + 2 * i, -3)
                act.sem_inc(ticks, 1)
                cols = (slice(0, GW), slice(GW, WW))[part]
                act.activation(w_hi[b][:, cols], raw[:, bass.ds(e, 1), cols].rearrange("p o w -> p (o w)"), ACT.Copy)\
                    .then_inc((g_hi, d_hi)[part].sem, 1)

            def turn_x(h, i):
                n = h * 4 + i
                wait(act, x_turned, n)
                wait(act, gu, n, -2)
                act.activation(xh[i % 2][:, :, :], ps_x[i % 2][:, :, :], ACT.Copy).then_inc(x_hi.sem, 1)

            def exp(h, i):
                n = h * 4 + i
                wait(act, gu, n)
                wait(act, turned, n, -2)
                act.activation(den[i % 2][:, :], ps_g[i % 2][:, 0:INTER], ACT.Exp, scale=-1.0).then_inc(expd.sem, 1)
                wait(act, expd, n)
                act.activation(den[i % 2][:, :], den[i % 2][:, :], ACT.Copy, bias=1.0).then_inc(plus1.sem, 1)

            def high(h, i):
                n = h * 4 + i
                wait(act, turned, n)
                wait(act, down_mm, n, -2)
                act.activation(aT_hi[i % 2][:, :, :], ps_a[i % 2][:, :, :], ACT.Copy).then_inc(a_hi.sem, 1)

            def copy_y(h, i):
                n = h * 4 + i
                wait(act, down_mm, n)
                act.wait_ge(y_put[i % 2].sem, (h * 2 + i // 2) * 16 + 16)
                act.activation(yt[i % 2][:, :], ps_y[i % 2][:, :], ACT.Copy).then_inc(y_out.sem, 1)

            def step(h, i):
                if has(h, i + 1):
                    turn_x(h, i + 1)
                if has(h, i):
                    exp(h, i)
                if has(h, i - 1):
                    high(h, i - 1)
                if has(h, i - 2):
                    copy_y(h, i - 2)
                if i % 2 == 1 and has(h, i + 3):
                    split(h, (i + 3) // 2, 0)
                if i % 2 == 0 and has(h, i):
                    split(h, i // 2, 1)

            act.wait_ge(planned, 1)
            split(0, 0, 0)
            turn_x(0, 0)
            split(0, 1, 0)
            run_units(act, step)

        @block.vector
        def _(dve):
            gated.open(dve)
            a_lo.open(dve)
            count = [0]

            def then(ins):
                count[0] += 1
                ins.then_inc(plan_step, 1)
                dve.wait_ge(plan_step, count[0])

            ROUND = RopeTables.ROUND
            dve.wait_ge(id_ready, 1)
            dve.tensor_copy(slot[:, :], slot_i[:, :])
            dve.tensor_scalar(tiles[:, :], run[:, :], 1.0 / ST, (ST - 1) / (2.0 * ST), ALU.mult, ALU.add)
            then(dve.memset(begin[:, :], 0.0))
            then(dve.tensor_scalar(tiles[:, :], tiles[:, :], ROUND, ROUND, ALU.add, ALU.subtract))
            for e in range(1, E):
                then(dve.tensor_tensor(begin[:, e:e + 1], begin[:, e - 1:e], tiles[:, e - 1:e], ALU.add))
            then(dve.tensor_tensor(behind[:, :, :], over_heads(slot[:, :], E), along(begin[:, :], NS + 1), ALU.is_ge))
            dve.tensor_tensor(past[:, 1:E, :], behind[:, 1:E, :], along(tiles[:, 0:E - 1], NS + 1), ALU.mult)
            then(dve.tensor_reduce(who[:, :], behind[:, 1:E, :].rearrange("p e s -> p s e"), AX.X, ALU.add))
            then(dve.tensor_reduce(skip[:, :], past[:, 1:E, :].rearrange("p e s -> p s e"), AX.X, ALU.add))
            then(dve.tensor_tensor(skip[:, :], slot[:, :], skip[:, :], ALU.subtract))
            then(dve.tensor_scalar(where[:, :], who[:, :], float(REGION), None, ALU.mult))
            then(dve.scalar_tensor_tensor(where[:, :], skip[:, :], float(ST), where[:, :], ALU.mult, ALU.add))
            dve.tensor_copy(who_i[:, :], who[:, :])
            dve.tensor_copy(where_i[:, :], where[:, :]).then_inc(planned, 1)

            def low_d(h, i):
                s, b = h * 2 + i, i % 2
                e = dve.value_load(who_i[0:1, bass.ds(s, 1)], min_val=0, max_val=E - 1)
                wait(dve, d_hi, s)
                dve.tensor_tensor(w_lo[b][:, GW:WW], raw[:, bass.ds(e, 1), GW:WW].rearrange("p o w -> p (o w)"),
                                  w_hi[b][:, GW:WW], ALU.subtract).then_inc(d_lo.sem, 1)

            def turn_x(h, i):
                wait(dve, x_hi, h * 4 + i)
                dve.tensor_tensor(xl[i % 2][:, :, :], ps_x[i % 2][:, :, :], xh[i % 2][:, :, :], ALU.subtract).then_inc(x_lo.sem, 1)

            def gate(h, i):
                n = h * 4 + i
                d, g = den[i % 2], ps_g[i % 2]
                wait(dve, plus1, n)
                dve.reciprocal(d[:, :], d[:, :]).then_inc(inverse.sem, 1)
                wait(dve, inverse, n)
                dve.tensor_tensor(d[:, :], g[:, 0:INTER], d[:, :], ALU.mult).then_inc(silu.sem, 1)
                wait(dve, silu, n)
                wait(dve, turned, n, -2)
                dve.tensor_tensor(a[i % 2][:, :], g[:, INTER:2 * INTER], d[:, :], ALU.mult).then_inc(gated.sem, 1)

            def low(h, i):
                wait(dve, a_hi, h * 4 + i)
                dve.tensor_tensor(aT_lo[i % 2][:, :, :], ps_a[i % 2][:, :, :], aT_hi[i % 2][:, :, :], ALU.subtract)\
                    .then_inc(a_lo.sem, 1)

            def step(h, i):
                if has(h, i + 1):
                    turn_x(h, i + 1)
                if has(h, i):
                    gate(h, i)
                if has(h, i - 1):
                    low(h, i - 1)
                if i % 2 == 0 and has(h, i):
                    low_d(h, i // 2)

            turn_x(0, 0)
            chosen = oh[:, :, :].rearrange("p t (c e) -> p t c e", c=2)
            one_hot = lambda n: chosen[:, :, :, 0:n]
            both = lambda ap: ap.unsqueeze(2).broadcast_to((P, TT, 2, ap.shape[2]))
            then(dve.scalar_tensor_tensor(place[:, :, :], begin[:, :].unsqueeze(1).broadcast_to((P, TT, E)), float(ST),
                                          place[:, :, :], ALU.mult, ALU.add))
            then(dve.tensor_tensor(fetch[:, :, :, :], one_hot(E), both(place[:, :, :]), ALU.mult))
            then(dve.tensor_reduce(fetch_f[:, :, :], fetch[:, :, :, :], AX.X, ALU.add))
            then(dve.tensor_copy(fetch_i[:, :, :], fetch_f[:, :, :]))
            then(dve.tensor_tensor(fetch[:, :, :, :], one_hot(E), both(weight[:, :, 0:E]), ALU.mult))
            then(dve.tensor_reduce(share[:, :, :], fetch[:, :, :, :], AX.X, ALU.add))
            run_units(dve, step)
            for t in range(TT):
                for c in range(2):
                    dve.wait_ge(fetched[2 * (t % 2) + c], 16 * (t // 2 + 1))
                    if c:
                        dve.wait_ge(summed, 2 * t + 1)
                    dve.scalar_tensor_tensor(acc[:, t, :], xg[2 * (t % 2) + c][:, :], share[:, t, c:c + 1],
                                             acc[:, t, :], ALU.mult, ALU.add).then_inc(summed, 1)


def build(nc, x, ctxT, pos_ctx, pos_x, inv_freq, q_proj, wq_rotT, wkvaT, kv_ln, kv_b, woT, xwqT, xwkT, xwvT,
          xwoT, q_norm, k_norm, clsT, bias, expert_w, out):
    dram = lambda name, shape: nc.dram_tensor(name, shape, F32).ap()
    tables = dram("rope_tables", (B, P, 5, 2, HD))
    vo = dram("value_output_weights", (P, H, D))
    x0T = dram("x0T_hi", (P, KD, T)), dram("x0T_lo", (P, KD, T))
    x1T = dram("x1T_hi", (P, KD, T)), dram("x1T_lo", (P, KD, T))
    o1T, o2T = dram("self_outT", (P, H, T)), dram("cross_outT", (P, H, T))
    x1 = dram("x1", (T, D))
    rows_n, rows_y = dram("x2_normed", (T, D)), dram("expert_rows", (NS * ST, D))
    tokens = nc.dram_tensor("tokens_of_experts", (DUMP + P, 1), I32).ap()
    x_rows = x.rearrange("b s d -> (b s) d")
    out_rows = out.rearrange("b s d -> (b s) d")
    kv_heads = kv_b.rearrange("(h c d) r -> c d h r", h=H, c=2)

    with ExitStack() as ctx:
        sb = lambda name, shape, dt=F32: ctx.enter_context(nc.sbuf_tensor(name, shape, dt))
        qf = sb("qf_hi", [P, KD, H, RANK], F32R), sb("qf_lo", [P, KD, H, RANK], F32R)
        qr = sb("qr_hi", [P, KD, H * ROPE], F32R), sb("qr_lo", [P, KD, H * ROPE], F32R)
        lat_kT = sb("lat_kT", [P, 3, T])
        lat_v = sb("lat_v", [S, B, RANK])
        with ExitStack() as early:
            esb = lambda name, shape, dt: early.enter_context(nc.sbuf_tensor(name, shape, dt))
            kva = esb("kva_hi", [P, KD, RANK + ROPE], F32R), esb("kva_lo", [P, KD, RANK + ROPE], F32R)
            fold_weights(nc, q_proj, kv_heads[0], kv_heads[1], woT, wq_rotT, wkvaT, *qf, *qr, *kva,
                         lat_kT[:, :, :].rearrange("p c t -> p (c t)"), vo)
            latents(nc, x, kv_ln, *kva, lat_kT, lat_v, *x0T)
        self_attention(nc, *x0T, *qf, *qr, lat_kT, lat_v, o1T)
    project_out(nc, o1T, vo, x_rows, x1, x1T, rope=(pos_ctx, pos_x, inv_freq, k_norm, q_norm, tables))
    cross_attention(nc, ctxT, *x1T, xwqT, xwkT, xwvT, tables, o2T)
    with ExitStack() as ctx:
        sb = lambda name, shape, dt=F32: ctx.enter_context(nc.sbuf_tensor(name, shape, dt))
        acc = sb("acc", [P, TT, D])
        oh = sb("choices_one_hot", [P, TT, 2 * TOTAL])
        place = sb("choice_place", [P, TT, E])
        weight = sb("choice_weight", [P, TT, TOTAL])
        run = sb("tokens_of_expert", [P, E])
        keep = acc, oh, place, weight, run, rows_n, tokens
        project_out(nc, o2T, xwoT, x1, None, None, router=(clsT, bias), keep=keep)
        experts(nc, expert_w, *keep, rows_y, out_rows)


def layouts(x, ctx_2048, pos_BxS2, itok_BxS_4096_4607, L0_attn_q_proj_w, L0_attn_kv_a_proj_w, L0_attn_kv_a_ln_w,
            L0_attn_kv_b_proj_w, L0_attn_o_proj_w, L0_xattn_Wq, L0_xattn_Wk, L0_xattn_Wv, L0_xattn_Wo,
            L0_xattn_q_norm_w, L0_xattn_k_norm_w, L0_ffn_classifier_w, L0_ffn_e_score_correction_bias,
            L0_ffn_gate_w, L0_ffn_up_w, L0_ffn_down_w):
    kT = lambda w: w.T.reshape(KD, P, -1).transpose(1, 0, 2)
    rows = lambda w, n: np.broadcast_to(w, (n, w.shape[0]))
    heads = lambda w: w.reshape(D, H, P).transpose(2, 1, 0)
    rot = L0_attn_q_proj_w.reshape(H, NOPE + ROPE, D)[:, NOPE:].reshape(H * ROPE, D)
    gu = np.concatenate([L0_ffn_gate_w, L0_ffn_up_w], axis=1)
    per_k = lambda w: w.transpose(0, 2, 1).reshape(E, -1, P, w.shape[1]).transpose(0, 2, 1, 3).reshape(E, P, -1)
    freq = 1.0 / np.float32(10000.0) ** (np.arange(0, HD, 2, dtype=np.float32) / np.float32(HD))
    return {
        "x": x,
        "ctxT": ctx_2048.reshape(B, C, KD, P).transpose(0, 3, 2, 1),
        "pos_ctx": pos_BxS2.reshape(B, 3, CT).transpose(2, 1, 0),
        "pos_x": itok_BxS_4096_4607.T,
        "inv_freq": rows(freq.astype(np.float32), P),
        "q_proj": L0_attn_q_proj_w,
        "wq_rotT": kT(rot),
        "wkvaT": kT(L0_attn_kv_a_proj_w),
        "kv_ln": rows(L0_attn_kv_a_ln_w, S),
        "kv_b": L0_attn_kv_b_proj_w,
        "woT": heads(L0_attn_o_proj_w),
        "xwqT": kT(L0_xattn_Wq),
        "xwkT": kT(L0_xattn_Wk),
        "xwvT": kT(L0_xattn_Wv),
        "xwoT": heads(L0_xattn_Wo),
        "q_norm": rows(L0_xattn_q_norm_w, P),
        "k_norm": rows(L0_xattn_k_norm_w, P),
        "clsT": kT(L0_ffn_classifier_w),
        "bias": rows(L0_ffn_e_score_correction_bias, P),
        "expert_w": np.concatenate([per_k(gu), per_k(L0_ffn_down_w)], axis=2),
    }


def kernel(**inputs):
    import concourse.bacc as bacc
    from concourse.bass_utils import run_bass_kernel_spmd

    nc = bacc.Bacc("TRN2", target_bir_lowering=False, num_devices=1)
    arrays, args = {}, {}
    for name, a in layouts(**{k: np.asarray(v) for k, v in inputs.items()}).items():
        a = np.ascontiguousarray(a)
        arrays[f"in_{name}"] = a
        args[name] = nc.dram_tensor(f"in_{name}", a.shape, mybir.dt.from_np(a.dtype), kind="ExternalInput").ap()
    out = nc.dram_tensor("out", (B, S, D), F32, kind="ExternalOutput").ap()
    build(nc, **args, out=out)
    r = run_bass_kernel_spmd(nc, [arrays], core_ids=[0])
    return r.results[0]["out"]
```

```python
from contextlib import ExitStack

import numpy as np

import concourse.bass as bass
from concourse import mybir

F32 = mybir.dt.float32
F32R = mybir.dt.float32r
I32 = mybir.dt.int32
U32 = mybir.dt.uint32
ALU = mybir.AluOpType
ACT = mybir.ActivationFunctionType
AX = mybir.AxisListType

B, S, D = 16, 112, 512
T = B * S
C = 375
KV = C + S
P = 128
KD = D // P
H = 16
HQ = 4
NQ = H // HQ
NOPE, ROPE, RANK = 128, 64, 128
HD, KVH = 128, 4
CT = C // 3
E, TOTAL, INTER = 8, 12, 256
TT = T // P
G = 4
GT = G * S
ST = 2 * P
NS = (2 * T - E) // ST + E
REGION = 2048
DUMP = (E - 1) * REGION + NS * ST
LN_EPS, RMS_EPS = 1e-5, 1e-6
MLA_SCALE = float((NOPE + ROPE) ** -0.5)
X_SCALE = float(HD ** -0.5)
ROUTE_SCALE = 1.5
MASKED = -3.0e9
PI2 = (6.28125, float(2 * np.pi) - 6.28125)


class Event:

    def __init__(self, sem, per, ahead, step):
        self.sem = sem
        self.per, self.ahead, self.step = per, ahead, step

    def at(self, item, n=0):
        return (item * self.per + (n + 1 + self.ahead)) * self.step

    def open(self, eng):
        eng.sem_inc(self.sem, self.ahead * self.step)


def wait(eng, event, item, n=0):
    eng.wait_ge(event.sem, event.at(item, n))


def carry(eng, item, ticks):
    if not isinstance(item, int):
        eng.sem_inc(ticks, 1)


def mm3(pe, out, a_hi, a_lo, b_hi, b_lo, start, stop):
    pe.matmul(out, a_hi, b_hi, start=start, stop=False)
    pe.matmul(out, a_hi, b_lo, start=False, stop=False)
    return pe.matmul(out, a_lo, b_hi, start=False, stop=stop)


def over_heads(ap, n):
    return ap.unsqueeze(1).broadcast_to((ap.shape[0], n, ap.shape[1]))


def along(ap, n):
    return ap.unsqueeze(2).broadcast_to((ap.shape[0], ap.shape[1], n))


class Phase(ExitStack):

    def __init__(self, nc, name):
        super().__init__()
        self.nc, self.name, self.sems = nc, name, []

    def sb(self, name, shape, dt=F32):
        return self.enter_context(self.nc.sbuf_tensor(f"{self.name}_{name}", shape, dt))

    def sem(self, name):
        self.sems.append(self.nc.alloc_semaphore(name=f"{self.name}_{name}"))
        return self.sems[-1]


    def ev(self, name, per, ahead=0, step=1):
        return Event(self.sem(name), per, ahead, step)

    def bank(self, name, *shape):
        flat = self.enter_context(self.nc.psum_tensor(f"{self.name}_{name}", [P, 512], F32))
        if len(shape) == 2:
            return flat[0:shape[0], 0:shape[1]]
        return flat[0:shape[0], 0:shape[1] * shape[2]].rearrange("p (a b) -> p a b", a=shape[1])


def clear(nc, *phases):
    nc.clear_and_free_semaphores([sem for phase in phases for sem in phase.sems])
    nc.all_engine_barrier()


def identity(pool, tile, sem, before=0):
    pool.memset(tile, 0.0).then_inc(sem, 1)
    pool.wait_ge(sem, before + 1)
    pool.affine_select(out=tile, in_=tile, compare_op=ALU.not_equal, fill=1.0, base=0,
                       pattern=[[-1, tile.shape[1]]], channel_multiplier=1).then_inc(sem, 1)


def fold_weights(nc, wq_nope, wkb, wvb, woT, wq_rotT, wkvaT, qf_hi, qf_lo, qr_hi, qr_lo, kva_hi, kva_lo, scratch, vo):
    ctx = Phase(nc, "fold")
    with ctx:
        sb = ctx.sb
        sem = ctx.sem
        wq = sb("wq_nat", [P, 2, HQ, D])
        kb = sb("kb_nat", [P, H, RANK])
        vb = sb("vb_nat", [P, H, RANK])
        wo = sb("wo_nat", [P, 2, HQ, D])
        rot = scratch[:, 0:KD * H * ROPE].rearrange("p (k n) -> p k n", k=KD)
        kva = sb("kva_raw", [P, KD, RANK + ROPE])
        vos = sb("vos", [P, 2, HQ, D])
        psq = [ctx.bank(f"psq{i}", P, 512) for i in range(4)]
        psv = [ctx.bank(f"psv{i}", P, 512) for i in range(4)]
        kb_in = [sem(f"kb_loaded{c}") for c in range(NQ)]
        wq_in = [sem("wq_loaded0"), sem("wq_loaded1")]
        wo_in = [sem("wo_loaded0"), sem("wo_loaded1")]
        kva_in, rot_in, vb_in = sem("kva_loaded"), sem("rot_loaded"), sem("vb_loaded")
        stored = [sem("vo_stored0"), sem("vo_stored1")]
        q_mm, v_mm, q_hi, q_lo, v_out, plain_hi, plain_lo = (sem(n) for n in (
            "q_products", "v_products", "q_hi", "q_lo", "v_copied", "plain_hi", "plain_lo"))
        block = ctx.enter_context(nc.Block())
        nope = wq_nope.rearrange("(h d) i -> d h i", h=H)

        @block.sync
        def _(sp):
            for c in range(NQ):
                heads = slice(c * HQ, (c + 1) * HQ)
                sp.dma_start(kb[:, heads, :], wkb[:, heads, :]).then_inc(kb_in[c], 16)
                if c >= 2:
                    sp.wait_ge(q_mm, KD * (c - 1))
                sp.dma_start(wq[:, c % 2], nope[0:NOPE, c * HQ:(c + 1) * HQ, :]).then_inc(wq_in[c % 2], 16)
            for c in range(NQ):
                sp.wait_ge(v_out, HQ * (c + 1))
                sp.dma_start(vo[:, c * HQ:(c + 1) * HQ, :], vos[:, c % 2]).then_inc(stored[c % 2], 16)
            for i in range(2):
                sp.wait_ge(stored[i], 16 * NQ // 2)

        @block.gpsimd
        def _(pool):
            pool.wait_ge(plain_hi, 1)
            pool.tensor_tensor(kva_lo[:, :, :], kva[:, :, :], kva_hi[:, :, :], ALU.subtract).then_inc(plain_lo, 1)
            pool.wait_ge(plain_hi, 2)
            pool.tensor_tensor(qr_lo[:, :, :], rot[:, :, :], qr_hi[:, :, :], ALU.subtract).then_inc(plain_lo, 1)

        @block.tensor
        def _(pe):
            for c in range(NQ):
                pe.wait_ge(kb_in[c], 16)
                pe.wait_ge(wq_in[c % 2], 16 * (c // 2 + 1))
                for k in range(KD):
                    n = c * KD + k
                    if n >= 4:
                        pe.wait_ge(q_lo, n - 3)
                    for j in range(HQ):
                        mm = pe.matmul(psq[n % 4][:, j * RANK:(j + 1) * RANK], wq[:, c % 2, j, k * P:(k + 1) * P],
                                       kb[:, c * HQ + j, :], start=True, stop=True)
                    mm.then_inc(q_mm, 1)
            pe.wait_ge(vb_in, 16)
            for c in range(NQ):
                pe.wait_ge(wo_in[c % 2], 16 * (c // 2 + 1))
                for j in range(HQ):
                    n = c * HQ + j
                    if n >= 4:
                        pe.wait_ge(v_out, n - 3)
                    pe.matmul(psv[n % 4][:, :], vb[:, n, :], wo[:, c % 2, j, :], start=True, stop=True).then_inc(v_mm, 1)

        @block.scalar
        def _(act):
            act.dma_start(kva[:, :, :], wkvaT).then_inc(kva_in, 16)
            for n in range(NQ * KD):
                c, k = n // KD, n % KD
                act.wait_ge(q_mm, n + 1)
                act.activation(qf_hi[:, k, c * HQ:(c + 1) * HQ, :], psq[n % 4][:, :], ACT.Copy).then_inc(q_hi, 1)
                if n == 0:
                    act.dma_start(vb[:, :, :], wvb).then_inc(vb_in, 16)
                if n in (KD, 2 * KD):
                    half = n // KD - 1
                    act.dma_start(wo[:, half], woT[:, half * HQ:(half + 1) * HQ, :]).then_inc(wo_in[half], 16)
                if n == 2 * KD:
                    act.dma_start(rot[:, :, :], wq_rotT).then_inc(rot_in, 16)
            act.wait_ge(kva_in, 16)
            act.activation(kva_hi[:, :, :], kva[:, :, :], ACT.Copy).then_inc(plain_hi, 1)
            for c in range(2, NQ):
                act.wait_ge(v_mm, HQ * (c - 1))
                act.dma_start(wo[:, c % 2], woT[:, c * HQ:(c + 1) * HQ, :]).then_inc(wo_in[c % 2], 16)
                if c == 2:
                    act.wait_ge(rot_in, 16)
                    act.activation(qr_hi[:, :, :], rot[:, :, :], ACT.Copy).then_inc(plain_hi, 1)

        @block.vector
        def _(dve):
            for n in range(NQ * KD):
                c, k = n // KD, n % KD
                dve.wait_ge(q_hi, n + 1)
                dve.tensor_tensor(qf_lo[:, k, c * HQ:(c + 1) * HQ, :], psq[n % 4][:, :].rearrange("p (j r) -> p j r", j=HQ),
                                  qf_hi[:, k, c * HQ:(c + 1) * HQ, :], ALU.subtract).then_inc(q_lo, 1)
            for n in range(H):
                c = n // HQ
                if c >= 2 and n % HQ == 0:
                    dve.wait_ge(stored[c % 2], 16 * (c // 2))
                dve.wait_ge(v_mm, n + 1)
                dve.tensor_copy(vos[:, c % 2, n % HQ, :], psv[n % 4][:, :]).then_inc(v_out, 1)
    return ctx


class LayerNorm:

    def __init__(self, ctx, rows):
        self.stats, self.mv = ctx.sb("stats", [rows, 6]), ctx.sb("mean_var", [rows, 2])
        self.counted, self.varied = ctx.ev("ln_stats", 1), ctx.ev("ln_var", 1)
        self.ticks = ctx.sem("ln_ticks")
        self.shifted, self.rooted = ctx.ev("ln_var_eps", 1), ctx.ev("ln_rstd", 1)

    def vector(self, dve, item, dst, src):
        self.statistics(dve, item, src)
        return self.scale(dve, item, dst, src)

    def statistics(self, dve, item, src):
        dve.bn_stats(self.stats[:, :], src).then_inc(self.counted.sem, 1)
        wait(dve, self.counted, item)
        carry(dve, item, self.ticks)
        dve.bn_aggr(self.mv[:, :], self.stats[:, :]).then_inc(self.varied.sem, 1)

    def scale(self, dve, item, dst, src):
        wait(dve, self.rooted, item)
        return dve.tensor_scalar(dst, src, self.mv[:, 0:1], self.mv[:, 1:2], ALU.subtract, ALU.mult)

    def root(self, pool, item, minus_half):
        var = self.mv[:, 1:2]
        wait(pool, self.varied, item)
        carry(pool, item, self.ticks)
        pool.tensor_scalar(var, var, LN_EPS, None, ALU.add).then_inc(self.shifted.sem, 1)
        wait(pool, self.shifted, item)
        pool.tensor_tensor(var, var, minus_half[0:var.shape[0], 0:1], ALU.pow).then_inc(self.rooted.sem, 1)


def exponent(pool, tile, sem):
    pool.memset(tile, -0.5).then_inc(sem, 1)
    pool.wait_ge(sem, 1)


def latents(nc, x, lnw, kva_hi, kva_lo, lat_kT, lat_v, xT_hi, xT_lo):
    W = RANK + ROPE
    ctx = Phase(nc, "lat")
    with ctx:
        sb = ctx.sb
        ev = ctx.ev
        ident = sb("ident", [S, S])
        w_ln = sb("w_ln", [S, RANK])
        xs = [sb(f"xs{i}", [S, D]) for i in range(2)]
        xn = [sb(f"xn{i}", [S, D]) for i in range(2)]
        norm = LayerNorm(ctx, S)
        minus_half = sb("minus_half", [S, 1])
        half_ready = ctx.sem("minus_half_ready")
        xh = [sb(f"xh{i}", [P, KD, S], F32R) for i in range(2)]
        xl = [sb(f"xl{i}", [P, KD, S], F32R) for i in range(2)]
        sq = sb("sq", [S, RANK])
        ms = sb("ms", [S, 2])
        rstd = sb("rstd", [S, 1])
        ln = [sb(f"ln{i}", [S, RANK]) for i in range(2)]
        kr = [sb(f"kr{i}", [S, 3, ROPE]) for i in range(2)]
        ps_x = [ctx.bank(f"ps_x{i}", P, KD, S) for i in range(2)]
        ps_l = [ctx.bank(f"ps_l{i}", S, W) for i in range(2)]
        ps_t = [ctx.bank(f"ps_t{i}", P, 3, S) for i in range(2)]
        id_ready = ctx.sem("id_ready")
        ticks = ctx.sem("ticks")
        w_in = ctx.sem("lnw_loaded")
        zeros = ctx.sem("kr_zeros")
        x_in = [ctx.ev(f"x_loaded{i}", 1, step=16) for i in range(2)]
        normed = ev("x_normed", 1, 2)
        x_turned = ev("x_turned", 1, 2)
        hi, lo = ev("x_hi", 1), ev("x_lo", 1, 2)
        put = [ctx.ev(f"xT_stored{i}", 2, 2, 16) for i in range(2)]
        lat_mm = ev("lat_products", 1)
        squared = ev("lat_squared", 1)
        rms_in = ev("lat_mean_square", 1)
        rms = ev("lat_rstd", 1, 1)
        lat_ready = ev("lat_normed", 1)
        kr_ready = ev("kr_copied", 1, 2)
        v_kept = ev("lat_v_kept", 1, 2)
        turned = ev("lat_turned", 1)
        kept = ev("lat_kept", 1, 2)
        block = ctx.enter_context(nc.Block())

        def has(h, i):
            return not isinstance(h, int) or 0 <= i < B

        def steps(eng, step):
            for i in range(-3, 0):
                step(0, i)
            with eng.Fori(0, (B - 3) // 2) as h:
                step(h, 0)
                step(h, 1)
            for i in range((B - 3) // 2 * 2, B):
                step(0, i)

        @block.sync
        def _(sp):
            sp.dma_start(w_ln[:, :], lnw).then_inc(w_in, 16)
            for i in range(2):
                put[i].open(sp)

            def body(b, par):
                wait(sp, normed, b, -2)
                sp.dma_start(xs[par][:, :], x[b]).then_inc(x_in[par].sem, 16)

            def store(b, h, par):
                cols = bass.ds(b * S, S)
                wait(sp, lo, b)
                sp.dma_start(xT_hi[:, :, cols], xh[par][:, :, :].bitcast(F32)).then_inc(put[par].sem, 16)
                sp.dma_start(xT_lo[:, :, cols], xl[par][:, :, :].bitcast(F32)).then_inc(put[par].sem, 16)

            body(0, 0)
            body(1, 1)
            with sp.Fori(0, B // 2 - 1) as h:
                for par in range(2):
                    body(h * 2 + 2 + par, par)
                    store(h * 2 + par, h, par)
            for par in range(2):
                store(B - 2 + par, B // 2 - 1, par)
            for par in range(2):
                sp.wait_ge(put[par].sem, put[par].at(B // 2 - 1, 1))

        @block.gpsimd
        def _(pool):
            identity(pool, ident[:, :], id_ready)
            for i in range(2):
                pool.memset(kr[i][:, :, :], 0.0).then_inc(zeros, 1)
            exponent(pool, minus_half[:, :], half_ready)
            v_kept.open(pool)
            rms.open(pool)

            def step(h, i):
                b = h * 2 + i
                if has(h, i + 3):
                    norm.root(pool, b + 3, minus_half)
                if has(h, i + 1):
                    wait(pool, rms_in, b + 1)
                    pool.tensor_tensor(rstd[:, :], ms[:, 1:2], minus_half[:, :], ALU.pow).then_inc(rms.sem, 1)
                    wait(pool, lat_ready, b + 1)
                    carry(pool, h, ticks)
                    pool.tensor_copy(lat_v[:, b + 1, :], ln[(i + 1) % 2][:, :]).then_inc(v_kept.sem, 1)

            steps(pool, step)

        @block.vector
        def _(dve):
            normed.open(dve)
            lo.open(dve)
            kr_ready.open(dve)
            dve.wait_ge(w_in, 16)
            dve.wait_ge(zeros, 2)

            def low(h, i):
                b, par = h * 2 + i, i % 2
                wait(dve, hi, b)
                wait(dve, put[par], h + i // 2, -1)
                dve.tensor_tensor(xl[par][:, :, :], ps_x[par][:, :, :], xh[par][:, :, :], ALU.subtract).then_inc(lo.sem, 1)

            def latent(h, i):
                b, par = h * 2 + i, i % 2
                wait(dve, squared, b)
                dve.tensor_scalar(ms[:, 1:2], ms[:, 0:1], 1.0 / RANK, RMS_EPS, ALU.mult, ALU.add).then_inc(rms_in.sem, 1)
                wait(dve, rms, b)
                wait(dve, v_kept, b, -2)
                wait(dve, kept, b, -2)
                dve.scalar_tensor_tensor(ln[par][:, :], ps_l[par][:, 0:RANK], rstd[:, 0:1], w_ln[:, :],
                                         ALU.mult, ALU.mult).then_inc(lat_ready.sem, 1)
                dve.tensor_copy(kr[par][:, 1, :], ps_l[par][:, RANK:W]).then_inc(kr_ready.sem, 1)

            def step(h, i):
                b, par = h * 2 + i + 3, (i + 3) % 2
                if has(h, i + 3):
                    wait(dve, x_in[par], h + (i + 3) // 2)
                    norm.statistics(dve, b, xs[par][:, :])
                if has(h, i + 2):
                    low(h, i + 2)
                if has(h, i + 3):
                    wait(dve, x_turned, b, -2)
                    norm.scale(dve, b, xn[par][:, :], xs[par][:, :]).then_inc(normed.sem, 1)
                if has(h, i + 1):
                    latent(h, i + 1)

            steps(dve, step)

        @block.scalar
        def _(act):
            kept.open(act)

            def step(h, i):
                b = h * 2 + i
                if has(h, i + 2):
                    par = i % 2
                    wait(act, x_turned, b + 2)
                    wait(act, put[par], h + (i + 2) // 2, -1)
                    act.activation(xh[par][:, :, :], ps_x[par][:, :, :], ACT.Copy).then_inc(hi.sem, 1)
                if has(h, i + 1):
                    wait(act, lat_mm, b + 1)
                    wait(act, rms, b)
                    act.activation(sq[:, :], ps_l[(i + 1) % 2][:, 0:RANK], ACT.Square, accum_out=ms[:, 0:1])\
                        .then_inc(squared.sem, 1)
                if has(h, i):
                    wait(act, turned, b)
                    act.activation(lat_kT[:, :, bass.ds(b * S, S)], ps_t[i % 2][:, :, :], ACT.Copy).then_inc(kept.sem, 1)

            steps(act, step)

        @block.tensor
        def _(pe):
            pe.wait_ge(id_ready, 2)

            x_turned.open(pe)

            def step(h, i):
                b = h * 2 + i
                if has(h, i + 2):
                    par = i % 2
                    wait(pe, normed, b + 2)
                    wait(pe, lo, b)
                    for k in range(KD):
                        mm = pe.transpose(ps_x[par][:, k, :], xn[par][:, k * P:(k + 1) * P], ident[:, :])
                    mm.then_inc(x_turned.sem, 1)
                if has(h, i + 1):
                    par = (i + 1) % 2
                    wait(pe, lo, b + 1)
                    wait(pe, kr_ready, b - 1)
                    for k in range(KD):
                        mm = mm3(pe, ps_l[par][:, :], xh[par][:, k, :], xl[par][:, k, :], kva_hi[:, k, :],
                                 kva_lo[:, k, :], k == 0, k == KD - 1)
                    mm.then_inc(lat_mm.sem, 1)
                if has(h, i):
                    par = i % 2
                    wait(pe, kr_ready, b)
                    wait(pe, kept, b - 2)
                    pe.transpose(ps_t[par][:, 0, :], ln[par][:, :], ident[:, :])
                    pe.transpose(ps_t[par][:, 1, :], kr[par][:, 1:3, :], ident[:, :])
                    pe.transpose(ps_t[par][:, 2, :], kr[par][:, 0:2, :], ident[:, :]).then_inc(turned.sem, 1)

            steps(pe, step)
    return ctx


def self_attention(nc, xT_hi, xT_lo, qf_hi, qf_lo, qr_hi, qr_lo, lat_kT, lat_v, oT):
    NU = NQ * G
    ctx = Phase(nc, "sa")
    with ctx:
        sb = ctx.sb
        ev = ctx.ev
        ident = sb("ident", [S, S])
        mask = sb("mask", [S, S])
        xh = sb("xh", [P, 2, KD, GT], F32R)
        xl = sb("xl", [P, 2, KD, GT], F32R)
        qn = [sb(f"qn{i}", [P, HQ, GT]) for i in range(2)]
        qr = [sb(f"qr{i}", [P, HQ // 2, GT]) for i in range(2)]
        prob = [sb(f"prob{i}", [S, HQ, S]) for i in range(2)]
        top = [sb(f"top{i}", [S, HQ]) for i in range(2)]
        total = [sb(f"total{i}", [S, HQ]) for i in range(2)]
        pT = [sb(f"pT{i}", [S, HQ, S]) for i in range(2)]
        val = [sb(f"val{i}", [S, RANK]) for i in range(2)]
        ov = [sb(f"ov{i}", [P, HQ, S]) for i in range(2)]
        ps_q = [ctx.bank(f"ps_q{i}", P, GT) for i in range(2)]
        ps_s = [ctx.bank(f"ps_s{i}", S, HQ, S) for i in range(2)]
        ps_t = [ctx.bank(f"ps_t{i}", S, HQ, S) for i in range(2)]
        ps_o = [ctx.bank(f"ps_o{i}", P, HQ, S) for i in range(2)]
        consts = ctx.sem("consts")
        ticks = ctx.sem("ticks")
        x_in = ev("xT_loaded", 2, step=16)
        q_mm = ev("q_projected", 6 * NQ, 1)
        qn_ready = ev("q_nope_copied", 4 * NQ)
        qr_ready = ev("q_rot_copied", 2 * NQ)
        scored = ev("scored", NU)
        masked = ev("masked", NU, 2)
        maxed = ev("maxed", NU)
        shifted = ev("shifted", NU)
        exped = ev("exped", NU)
        summed = ev("summed", 2 * NU)
        probs = ev("probs", NU)
        p_turned = ev("p_turned", NU, 2)
        pT_ready = ev("pT_ready", NU, 2)
        val_ready = ev("values_ready", NU)
        pv = ev("weighted", NU, 2)
        o_ready = ev("o_ready", NU, 2)
        o_put = [ev(f"o_stored{i}", NU // 2, 1, 16) for i in range(2)]
        block = ctx.enter_context(nc.Block())
        NG = B // G

        def groups(eng, body):
            body(0, True)
            with eng.Fori(1, NG - 1) as g:
                body(g, True)
            body(NG - 1, False)

        def begun(g, n):
            return not isinstance(g, int) or g or n >= 0

        def following(g, hq, more):
            if hq + 1 < NQ:
                return g, hq + 1
            return (g + 1, 0) if more else None

        @block.sync
        def _(sp):
            def load(g, n_free):
                for src, dst in ((xT_hi, xh), (xT_lo, xl)):
                    sp.dma_start(dst[:, bass.ds(n_free, 1), :, :].bitcast(F32),
                                 src[:, :, bass.ds(g * GT, GT)]).then_inc(x_in.sem, 16)

            for i in range(2):
                o_put[i].open(sp)
            load(0, 0)

            def body(g, more):
                for n in range(NU):
                    if n == 0 and more:
                        wait(sp, q_mm, g, -1)
                        wait(sp, x_in, g, 1)
                        load(g + 1, (g + 1) % 2)
                    hq, s = n // G, n % G
                    wait(sp, o_ready, g, n)
                    sp.dma_start(oT[:, hq * HQ:(hq + 1) * HQ, bass.ds(g * GT + s * S, S)], ov[n % 2][:, :, :])\
                        .then_inc(o_put[n % 2].sem, 16)

            groups(sp, body)
            for i in range(2):
                sp.wait_ge(o_put[i].sem, o_put[i].at(NG - 1, NU // 2 - 1))

        @block.gpsimd
        def _(pool):
            identity(pool, ident[:, :], consts)
            pool.memset(mask[:, :], 0.0).then_inc(consts, 1)
            pool.wait_ge(consts, 3)
            pool.affine_select(out=mask[:, :], in_=mask[:, :], compare_op=ALU.is_ge, fill=MASKED, base=0,
                               pattern=[[-1, S]], channel_multiplier=1).then_inc(consts, 1)

            def body(g, more):
                for n in range(NU):
                    wait(pool, pv, g, n - 2)
                    carry(pool, g, ticks)
                    pool.tensor_copy(val[n % 2][:, :], lat_v[:, g * G + n % G, :]).then_inc(val_ready.sem, 1)

            groups(pool, body)

        @block.tensor
        def _(pe):
            pe.wait_ge(consts, 4)
            p_turned.open(pe)
            pv.open(pe)
            q_mm.open(pe)

            def project(g, hq, j, rot):
                u = (0, 2, 3, 5)[j] if not rot else (1, 4)[j]
                first = isinstance(g, int) and g == 0 and hq == 0
                if u == 3 or (u == 0 and not first):
                    wait(pe, qr_ready, g, 2 * hq + (0 if u else -1))
                elif u != 0 and not (u == 1 and first):
                    wait(pe, qn_ready, g, 4 * hq + {1: -1, 2: 0, 4: 1, 5: 2}[u])
                if u == 0 and hq == 0:
                    wait(pe, x_in, g, 1)
                w_hi, w_lo, w = (qr_hi, qr_lo, P) if rot else (qf_hi, qf_lo, RANK)
                for k in range(KD):
                    c0 = (2 * hq + j) * P if rot else 0
                    a_hi = w_hi[:, k, c0:c0 + P] if rot else w_hi[:, k, hq * HQ + j, :]
                    a_lo = w_lo[:, k, c0:c0 + P] if rot else w_lo[:, k, hq * HQ + j, :]
                    slot = g % 2
                    mm = mm3(pe, ps_q[u % 2][:, :], a_hi, a_lo, xh[:, slot, k, :], xl[:, slot, k, :],
                             k == 0, k == KD - 1)
                mm.then_inc(q_mm.sem, 1)

            def score(g, n):
                hq, s = n // G, n % G
                if s == 0:
                    wait(pe, qn_ready, g, 4 * hq + 3)
                    wait(pe, qr_ready, g, 2 * hq + 1)
                wait(pe, masked, g, n - 2)
                for j in range(HQ):
                    cols = slice(s * S, (s + 1) * S)
                    keys = lambda c: lat_kT[:, c, bass.ds(g * GT + s * S, S)]
                    pe.matmul(ps_s[n % 2][:, j, :], qn[hq % 2][:, j, cols], keys(0), start=True, stop=False)
                    mm = pe.matmul(ps_s[n % 2][:, j, :], qr[hq % 2][:, j // 2, cols], keys(1 + j % 2),
                                   start=False, stop=True)
                mm.then_inc(scored.sem, 1)

            def turn(g, n):
                wait(pe, probs, g, n)
                wait(pe, pT_ready, g, n - 2)
                for j in range(HQ):
                    mm = pe.transpose(ps_t[n % 2][:, j, :], prob[n % 2][:, j, :], ident[:, :])
                mm.then_inc(p_turned.sem, 1)

            def weigh(g, n):
                wait(pe, pT_ready, g, n)
                wait(pe, val_ready, g, n)
                wait(pe, o_ready, g, n - 2)
                pe.matmul(ps_o[n % 2][:, :, :], val[n % 2][:, :], pT[n % 2][:, :, :], start=True, stop=True)\
                    .then_inc(pv.sem, 1)

            def queries(g):
                for j in range(HQ):
                    project(g, 0, j, False)
                    if j % 2 == 0:
                        project(g, 0, j // 2, True)

            def body(g, more):
                for n in range(NU):
                    hq, s = n // G, n % G
                    heads = following(g, hq, more)
                    score(g, n)
                    if begun(g, n - 2):
                        weigh(g, n - 2)
                    if heads:
                        project(*heads, s, False)
                    if begun(g, n - 1):
                        turn(g, n - 1)
                    if heads and s % 2 == 0:
                        project(*heads, s // 2, True)

            queries(0)
            groups(pe, body)
            turn(NG - 1, NU - 1)
            weigh(NG - 1, NU - 2)
            weigh(NG - 1, NU - 1)

        @block.scalar
        def _(act):
            pT_ready.open(act)
            o_ready.open(act)

            def query(g, hq, j):
                wait(act, q_mm, g, 6 * hq + (0, 2, 3, 5)[j])
                act.activation(qn[hq % 2][:, j, :], ps_q[(0, 2, 3, 5)[j] % 2][:, :], ACT.Copy).then_inc(qn_ready.sem, 1)

            def exp(g, n):
                wait(act, shifted, g, n)
                act.activation(prob[n % 2][:, :, :], prob[n % 2][:, :, :], ACT.Exp, scale=MLA_SCALE).then_inc(exped.sem, 1)

            def copy_pT(g, n):
                wait(act, p_turned, g, n)
                wait(act, pv, g, n - 2)
                act.activation(pT[n % 2][:, :, :], ps_t[n % 2][:, :, :], ACT.Copy).then_inc(pT_ready.sem, 1)

            def copy_o(g, n):
                wait(act, pv, g, n)
                wait(act, o_put[n % 2], g, n // 2 - 1)
                act.activation(ov[n % 2][:, :, :], ps_o[n % 2][:, :, :], ACT.Copy).then_inc(o_ready.sem, 1)

            def body(g, more):
                for n in range(NU):
                    hq, s = n // G, n % G
                    heads = following(g, hq, more)
                    if begun(g, n - 2):
                        copy_o(g, n - 2)
                    exp(g, n)
                    if heads:
                        query(*heads, s)
                    if begun(g, n - 1):
                        copy_pT(g, n - 1)

            for j in range(HQ):
                query(0, 0, j)
            groups(act, body)
            copy_pT(NG - 1, NU - 1)
            copy_o(NG - 1, NU - 2)
            copy_o(NG - 1, NU - 1)

        @block.vector
        def _(dve):
            masked.open(dve)
            dve.wait_ge(consts, 4)

            def query(g, hq, j):
                wait(dve, q_mm, g, 6 * hq + (1, 4)[j])
                dve.tensor_copy(qr[hq % 2][:, j, :], ps_q[(1, 4)[j] % 2][:, :]).then_inc(qr_ready.sem, 1)

            def softmax(g, n):
                p, mx = prob[n % 2], top[n % 2]
                wait(dve, scored, g, n)
                wait(dve, p_turned, g, n - 2)
                dve.tensor_tensor(p[:, :, :], ps_s[n % 2][:, :, :], over_heads(mask[:, :], HQ), ALU.add).then_inc(masked.sem, 1)
                wait(dve, masked, g, n)
                dve.tensor_reduce(mx[:, :], p[:, :, :], AX.X, ALU.max).then_inc(maxed.sem, 1)
                wait(dve, maxed, g, n)
                dve.tensor_tensor(p[:, :, :], p[:, :, :], along(mx[:, :], S), ALU.subtract).then_inc(shifted.sem, 1)

            def divide(g, n):
                p, sm = prob[n % 2], total[n % 2]
                wait(dve, exped, g, n)
                dve.tensor_reduce(sm[:, :], p[:, :, :], AX.X, ALU.add).then_inc(summed.sem, 1)
                wait(dve, summed, g, 2 * n)
                dve.reciprocal(sm[:, :], sm[:, :]).then_inc(summed.sem, 1)
                wait(dve, summed, g, 2 * n + 1)
                dve.tensor_tensor(p[:, :, :], p[:, :, :], along(sm[:, :], S), ALU.mult).then_inc(probs.sem, 1)

            def body(g, more):
                for n in range(NU):
                    hq, s = n // G, n % G
                    heads = following(g, hq, more)
                    softmax(g, n)
                    divide(g, n)
                    if heads and s % 2 == 0:
                        query(*heads, s // 2)

            query(0, 0, 0)
            query(0, 0, 1)
            groups(dve, body)
    return ctx


class RopeTables:

    HF = HD // 2
    ROUND = 1.5 * 2.0 ** 23
    STEPS = 7

    def __init__(self, ctx, pos_ctx, pos_x, inv_freq, k_norm_w, q_norm_w, tables):
        sb, HF = ctx.sb, self.HF
        self.src = pos_ctx, pos_x, inv_freq, k_norm_w, q_norm_w
        self.tables = tables
        self.pos_i = sb("pos_i", [P, 4, B], I32)
        self.pos = sb("pos", [P, B, 4])
        self.freq = sb("freq", [P, HF])
        self.w = [sb(f"{n}_norm_w", [P, HD]) for n in "kq"]
        self.w_rot = [sb(f"{n}_norm_w_rot", [P, HD]) for n in "kq"]
        self.turns = sb("turns", [P, 4, HF])
        self.ang = [sb(f"ang{i}", [P, 4, HF]) for i in range(2)]
        self.sin = [sb(f"sin{i}", [P, 4, HF]) for i in range(2)]
        self.cos = [sb(f"cos{i}", [P, 4, HF]) for i in range(2)]
        self.tab = [sb(f"tab{i}", [P, 5, 2, HD]) for i in range(2)]
        self.loaded, self.zeroed, self.ready = (ctx.sem(n) for n in ("rope_loaded", "rope_zeroed", "rope_ready"))
        self.reduced = ctx.ev("angle_steps", self.STEPS)
        self.sines = ctx.ev("sines", 2)
        self.cosine = ctx.ev("cosine_steps", 2)
        self.made = ctx.ev("tables_made", 1)
        self.put = [ctx.ev(f"tables_stored{i}", 1, 1, 16) for i in range(2)]
        self.ticks = ctx.sem("rope_ticks")

    def load(self, sp):
        pos_ctx, pos_x, inv_freq, k_norm_w, q_norm_w = self.src
        for i in range(2):
            self.put[i].open(sp)
        sp.wait_ge(self.zeroed, 1)
        sp.dma_start(self.pos_i[0:CT, 0:3, :], pos_ctx).then_inc(self.loaded, 16)
        sp.dma_start(self.pos_i[0:S, 3, :], pos_x).then_inc(self.loaded, 16)
        sp.dma_start(self.freq[:, :], inv_freq).then_inc(self.loaded, 16)
        sp.dma_start(self.w[0][:, :], k_norm_w).then_inc(self.loaded, 16)
        sp.dma_start(self.w[1][:, :], q_norm_w).then_inc(self.loaded, 16)

    def store(self, sp, b, par):
        wait(sp, self.made, b)
        carry(sp, b, self.ticks)
        sp.dma_start(self.tables[b], self.tab[par][:, :, :, :]).then_inc(self.put[par].sem, 16)

    def prepare(self, dve):
        HF = self.HF
        dve.memset(self.pos_i[:, :, :], 0).then_inc(self.zeroed, 1)
        dve.wait_ge(self.loaded, 80)
        dve.tensor_copy(self.pos[:, :, :], self.pos_i[:, :, :].rearrange("p t b -> p b t")).then_inc(self.ready, 1)
        for w, rot in zip(self.w, self.w_rot):
            dve.tensor_scalar(rot[:, 0:HF], w[:, HF:HD], -1.0, None, ALU.mult).then_inc(self.ready, 1)
            dve.tensor_copy(rot[:, HF:HD], w[:, 0:HF]).then_inc(self.ready, 1)
        dve.wait_ge(self.ready, 5)

    def angles(self, dve, b, par):
        HF, step = self.HF, [0]
        ang, turns = self.ang[par][:, :, :], self.turns[:, :, :]

        def then(ins):
            ins.then_inc(self.reduced.sem, 1)
            wait(dve, self.reduced, b, step[0])
            step[0] += 1

        if not isinstance(b, int) or b > 1:
            wait(dve, self.sines, b, -3)
        pos = self.pos[:, bass.ds(b, 1), :].rearrange("p o t -> p (o t)")
        then(dve.tensor_tensor(ang, along(pos, HF), over_heads(self.freq[:, :], 4), ALU.mult))
        then(dve.tensor_scalar(turns, ang, float(1 / (2 * np.pi)), self.ROUND, ALU.mult, ALU.add))
        then(dve.tensor_scalar(turns, turns, self.ROUND, -PI2[0], ALU.subtract, ALU.mult))
        then(dve.tensor_tensor(ang, ang, turns, ALU.add))
        then(dve.scalar_tensor_tensor(ang, turns, PI2[1] / PI2[0], ang, ALU.mult, ALU.add))
        then(dve.tensor_scalar(ang, ang, 3.1415925, None, ALU.min))
        then(dve.tensor_scalar(ang, ang, -3.1415925, None, ALU.max))

    def sine(self, act, b, par):
        wait(act, self.reduced, b, self.STEPS - 1)
        if not isinstance(b, int) or b > 1:
            wait(act, self.made, b, -2)
        ang = self.ang[par][:, :, :]
        act.activation(self.sin[par][:, :, :], ang, ACT.Sin).then_inc(self.sines.sem, 1)
        act.activation(self.cos[par][:, :, :], ang, ACT.Sin, scale=0.5).then_inc(self.sines.sem, 1)

    def make(self, pool, b, h, par):
        sin, cos = self.sin[par], self.cos[par]
        if isinstance(b, int) and b == 0:
            pool.wait_ge(self.ready, 5)
        wait(pool, self.sines, b, 1)
        pool.tensor_tensor(cos[:, :, :], cos[:, :, :], cos[:, :, :], ALU.mult).then_inc(self.cosine.sem, 1)
        wait(pool, self.cosine, b, 0)
        carry(pool, b, self.ticks)
        pool.tensor_scalar(cos[:, :, :], cos[:, :, :], -2.0, 1.0, ALU.mult, ALU.add).then_inc(self.cosine.sem, 1)
        wait(pool, self.cosine, b, 1)
        wait(pool, self.put[par], h, -1)
        for tiles, src, i in ((slice(0, 4), slice(0, 4), 0), (slice(4, 5), slice(3, 4), 1)):
            n = tiles.stop - tiles.start
            for c, part, w in ((0, cos, self.w[i]), (1, sin, self.w_rot[i])):
                angles = part[:, src, :].unsqueeze(2).broadcast_to((P, n, 2, self.HF))
                weights = w[:, :].rearrange("p (h f) -> p h f", h=2).unsqueeze(1).broadcast_to((P, n, 2, self.HF))
                out = self.tab[par][:, tiles, c, :].rearrange("p t (h f) -> p t h f", h=2)
                ins = pool.tensor_tensor(out, angles, weights, ALU.mult)
        ins.then_inc(self.made.sem, 1)


def project_out(nc, oT, w_src, res, store_x, store_xT, rope=None, router=None, keep=None):
    CH = HQ * P
    ctx = Phase(nc, "out2" if router is not None else "out1")
    with ctx:
        sb = ctx.sb
        ev = ctx.ev
        ident = sb("ident", [P, P])
        RAW = 8
        w_raw = sb("w_raw", [P, RAW, D])
        w_hi = sb("w_hi", [P, H, D], F32R)
        w_lo = sb("w_lo", [P, H, D], F32R)
        o_raw = sb("o_raw", [P, NQ, HQ, P])
        o_hi = sb("o_hi", [P, NQ, HQ, P], F32R)
        o_lo = sb("o_lo", [P, NQ, HQ, P], F32R)
        r_in = [sb(f"r_in{i}", [P, D]) for i in range(2)]
        y = [sb(f"y{i}", [P, D]) for i in range(2)]
        yn = [sb(f"yn{i}", [P, D]) for i in range(2)]
        layer = LayerNorm(ctx, P)
        minus_half = sb("minus_half", [P, 1])
        half_ready = ctx.sem("minus_half_ready")
        xh = [sb(f"xh{i}", [P, KD, P], F32R) for i in range(2)]
        xl = [sb(f"xl{i}", [P, KD, P], F32R) for i in range(2)]
        ps_y = [ctx.bank(f"ps_y{i}", P, D) for i in range(2)]
        ps_x = [ctx.bank(f"ps_x{i}", P, KD, P) for i in range(2)]
        ps_r = ctx.bank("ps_r", P, TOTAL)
        id_ready = ctx.sem("id_ready")
        w_in = [ctx.sem(f"w_loaded{i}") for i in range(RAW)]
        w_hi_ready = ctx.sem("w_hi_ready")
        w_lo_ready = ctx.sem("w_lo_ready")
        o_in = [ev(f"o_loaded{c}", 1, step=16) for c in range(NQ)]
        o_hi_ready, o_lo_ready = ev("o_hi_ready", NQ), ev("o_lo_ready", NQ)
        used = ev("o_used", NQ, NQ)
        r_loaded = [ev(f"r_loaded{i}", 1, step=16) for i in range(2)]
        added = ev("y_added", 1, 2)
        normed = ev("y_normed", 1)
        turned = ev("y_turned", 1, 2)
        hi, lo = ev("x_hi", 1), ev("x_lo", 1)
        y_put = [ev(f"y_stored{i}", 1, 1, 16) for i in range(2)]
        x_put = [ev(f"xT_stored{i}", 2, 2, 16) for i in range(2)]
        ticks = ctx.sem("ticks")
        if rope is not None:
            guest = RopeTables(ctx, *rope)
        if router is not None:
            cls_src, bias_src = router
            acc, oh, place, weight, run, rows_n, tokens = keep
            cls = sb("cls", [P, KD, TOTAL])
            cls_hi = sb("cls_hi", [P, KD, TOTAL], F32R)
            cls_lo = sb("cls_lo", [P, KD, TOTAL], F32R)
            bias = sb("bias", [P, TOTAL])
            iota = sb("iota", [P, TOTAL])
            iota_i = sb("iota_i", [P, TOTAL], I32)
            small = sb("small", [P, 4])
            prob = sb("prob", [P, TOTAL])
            biased = sb("biased", [P, TOTAL])
            best = sb("best", [P, 8])
            best_i = sb("best_i", [P, 8], U32)
            best_f = sb("best_f", [P, 8])
            share = sb("share", [P, TOTAL])
            hot = sb("hot", [P, 2, TOTAL])
            chosen = sb("chosen", [P, TOTAL])
            below = sb("below", [P, P])
            ones = sb("ones", [P, P])
            spot = sb("spot", [P, TOTAL])
            spots = sb("spots", [P, 2, TOTAL])
            dest = sb("dest", [P, 2])
            dest_i = [sb(f"dest_i{i}", [P, 2], U32) for i in range(2)]
            base = sb("base", [P, TOTAL])
            base_i = sb("base_i", [P, TOTAL], I32)
            ids_i = sb("ids_i", [P, TT], I32)
            ids_f = sb("ids_f", [P, TT])
            id_i = [sb(f"id_i{i}", [P, 1], I32) for i in range(2)]
            fill = sb("fill", [P, (DUMP + P) // P], I32)
            ps_c = ctx.bank("ps_c", P, 2, E)
            list_ready = ctx.sem("list_filled")
            zeroed = ctx.sem("list_zeros")
            tables_ready = ctx.sem("place_tables")
            counted = ev("choices_counted", 1)
            p_step = ev("place_step", 5)
            scattered = ev("tokens_listed", 2, 0, 16)
            r_src = ctx.sem("router_loaded")
            r_split = ctx.sem("router_split")
            logits = ev("logits", 1)
            r_step = ev("route_step", 11)
            r_exp = ev("route_exp", 1)
            r_done = ev("routed", 1)
        block = ctx.enter_context(nc.Block())

        @block.sync
        def _(sp):
            for i in range(2):
                y_put[i].open(sp)
                x_put[i].open(sp)
            if rope is not None:
                guest.load(sp)
            if router is not None:
                sp.dma_start(cls[:, :, :], cls_src).then_inc(r_src, 16)
                sp.dma_start(bias[:, :], bias_src).then_inc(r_src, 16)
                sp.wait_ge(zeroed, 1)
                sp.dma_start(tokens.rearrange("(p n) o -> p (n o)", p=P), fill[:, :]).then_inc(list_ready, 16)

            def load(t, h, par, chunks=range(NQ), residual=True):
                cols = bass.ds(t * P, P)
                for c in chunks:
                    if not isinstance(t, int) or t:
                        wait(sp, o_lo_ready, t, c - NQ)
                    sp.dma_start(o_raw[:, c, :, :], oT[:, c * HQ:(c + 1) * HQ, cols]).then_inc(o_in[c].sem, 16)
                if residual:
                    wait(sp, added, t, -2)
                    sp.dma_start(r_in[par][:, :], res[cols, :]).then_inc(r_loaded[par].sem, 16)

            def store(t, h, par):
                cols = bass.ds(t * P, P)
                if store_x is not None:
                    wait(sp, added, t)
                    sp.dma_start(store_x[cols, :], y[par][:, :]).then_inc(y_put[par].sem, 16)
                else:
                    wait(sp, normed, t)
                    sp.dma_start(rows_n[cols, :], yn[par][:, :]).then_inc(y_put[par].sem, 16)
                    return
                wait(sp, lo, t)
                carry(sp, t, ticks)
                dst_hi, dst_lo = store_xT
                sp.dma_start(dst_hi[:, :, cols], xh[par][:, :, :].bitcast(F32)).then_inc(x_put[par].sem, 16)
                sp.dma_start(dst_lo[:, :, cols], xl[par][:, :, :].bitcast(F32)).then_inc(x_put[par].sem, 16)

            for h in range(H):
                if h >= RAW:
                    sp.wait_ge(w_lo_ready, h - RAW + 1)
                sp.dma_start(w_raw[:, h % RAW, :], w_src[:, h, :]).then_inc(w_in[h % RAW], 16)
                if h % HQ == 0:
                    load(0, 0, 0, [h // HQ], h == H - HQ)
            load(1, 0, 1)
            with sp.Fori(0, TT // 2 - 1) as h:
                for par in range(2):
                    load(h * 2 + 2 + par, h + 1, par)
                    store(h * 2 + par, h, par)
                    if rope is not None:
                        guest.store(sp, h * 2 + par, par)
            for par in range(2):
                store(TT - 2 + par, TT // 2 - 1, par)
                if rope is not None:
                    guest.store(sp, TT - 2 + par, par)
            if rope is not None:
                for par in range(2):
                    guest.store(sp, TT + par, par)
            for par in range(2):
                if rope is not None:
                    sp.wait_ge(guest.put[par].sem, guest.put[par].at(B // 2 - 1))
                sp.wait_ge(y_put[par].sem, y_put[par].at(TT // 2 - 1))
                if store_xT is not None:
                    sp.wait_ge(x_put[par].sem, x_put[par].at(TT // 2 - 1, 1))

        @block.gpsimd
        def _(pool):
            identity(pool, ident[:, :], id_ready)
            if router is not None:
                pool.iota(iota_i[:, :], pattern=[[1, TOTAL]], base=0, channel_multiplier=0).then_inc(id_ready, 1)
                pool.wait_ge(id_ready, 3)
                pool.tensor_copy(iota[:, :], iota_i[:, :]).then_inc(id_ready, 1)
                pool.memset(fill[:, :], 0).then_inc(zeroed, 1)
                pool.iota(ids_i[:, :], pattern=[[P, TT]], base=0, channel_multiplier=1).then_inc(tables_ready, 1)
                pool.iota(base_i[:, 0:E], pattern=[[REGION, E]], base=0, channel_multiplier=0).then_inc(tables_ready, 1)
                pool.iota(base_i[:, E:TOTAL], pattern=[[0, TOTAL - E]], base=DUMP, channel_multiplier=1)\
                    .then_inc(tables_ready, 1)
                pool.memset(ones[:, :], 1.0).then_inc(tables_ready, 1)
                pool.wait_ge(tables_ready, 4)
                pool.tensor_copy(ids_f[:, :], ids_i[:, :]).then_inc(tables_ready, 1)
                pool.tensor_copy(base[:, :], base_i[:, :]).then_inc(tables_ready, 1)
                pool.affine_select(out=below[:, :], in_=ones[:, :], compare_op=ALU.is_ge, fill=0.0, base=-1,
                                   pattern=[[1, P]], channel_multiplier=-1).then_inc(tables_ready, 1)
                pool.wait_ge(r_src, 32)
                pool.tensor_copy(cls_hi[:, :, :], cls[:, :, :]).then_inc(r_split, 1)
                pool.wait_ge(r_split, 1)
                pool.tensor_tensor(cls_lo[:, :, :], cls[:, :, :], cls_hi[:, :, :], ALU.subtract).then_inc(r_split, 1)
            exponent(pool, minus_half[:, :], half_ready)
            if rope is not None:
                guest.make(pool, 0, 0, 0)

            def scatter(t, par):
                for c in range(2):
                    if c == 0:
                        wait(pool, p_step, t, 4)
                    if c or not isinstance(t, int) or t:
                        wait(pool, scattered, t, c - 1)
                    carry(pool, t, ticks)
                    pool.indirect_dma_start(tokens, bass.IndirectOffsetOnAxis(ap=dest_i[par][:, c:c + 1], axis=0),
                                            id_i[par][:, :], None).then_inc(scattered.sem, 16)

            if router is not None:
                pool.wait_ge(list_ready, 16)
            for par in range(2):
                layer.root(pool, par, minus_half)
                if rope is not None:
                    guest.make(pool, par + 1, par, 1 - par)

            def pair(h):
                for par in range(2):
                    layer.root(pool, h * 2 + par, minus_half)
                    if rope is not None:
                        guest.make(pool, h * 2 + par + 1, h + par, 1 - par)
                    if router is not None:
                        scatter(h * 2 + par - 2, par)

            pair(1)
            with pool.Fori(2, TT // 2) as h:
                pair(h)
            if rope is not None:
                guest.make(pool, B - 1, B // 2 - 1, 1)
            if router is not None:
                scatter(TT - 2, 0)
                scatter(TT - 1, 1)
                pool.wait_ge(scattered.sem, scattered.at(TT - 1, 1))

        @block.scalar
        def _(act):
            def high(t, c):
                wait(act, o_in[c], t)
                wait(act, used, t, c - NQ)
                act.activation(o_hi[:, c, :, :], o_raw[:, c, :, :], ACT.Copy).then_inc(o_hi_ready.sem, 1)

            def turn(t, h, par):
                wait(act, turned, t)
                if store_xT is not None:
                    wait(act, x_put[par], h, -1)
                elif not (isinstance(t, int) and t < 2):
                    wait(act, logits, t, -2)
                act.activation(xh[par][:, :, :], ps_x[par][:, :, :], ACT.Copy).then_inc(hi.sem, 1)

            def route(t):
                wait(act, r_step, t, 0)
                act.activation(prob[:, :], ps_r[:, :], ACT.Exp, bias=small[:, 0:1],
                               accum_out=small[:, 1:2]).then_inc(r_exp.sem, 1)

            def body(t, h, par, ahead=True):
                if ahead:
                    high(t + 2, 0)
                if router is not None and not (isinstance(t, int) and t == 0):
                    route(t - 1)
                turn(t, h, par)
                if ahead:
                    high(t + 2, 1)
                    high(t + 2, 2)
                if rope is not None:
                    guest.sine(act, t + 2, par)
                if ahead:
                    high(t + 2, 3)

            if rope is not None:
                guest.sine(act, 0, 0)
                guest.sine(act, 1, 1)
            for h in range(H):
                act.wait_ge(w_in[h % RAW], 16 * (h // RAW + 1))
                act.activation(w_hi[:, h, :], w_raw[:, h % RAW, :], ACT.Copy).then_inc(w_hi_ready, 1)
                if h % HQ == 0:
                    high(0, h // HQ)
            for c in range(NQ):
                high(1, c)
            for par in range(2):
                body(par, 0, par)
            with act.Fori(1, TT // 2 - 1) as h:
                body(h * 2, h, 0)
                body(h * 2 + 1, h, 1)
            for par in range(2):
                body(TT - 2 + par, TT // 2 - 1, par, ahead=False)
            if router is not None:
                route(TT - 1)

        @block.vector
        def _(dve):
            added.open(dve)

            def low(t, c):
                wait(dve, o_hi_ready, t, c)
                dve.tensor_tensor(o_lo[:, c, :, :], o_raw[:, c, :, :], o_hi[:, c, :, :], ALU.subtract).then_inc(o_lo_ready.sem, 1)

            def norm(t, h, par):
                wait(dve, r_loaded[par], h)
                wait(dve, used, t, NQ - 1)
                wait(dve, y_put[par], h, -1)
                if router is not None and not (isinstance(t, int) and t < 2):
                    wait(dve, r_done, t, -2)
                dve.tensor_tensor(y[par][:, :], ps_y[par][:, :], r_in[par][:, :], ALU.add).then_inc(added.sem, 1)
                wait(dve, added, t)
                wait(dve, turned, t, -2)
                layer.vector(dve, t, yn[par][:, :], y[par][:, :]).then_inc(normed.sem, 1)

            def turn(t, h, par):
                wait(dve, hi, t)
                dve.tensor_tensor(xl[par][:, :, :], ps_x[par][:, :, :], xh[par][:, :, :], ALU.subtract).then_inc(lo.sem, 1)

            def route(t, par):
                m, total, inv, back = (small[:, i:i + 1] for i in range(4))

                def then(n, ins):
                    ins.then_inc(r_step.sem, 1)
                    wait(dve, r_step, t, n)

                wait(dve, logits, t)
                then(0, dve.tensor_reduce(m, ps_r[:, :], AX.X, ALU.max, negate=True))
                wait(dve, r_exp, t)
                then(1, dve.reciprocal(inv, total))
                then(2, dve.tensor_scalar(prob[:, :], prob[:, :], inv, None, ALU.mult))
                then(3, dve.tensor_tensor(biased[:, :], prob[:, :], bias[:, :], ALU.add))
                carry(dve, t, ticks)
                then(4, dve.max(best[:, :], biased[:, :]))
                carry(dve, t, ticks)
                then(5, dve.max_index(best_i[:, :], best[:, :], biased[:, :]))
                then(6, dve.tensor_copy(best_f[:, :], best_i[:, :]))
                for c in range(2):
                    ins = dve.tensor_scalar(hot[:, c, :], iota[:, :], best_f[:, c:c + 1], None, ALU.is_equal)
                then(7, ins)
                then(8, dve.tensor_tensor(chosen[:, :], hot[:, 0, :], hot[:, 1, :], ALU.add))
                dve.tensor_tensor(oh[:, bass.ds(t, 1), :], hot[:, :, :].rearrange("p c e -> p (c e)").unsqueeze(1),
                                  hot[:, :, :].rearrange("p c e -> p (c e)").unsqueeze(1), ALU.mult)
                then(9, dve.scalar_tensor_tensor(share[:, :], chosen[:, :], ROUTE_SCALE, prob[:, :],
                                                 ALU.mult, ALU.mult))
                dve.tensor_scalar(weight[:, bass.ds(t, 1), :], share[:, :].unsqueeze(1), 1.0, None, ALU.mult)
                then(10, dve.tensor_reduce(back, share[:, E:TOTAL], AX.X, ALU.add))
                dve.scalar_tensor_tensor(acc[:, t, :], yn[par][:, :], back, y[par][:, :], ALU.mult, ALU.add)\
                    .then_inc(r_done.sem, 1)

            def locate(t, par):
                def then(n, ins):
                    ins.then_inc(p_step.sem, 1)
                    wait(dve, p_step, t, n)

                wait(dve, counted, t)
                if not isinstance(t, int) or t > 1:
                    wait(dve, scattered, t, -3)
                then(0, dve.tensor_tensor(place[:, t, :], ps_c[:, 0, :], run[:, :], ALU.add))
                dve.tensor_tensor(run[:, :], ps_c[:, 1, :], run[:, :], ALU.add)
                dve.tensor_scalar(id_i[par][:, :], ids_f[:, bass.ds(t, 1)], 0.0, None, ALU.add)
                then(1, dve.tensor_tensor(spot[:, 0:E], place[:, t, :], base[:, 0:E], ALU.add))
                then(2, dve.tensor_tensor(spots[:, :, :], oh[:, t, :].rearrange("p (c e) -> p c e", c=2),
                                          over_heads(spot[:, :], 2), ALU.mult))
                then(3, dve.tensor_reduce(dest[:, :], spots[:, :, :], AX.X, ALU.add))
                then(4, dve.tensor_copy(dest_i[par][:, :], dest[:, :]))

            def body(t, h, par, ahead=True):
                norm(t, h, par)
                if ahead:
                    low(t + 2, 0)
                if router is not None and not (isinstance(t, int) and t == 0):
                    route(t - 1, 1 - par)
                turn(t, h, par)
                if ahead:
                    low(t + 2, 1)
                if rope is not None:
                    guest.angles(dve, t + 2, par)
                if router is not None and not (isinstance(t, int) and t < 2):
                    locate(t - 2, par)
                if ahead:
                    low(t + 2, 2)
                    low(t + 2, 3)

            if rope is not None:
                guest.prepare(dve)
                guest.angles(dve, 0, 0)
                guest.angles(dve, 1, 1)
            if router is not None:
                dve.wait_ge(r_src, 32)
                dve.wait_ge(id_ready, 4)
                dve.wait_ge(tables_ready, 7)
                dve.memset(run[:, :], 0.0).then_inc(tables_ready, 1)
                dve.tensor_copy(spot[:, :], base[:, :]).then_inc(tables_ready, 1)
                dve.wait_ge(tables_ready, 9)
            for h in range(H):
                dve.wait_ge(w_hi_ready, h + 1)
                dve.tensor_tensor(w_lo[:, h, :], w_raw[:, h % RAW, :], w_hi[:, h, :], ALU.subtract).then_inc(w_lo_ready, 1)
                if h % HQ == 0:
                    low(0, h // HQ)
            for c in range(NQ):
                low(1, c)
            for t in range(4):
                body(t, t // 2, t % 2)
            with dve.Fori(2, TT // 2 - 1) as h:
                body(h * 2, h, 0)
                body(h * 2 + 1, h, 1)
            for par in range(2):
                body(TT - 2 + par, TT // 2 - 1, par, ahead=False)
            if router is not None:
                route(TT - 1, 1)
                locate(TT - 2, 0)
                locate(TT - 1, 1)

        @block.tensor
        def _(pe):
            used.open(pe)
            turned.open(pe)
            pe.wait_ge(id_ready, 2)

            def project(t, par, chunks):
                for c in chunks:
                    wait(pe, o_lo_ready, t, c)
                    if c == 0 and (not isinstance(t, int) or t > 1):
                        wait(pe, added, t, -2)
                    for j in range(HQ):
                        h = c * HQ + j
                        if isinstance(t, int) and t == 0:
                            pe.wait_ge(w_lo_ready, h + 1)
                        mm = mm3(pe, ps_y[par][:, :], o_hi[:, c, j, :], o_lo[:, c, j, :], w_hi[:, h, :], w_lo[:, h, :],
                                 h == 0, h == H - 1)
                    mm.then_inc(used.sem, 1)

            def turn(t, par):
                wait(pe, normed, t)
                if not isinstance(t, int) or t > 1:
                    wait(pe, lo, t, -2)
                for k in range(KD):
                    mm = pe.transpose(ps_x[par][:, k, :], yn[par][:, k * P:(k + 1) * P], ident[:, :])
                mm.then_inc(turned.sem, 1)

            def route(t, par):
                wait(pe, lo, t)
                if isinstance(t, int) and t == 0:
                    pe.wait_ge(r_split, 2)
                else:
                    wait(pe, r_done, t, -1)
                for k in range(KD):
                    mm = mm3(pe, ps_r[:, :], xh[par][:, k, :], xl[par][:, k, :], cls_hi[:, k, :], cls_lo[:, k, :],
                             k == 0, k == KD - 1)
                mm.then_inc(logits.sem, 1)

            def count(t):
                wait(pe, r_done, t)
                if isinstance(t, int) and t == 0:
                    pe.wait_ge(tables_ready, 7)
                else:
                    wait(pe, p_step, t, -1)
                pe.matmul(ps_c[:, 0, :], below[:, :], chosen[:, 0:E], start=True, stop=True)
                pe.matmul(ps_c[:, 1, :], ones[:, :], chosen[:, 0:E], start=True, stop=True).then_inc(counted.sem, 1)

            def body(t, par, last=False):
                if not last:
                    project(t + 1, 1 - par, (0, 1))
                turn(t, par)
                if not last:
                    project(t + 1, 1 - par, (2, 3))
                if router is not None:
                    if not (isinstance(t, int) and t == 0):
                        count(t - 1)
                    route(t, par)
                    if last:
                        count(t)

            project(0, 0, range(NQ))
            body(0, 0)
            body(1, 1)
            with pe.Fori(1, TT // 2 - 1) as h:
                body(h * 2, 0)
                body(h * 2 + 1, 1)
            body(TT - 2, 0)
            body(TT - 1, 1, last=True)
    return ctx


def cross_attention(nc, ctxT, xT_hi, xT_lo, wqT, wkT, wvT, tables, oT):
    M = (CT, CT, CT, S)
    HF = HD // 2
    ctx = Phase(nc, "ca")
    with ctx:
        sb = ctx.sb
        ev = ctx.ev
        ident = sb("ident", [P, P])
        NW = (H * HD + 2 * D) // D
        w_hi = sb("w_hi", [P, NW, KD, D], F32R)
        w_lo = sb("w_lo", [P, NW, KD, D], F32R)
        w_src = [wqT[:, :, i * D:(i + 1) * D] for i in range(4)] + [wkT, wvT]
        W_ORDER = (0, 4, 5, 1, 2, 3)
        W_SLOT = (0, 1, 0, 1, 1, 1)
        W_BEFORE = (0, 0, 1, 2, 4, 5)
        WK, WV = 4, 5
        c_raw = sb("c_raw", [P, KD, C])
        c_hi = [sb(f"c_hi{i}", [P, KD, CT], F32R) for i in range(2)]
        c_lo = [sb(f"c_lo{i}", [P, KD, CT], F32R) for i in range(2)]
        xh = [sb(f"xh{i}", [P, KD, S], F32R) for i in range(2)]
        xl = [sb(f"xl{i}", [P, KD, S], F32R) for i in range(2)]
        tab = [sb(f"tab{i}", [P, 5, 2, HD]) for i in range(2)]
        qT = sb("qT", [P, KVH, HQ, S])
        kT = [sb(f"kT{i}", [P, KVH, KV]) for i in range(2)]
        v = [sb(f"v{i}", [P, 4, KVH * HD]) for i in range(2)]
        prob = [sb(f"prob{j}", [S, 4 * CT]) for j in range(HQ)]
        top = sb("top", [S, HQ])
        down = sb("down", [S, HQ])
        total = sb("total", [S, HQ])
        inv = sb("inv", [S, HQ])
        pT = [sb(f"pT{i}", [P, 4, HQ, S]) for i in range(2)]
        ov = [sb(f"ov{i}", [P, HQ, S]) for i in range(2)]
        sq = sb("sq", [P, D])
        q1, q2, k1, k2 = (sb(n, [P, D]) for n in ("q1", "q2", "k1", "k2"))
        ssum = sb("ssum", [P, 2, HQ])
        k_rstd = sb("k_rstd", [P, HQ])
        minus_half = sb("minus_half", [P, HQ])
        half_ready = ctx.sem("minus_half_ready")
        q_scale = [sb(f"q_scale{i}", [S, KVH, HQ]) for i in range(2)]
        ps_p = [ctx.bank(f"ps_p{i}", P, D) for i in range(2)]
        ps_s = [ctx.bank(f"ps_s{i}", S, KV) for i in range(2)]
        ps_t = [ctx.bank(f"ps_t{i}", P, 4, S) for i in range(2)]
        ps_r = ctx.bank("ps_r", P, HQ * P)
        ps_o = ctx.bank("ps_o", P, HQ, S)
        id_ready = ctx.sem("id_ready")
        padded = ctx.sem("prob_padded")
        w_in = [ctx.sem(f"w_loaded{i}") for i in range(2)]
        w_hi_ready = ctx.sem("w_hi_ready")
        w_lo_ready = ctx.sem("w_lo_ready")
        c_in = ev("ctx_loaded", 1, step=16)
        c_hi_ready, c_lo_ready = ev("ctx_hi", 3), ev("ctx_lo", 3)
        x_in = [ctx.sem(f"x_loaded{i}") for i in range(2)]
        q_mm, k_mm, v_mm = ev("q_projected", 4), ev("k_projected", 4), ev("v_projected", 4)
        q_sq, k_sq = ev("q_squared", 4), ev("k_squared", 4)
        q_rot, k_rot = ev("q_products", 4), ev("k_products", 4)
        q_sum, k_sum = ev("q_squares_summed", 8, 1), ev("k_squares_summed", 8, 1)
        q_scaled, k_scaled = ev("q_scale_ready", 4), ev("k_rstd_ready", 4)
        q_added, k_added = ev("q_rotated", 4), ev("k_added", 4)
        k_normed = ev("k_rotated", 4)
        q_turned, k_turned = ev("q_turned", 4), ev("k_turned", 4)
        qT_ready, kT_ready = ev("qT_ready", 4), ev("kT_ready", 4)
        v_ready = ev("v_ready", 4)
        N = KVH * HQ
        scored = ev("scored", N)
        maxed, shifted = ev("maxed", N), ev("shift_ready", N)
        exped = ev("exped", N, 2)
        inverted = ev("inverted", N)
        probs = ev("probs", N)
        p_turned = ev("p_turned", N, HQ)
        pT_ready = ev("pT_ready", N, 2)
        pv = ev("weighted", 4, 8)
        o_ready = ev("o_ready", 4, 1)
        o_put = [ev(f"o_stored{i}", 2, 1, 16) for i in range(2)]
        block = ctx.enter_context(nc.Block())

        def inputs(eng, b, par):
            eng.wait_ge(x_in[par], b * 24 + 48 - 24 * par)

        def batches(eng, project, step, then=lambda: None):
            for i in range(4):
                project(0, i, 0)
            then()
            with eng.Fori(0, B // 2 - 1) as h:
                for par in range(2):
                    for i in range(4):
                        step(h * 2 + par, i, par, True)
            for i in range(4):
                step(B - 2, i, 0, True)
            for i in range(4):
                step(B - 1, i, 1, False)

        @block.sync
        def _(sp):
            for i in range(2):
                o_put[i].open(sp)

            def load(b, h, par):
                cols = bass.ds(b * S, S)
                if not isinstance(b, int) or b > 1:
                    wait(sp, v_mm, b, -5)
                    wait(sp, q_mm, b, -5)
                    wait(sp, q_rot, b, -5)
                    wait(sp, k_rot, b, -5)
                sp.dma_start(xh[par][:, :, :].bitcast(F32), xT_hi[:, :, cols]).then_inc(x_in[par], 16)
                sp.dma_start(xl[par][:, :, :].bitcast(F32), xT_lo[:, :, cols]).then_inc(x_in[par], 16)
                if not isinstance(b, int) or b:
                    wait(sp, c_lo_ready, b, -1)
                sp.dma_start(c_raw[:, :, :], ctxT[b]).then_inc(c_in.sem, 16)
                sp.dma_start(tab[par][:, :, :, :], tables[b]).then_inc(x_in[par], 16)

            def store(b, i):
                wait(sp, o_ready, b, i)
                sp.dma_start(oT[:, i * HQ:(i + 1) * HQ, bass.ds(b * S, S)], ov[i % 2][:, :, :])\
                    .then_inc(o_put[i % 2].sem, 16)

            for n in range(NW):
                if n >= 2:
                    sp.wait_ge(w_lo_ready, W_BEFORE[n])
                sp.dma_start(v[W_SLOT[n]][:, :, :], w_src[W_ORDER[n]]).then_inc(w_in[W_SLOT[n]], 16)
                if n == 0:
                    load(0, 0, 0)
            load(1, 0, 1)
            with sp.Fori(0, B // 2 - 1) as h:
                for par in range(2):
                    store(h * 2 + par, 0)
                    store(h * 2 + par, 1)
                    load(h * 2 + par + 2, h + 1, par)
                    store(h * 2 + par, 2)
                    store(h * 2 + par, 3)
            for b in (B - 2, B - 1):
                for i in range(4):
                    store(b, i)
            for i in range(2):
                sp.wait_ge(o_put[i].sem, o_put[i].at(B - 1, 1))

        @block.gpsimd
        def _(pool):
            identity(pool, ident[:, :], id_ready)
            exponent(pool, minus_half[:, :], half_ready)
            for j in range(HQ):
                pool.memset(prob[j][:, KV:4 * CT], 0.0).then_inc(padded, 1)

            def low(b, t, par):
                wait(pool, c_hi_ready, b, t)
                slot = (par + t) % 2
                pool.tensor_tensor(c_lo[slot][:, :, :], c_raw[:, :, t * CT:(t + 1) * CT], c_hi[slot][:, :, :],
                                   ALU.subtract).then_inc(c_lo_ready.sem, 1)

            def project(b, i, par):
                m = M[i]
                wait(pool, q_sum, b, 2 * i + 1)
                pool.tensor_tensor(q_scale[par][:, i, :], ssum[0:S, 0, :], minus_half[0:S, :], ALU.pow).then_inc(q_scaled.sem, 1)
                wait(pool, q_rot, b, i)
                pool.tensor_tensor(q1[0:S, :], q1[0:S, :], q2[0:S, :], ALU.add).then_inc(q_added.sem, 1)
                wait(pool, k_rot, b, i)
                pool.tensor_tensor(k1[0:m, :], k1[0:m, :], k2[0:m, :], ALU.add).then_inc(k_added.sem, 1)
                wait(pool, k_sum, b, 2 * i + 1)
                pool.tensor_tensor(k_rstd[0:m, :], ssum[0:m, 1, :], minus_half[0:m, :], ALU.pow).then_inc(k_scaled.sem, 1)
                wait(pool, k_scaled, b, i)
                wait(pool, k_added, b, i)
                heads = k1[0:m, :].rearrange("p (h d) -> p h d", h=KVH)
                pool.tensor_tensor(heads, heads, along(k_rstd[0:m, :], HD), ALU.mult).then_inc(k_normed.sem, 1)
                if i in (0, 1):
                    low(b, i + 1, par)
                elif i == 3 and not (isinstance(b, int) and b == B - 1):
                    low(b + 1, 0, 1 - par)

            def step(b, i, par, more):
                if more:
                    project(b + 1, i, 1 - par)

            low(0, 0, 0)
            batches(pool, project, step)

        @block.tensor
        def _(pe):
            pe.wait_ge(id_ready, 2)
            pe.wait_ge(padded, HQ)
            p_turned.open(pe)
            pv.open(pe)
            first = lambda b: isinstance(b, int) and b == 0

            def weights(b, c):
                if first(b):
                    pe.wait_ge(w_lo_ready, W_ORDER.index(c) + 1)

            def project(b, i, unit, par):
                out = ps_p[(3 * i + unit) % 2]
                done = (q_mm, k_mm, v_mm)[unit]
                c = (i, WK, WV)[unit]
                weights(b, c)
                if i == 0 and unit == 0:
                    inputs(pe, b, par)
                if unit == 0 or i == 3:
                    m, a_hi, a_lo = S, xh[par], xl[par]
                else:
                    slot = (par + i) % 2
                    m, a_hi, a_lo = CT, c_hi[slot], c_lo[slot]
                    wait(pe, c_lo_ready, b, i)
                if unit == 2:
                    wait(pe, q_rot, b, i)
                    wait(pe, q_sq, b, i)
                elif unit == 0 and not (first(b) and i == 0):
                    wait(pe, k_rot, b, i - 1)
                    wait(pe, k_sq, b, i - 1)
                elif unit == 1 and not (first(b) and i == 0):
                    wait(pe, v_ready, b, i - 1)
                for k in range(KD):
                    mm = mm3(pe, out[0:m, :], a_hi[:, k, :], a_lo[:, k, :], w_hi[:, c, k, :], w_lo[:, c, k, :],
                             k == 0, k == KD - 1)
                mm.then_inc(done.sem, 1)

            def turn_q(b, i):
                wait(pe, q_added, b, i)
                if not (first(b) and i == 0):
                    wait(pe, kT_ready, b, i - 1)
                for j in range(HQ):
                    mm = pe.transpose(ps_r[:, j * S:(j + 1) * S], q1[0:S, j * HD:(j + 1) * HD], ident[0:S, 0:S])
                mm.then_inc(q_turned.sem, 1)

            def turn_k(b, i):
                m = M[i]
                wait(pe, k_normed, b, i)
                wait(pe, qT_ready, b, i)
                for j in range(KVH):
                    mm = pe.transpose(ps_r[:, j * m:(j + 1) * m], k1[0:m, j * HD:(j + 1) * HD], ident[0:m, 0:m])
                mm.then_inc(k_turned.sem, 1)

            def score(b, i, j, par):
                if j == 0:
                    wait(pe, qT_ready, b, i)
                    if i == 0:
                        wait(pe, kT_ready, b, 3)
                wait(pe, exped, b, i * HQ + j - 2)
                pe.matmul(ps_s[j % 2][:, :], qT[:, i, j, :], kT[par][:, i, :], start=True, stop=True).then_inc(scored.sem, 1)

            def turn(b, i, j):
                n = i * HQ + j
                wait(pe, probs, b, n)
                wait(pe, pT_ready, b, n - 2)
                for t in range(4):
                    mm = pe.transpose(ps_t[j % 2][0:CT, t, :], prob[j][:, t * CT:(t + 1) * CT], ident[0:S, 0:S])
                mm.then_inc(p_turned.sem, 1)

            def weigh(b, i, par, tiles):
                if 0 in tiles:
                    wait(pe, pT_ready, b, i * HQ + HQ - 1)
                    if i == 0:
                        wait(pe, v_ready, b, 3)
                    if not (first(b) and i == 0):
                        wait(pe, o_ready, b, i - 1)
                for t in tiles:
                    mm = pe.matmul(ps_o[:, :, :], v[par][0:M[t], t, i * HD:(i + 1) * HD], pT[i % 2][0:M[t], t, :, :],
                                   start=(t == 0), stop=(t == 3))
                if 3 in tiles:
                    mm.then_inc(pv.sem, 1)

            def start(b, i, par):
                project(b, i, 0, par)
                if i:
                    turn_k(b, i - 1)
                project(b, i, 1, par)
                turn_q(b, i)
                project(b, i, 2, par)
                if i == 3:
                    turn_k(b, i)

            def step(b, i, par, more):
                score(b, i, 0, par)
                score(b, i, 1, par)
                if more:
                    project(b + 1, i, 0, 1 - par)
                turn(b, i, 0)
                score(b, i, 2, par)
                turn(b, i, 1)
                score(b, i, 3, par)
                if more:
                    project(b + 1, i, 1, 1 - par)
                    turn_q(b + 1, i)
                turn(b, i, 2)
                turn(b, i, 3)
                if more:
                    project(b + 1, i, 2, 1 - par)
                weigh(b, i, par, (0, 1))
                if more:
                    turn_k(b + 1, i)
                weigh(b, i, par, (2, 3))

            batches(pe, start, step)

        @block.scalar
        def _(act):
            def high(b, t, par):
                wait(act, c_in, b)
                if not (isinstance(b, int) and b == 0 and t < 2):
                    wait(act, v_mm, b, (-3, -2, 0)[t])
                act.activation(c_hi[(par + t) % 2][:, :, :], c_raw[:, :, t * CT:(t + 1) * CT], ACT.Copy)\
                    .then_inc(c_hi_ready.sem, 1)

            def square(b, i, unit, par):
                m = (S, M[i])[unit]
                wait(act, (q_mm, k_mm)[unit], b, i)
                if unit == 0:
                    if not (isinstance(b, int) and b == 0 and i == 0):
                        wait(act, k_sum, b, 2 * i - 2)
                else:
                    wait(act, q_sum, b, 2 * i)
                act.activation(sq[0:m, :], ps_p[(3 * i + unit) % 2][0:m, :], ACT.Square)\
                    .then_inc((q_sq, k_sq)[unit].sem, 1)

            def keep_q(b, i):
                wait(act, q_turned, b, i)
                act.activation(qT[:, i, :, :], ps_r[:, 0:HQ * S].rearrange("p (j q) -> p j q", j=HQ), ACT.Copy)\
                    .then_inc(qT_ready.sem, 1)

            def keep_k(b, i, par):
                m = M[i]
                wait(act, k_turned, b, i)
                act.activation(kT[par][:, :, i * CT:i * CT + m],
                               ps_r[:, 0:KVH * m].rearrange("p (h t) -> p h t", h=KVH), ACT.Copy)\
                    .then_inc(kT_ready.sem, 1)

            def keep_v(b, i, par):
                m = M[i]
                wait(act, v_mm, b, i)
                wait(act, pv, b, -5)
                act.activation(v[par][0:m, i, :], ps_p[(3 * i + 2) % 2][0:m, :], ACT.Copy).then_inc(v_ready.sem, 1)

            def exp(b, i, j, par):
                n = i * HQ + j
                wait(act, shifted, b, n)
                wait(act, p_turned, b, n - HQ)
                act.activation(prob[j][:, 0:KV], ps_s[j % 2][:, :], ACT.Exp, bias=down[:, j:j + 1],
                               scale=q_scale[par][:, i, j:j + 1], accum_out=total[:, j:j + 1]).then_inc(exped.sem, 1)

            def copy_pT(b, i, j):
                wait(act, p_turned, b, i * HQ + j)
                if j == 0:
                    wait(act, pv, b, i - 2)
                act.activation(pT[i % 2][0:CT, :, j, :], ps_t[j % 2][0:CT, :, :], ACT.Copy).then_inc(pT_ready.sem, 1)

            def copy_o(b, i):
                wait(act, pv, b, i)
                wait(act, o_put[i % 2], b, i // 2 - 1)
                act.activation(ov[i % 2][:, :, :], ps_o[:, :, :], ACT.Copy).then_inc(o_ready.sem, 1)

            def next_high(b, i, par):
                if i in (0, 1):
                    high(b, i + 1, par)
                elif i == 3 and not (isinstance(b, int) and b == B - 1):
                    high(b + 1, 0, 1 - par)

            def split(n):
                slot = W_SLOT[n]
                act.wait_ge(w_in[slot], 16 * (W_SLOT[:n].count(slot) + 1))
                act.activation(w_hi[:, W_ORDER[n], :, :], v[slot][:, :, :], ACT.Copy).then_inc(w_hi_ready, 1)

            def start(b, i, par):
                square(b, i, 0, par)
                if i:
                    keep_k(b, i - 1, par)
                square(b, i, 1, par)
                keep_q(b, i)
                next_high(b, i, par)
                if i < 3:
                    split(i + 3)
                keep_v(b, i, par)
                if i == 3:
                    keep_k(b, i, par)

            def step(b, i, par, more):
                nb, npar = b + 1, 1 - par
                exp(b, i, 0, par)
                exp(b, i, 1, par)
                if more:
                    square(nb, i, 0, npar)
                copy_pT(b, i, 0)
                copy_pT(b, i, 1)
                exp(b, i, 2, par)
                exp(b, i, 3, par)
                if more:
                    square(nb, i, 1, npar)
                    keep_q(nb, i)
                copy_pT(b, i, 2)
                copy_pT(b, i, 3)
                if more:
                    next_high(nb, i, npar)
                    keep_v(nb, i, npar)
                    keep_k(nb, i, npar)
                copy_o(b, i)

            exped.open(act)
            o_ready.open(act)
            pT_ready.open(act)
            split(0)
            high(0, 0, 0)
            split(1)
            split(2)
            act.wait_ge(w_lo_ready, 3)
            batches(act, start, step, lambda: act.wait_ge(w_lo_ready, NW))

        @block.vector
        def _(dve):
            q_sum.open(dve)
            k_sum.open(dve)

            def rotate(b, i, unit, par):
                m = (S, M[i])[unit]
                ps = ps_p[(3 * i + unit) % 2][0:m, :]
                r1, r2 = ((q1, q2), (k1, k2))[unit]
                t = (4, i)[unit]
                turned, rot = ((q_turned, q_rot), (k_turned, k_rot))[unit]
                sq_done, summed, scaled = ((q_sq, q_sum, q_scaled), (k_sq, k_sum, k_scaled))[unit]
                wait(dve, sq_done, b, i)
                if i == 0:
                    inputs(dve, b, par)
                if not (isinstance(b, int) and b == 0 and i == 0):
                    wait(dve, turned, b, i - 1)
                h4 = lambda ap: ap.rearrange("p (h d) -> p h d", h=HQ)
                dve.tensor_tensor(h4(r1[0:m, :]), h4(ps), over_heads(tab[par][0:m, t, 0, :], HQ), ALU.mult)
                for half in range(2):
                    this, other = slice(half * HF, (half + 1) * HF), slice((1 - half) * HF, (2 - half) * HF)
                    ins = dve.tensor_tensor(h4(r2[0:m, :])[:, :, this], h4(ps)[:, :, other],
                                            over_heads(tab[par][0:m, t, 1, this], HQ), ALU.mult)
                ins.then_inc(rot.sem, 1)
                if not (isinstance(b, int) and b == 0 and i == 0):
                    wait(dve, scaled, b, i - 1)
                dve.tensor_reduce(ssum[0:m, unit, :], h4(sq[0:m, :]), AX.X, ALU.add).then_inc(summed.sem, 1)
                wait(dve, summed, b, 2 * i)
                if unit == 0:
                    f = 1.0 / X_SCALE ** 2
                    dve.tensor_scalar(ssum[0:m, unit, :], ssum[0:m, unit, :], f / HD, RMS_EPS * f,
                                      ALU.mult, ALU.add).then_inc(summed.sem, 1)
                else:
                    dve.tensor_scalar(ssum[0:m, unit, :], ssum[0:m, unit, :], 1.0 / HD, RMS_EPS,
                                      ALU.mult, ALU.add).then_inc(summed.sem, 1)

            def maximum(b, i, j, par):
                n = i * HQ + j
                if i == 0 and j == 0:
                    wait(dve, q_scaled, b, 3)
                wait(dve, scored, b, n)
                dve.tensor_reduce(top[:, j:j + 1], ps_s[j % 2][:, :], AX.X, ALU.max, negate=True).then_inc(maxed.sem, 1)
                wait(dve, maxed, b, n)
                dve.tensor_tensor(down[:, j:j + 1], top[:, j:j + 1], q_scale[par][:, i, j:j + 1], ALU.mult).then_inc(shifted.sem, 1)

            def divide(b, i, j):
                n = i * HQ + j
                wait(dve, exped, b, n)
                dve.reciprocal(inv[:, j:j + 1], total[:, j:j + 1]).then_inc(inverted.sem, 1)
                wait(dve, inverted, b, n)
                dve.tensor_scalar(prob[j][:, 0:KV], prob[j][:, 0:KV], inv[:, j:j + 1], None, ALU.mult).then_inc(probs.sem, 1)

            def split(n):
                dve.wait_ge(w_hi_ready, n + 1)
                dve.tensor_tensor(w_lo[:, W_ORDER[n], :, :], v[W_SLOT[n]][:, :, :], w_hi[:, W_ORDER[n], :, :],
                                  ALU.subtract).then_inc(w_lo_ready, 1)

            def start(b, i, par):
                rotate(b, i, 0, par)
                rotate(b, i, 1, par)
                if i < 3:
                    split(i + 3)

            def step(b, i, par, more):
                maximum(b, i, 0, par)
                maximum(b, i, 1, par)
                divide(b, i, 0)
                divide(b, i, 1)
                if more:
                    rotate(b + 1, i, 0, 1 - par)
                maximum(b, i, 2, par)
                maximum(b, i, 3, par)
                divide(b, i, 2)
                divide(b, i, 3)
                if more:
                    rotate(b + 1, i, 1, 1 - par)

            for n in range(3):
                split(n)
            batches(dve, start, step)
    return ctx


def experts(nc, weights, acc, oh, place, weight, run, rows_n, tokens, rows_y, out):
    KI = INTER // P
    NU = 2 * NS
    AHEAD = 2
    GW = KD * 2 * INTER
    WW = GW + KI * D
    ctx = Phase(nc, "ffn")
    with ctx:
        sb = ctx.sb
        ev = ctx.ev
        ident = sb("ident", [P, P])
        raw = sb("raw", [P, E, WW])
        w_hi = [sb(f"w_hi{i}", [P, WW], F32R) for i in range(2)]
        w_lo = [sb(f"w_lo{i}", [P, WW], F32R) for i in range(2)]
        gu_of = lambda w: w[:, 0:GW].rearrange("p (k i) -> p k i", k=KD)
        down_of = lambda w: w[:, GW:WW].rearrange("p (k o) -> p k o", k=KI)
        xg = [sb(f"xg{i}", [P, D]) for i in range(4)]
        xh = [sb(f"xh{i}", [P, KD, P], F32R) for i in range(2)]
        xl = [sb(f"xl{i}", [P, KD, P], F32R) for i in range(2)]
        sig = [sb(f"sig{i}", [P, INTER]) for i in range(2)]
        a = [sb(f"a{i}", [P, INTER]) for i in range(2)]
        aT_hi = [sb(f"aT_hi{i}", [P, KI, P], F32R) for i in range(2)]
        aT_lo = [sb(f"aT_lo{i}", [P, KI, P], F32R) for i in range(2)]
        yt = [sb(f"yt{i}", [P, D]) for i in range(2)]
        slot_i = sb("slot_i", [P, NS + 1], I32)
        slot = sb("slot", [P, NS + 1])
        tiles = sb("tiles", [P, E])
        begin = sb("begin", [P, E])
        behind = sb("behind", [P, E, NS + 1])
        past = sb("past", [P, E, NS + 1])
        who = sb("who", [P, NS + 1])
        skip = sb("skip", [P, NS + 1])
        where = sb("where", [P, NS + 1])
        who_i = sb("who_i", [P, NS + 1], I32)
        where_i = sb("where_i", [P, NS + 1], I32)
        list_i = sb("list_i", [P, NS, 2], I32)
        row_i = [sb(f"row_i{i}", [P, 2], U32) for i in range(2)]
        fetch = sb("fetch", [P, TT, 2, E])
        fetch_f = sb("fetch_f", [P, TT, 2])
        fetch_i = sb("fetch_i", [P, TT, 2], U32)
        share = sb("share", [P, TT, 2])
        ps_x = [ctx.bank(f"ps_x{i}", P, KD, P) for i in range(2)]
        ps_g = [ctx.bank(f"ps_g{i}", P, 2 * INTER) for i in range(2)]
        ps_a = [ctx.bank(f"ps_a{i}", P, KI, P) for i in range(2)]
        ps_y = [ctx.bank(f"ps_y{i}", P, D) for i in range(2)]
        id_ready = ctx.sem("id_ready")
        planned = ctx.sem("slots_planned")
        plan_step = ctx.sem("plan_step")
        w_in = ctx.sem("weights_loaded")
        list_in = ev("lists_loaded", 1, step=16)
        ticks = ctx.sem("ticks")
        row_ready = ev("row_indices", 1)
        x_in = [ev(f"x_gathered{i}", 1, step=16) for i in range(4)]
        x_turned = ev("x_turned", 1, 4)
        x_hi, x_lo = ev("x_hi", 1), ev("x_lo", 1)
        g_hi, d_hi = ev("w_gate_up_hi", 1), ev("w_down_hi", 1)
        g_lo, d_lo = ev("w_gate_up_lo", 1), ev("w_down_lo", 1)
        gu = ev("gate_up", 1, 4)
        sigmoid = ev("sigmoid", 1)
        silu = ev("silu", 1)
        gated = ev("gated", 1, 2)
        turned = ev("a_turned", 1, 2)
        a_hi, a_lo = ev("aT_hi", 1), ev("aT_lo", 1, 2)
        down_mm = ev("down", 1, 4)
        y_out = ev("y_copied", 1, 2)
        y_put = [ev(f"y_stored{i}", 1, 1, 16) for i in range(2)]
        fetched = [ctx.sem(f"y_fetched{i}") for i in range(4)]
        summed = ctx.sem("summed")
        stored = ctx.sem("stored")
        block = ctx.enter_context(nc.Block())

        LOOPS = (NU - 4) // 4

        def run_units(eng, step):
            step(0, 0)
            step(0, 1)
            with eng.Fori(0, LOOPS) as h:
                for i in range(2, 6):
                    step(h, i)
            for i in range(4 * LOOPS + 2, NU + 2):
                step(0, i)

        def has(h, i):
            return not isinstance(h, int) or 0 <= i < NU

        @block.sync
        def _(sp):
            sp.dma_start(raw[:, 0, :], weights[0]).then_inc(w_in, 16)
            for e in range(1, E):
                sp.wait_ge(w_in, 16 * e)
                sp.dma_start(raw[:, e, :], weights[e]).then_inc(w_in, 16)

            for t in range(TT):
                sp.wait_ge(summed, 2 * t + 2)
                sp.dma_start(out[t * P:(t + 1) * P, :], acc[:, t, :]).then_inc(stored, 16)
            sp.wait_ge(stored, 16 * TT)

        @block.gpsimd
        def _(pool):
            pool.iota(slot_i[:, :], pattern=[[1, NS + 1]], base=0, channel_multiplier=0).then_inc(id_ready, 1)
            identity(pool, ident[:, :], id_ready, 1)
            pool.wait_ge(planned, 1)

            def prepare(h, i):
                s = h * 2 + i
                b = i % 2
                e = pool.value_load(who_i[0:1, bass.ds(s, 1)], min_val=0, max_val=E - 1)
                wait(pool, list_in, s)
                wait(pool, x_turned, h * 4 + 2 * i, -3)
                carry(pool, h, ticks)
                pool.tensor_copy(row_i[b][:, :], list_i[:, bass.ds(s, 1), :].rearrange("p o h -> p (o h)"))\
                    .then_inc(row_ready.sem, 1)
                wait(pool, row_ready, s)
                carry(pool, h, ticks)
                for half in range(2):
                    pool.indirect_dma_start(xg[2 * b + half][:, :], None, rows_n,
                                            bass.IndirectOffsetOnAxis(ap=row_i[b][:, half:half + 1], axis=0))\
                        .then_inc(x_in[2 * b + half].sem, 16)
                wait(pool, g_hi, s)
                carry(pool, h, ticks)
                pool.tensor_tensor(w_lo[b][:, 0:GW], raw[:, bass.ds(e, 1), 0:GW].rearrange("p o w -> p (o w)"),
                                   w_hi[b][:, 0:GW], ALU.subtract).then_inc(g_lo.sem, 1)

            with pool.Fori(0, NS // 2) as h:
                prepare(h, 0)
                prepare(h, 1)
            for s in range(NS // 2 * 2, NS):
                prepare(0, s)
            for i in range(2):
                pool.wait_ge(y_put[i].sem, y_put[i].at(NU // 2 - 1))
            for t in range(TT):
                for c in range(2):
                    b = 2 * (t % 2) + c
                    if t >= 2:
                        pool.wait_ge(summed, 2 * (t - 2) + c + 1)
                    pool.indirect_dma_start(xg[b][:, :], None, rows_y,
                                            bass.IndirectOffsetOnAxis(ap=fetch_i[:, t, c:c + 1], axis=0))\
                        .then_inc(fetched[b], 16)

        @block.tensor
        def _(pe):
            pe.wait_ge(id_ready, 3)
            x_turned.open(pe)
            gu.open(pe)
            turned.open(pe)
            down_mm.open(pe)

            def turn_x(h, i):
                n = h * 4 + i
                pe.wait_ge(x_in[i % 4].sem, (h + i // 4) * 16 + 16)
                if not (isinstance(h, int) and i < 2):
                    wait(pe, x_lo, n, -2)
                for k in range(KD):
                    mm = pe.transpose(ps_x[i % 2][:, k, :], xg[i % 4][:, k * P:(k + 1) * P], ident[:, :])
                mm.then_inc(x_turned.sem, 1)

            def project(h, i):
                n, s, b = h * 4 + i, h * 2 + i // 2, i // 2 % 2
                if i % 2 == 0:
                    wait(pe, g_lo, s)
                wait(pe, x_lo, n)
                wait(pe, gated, n, -2)
                for k in range(KD):
                    mm = mm3(pe, ps_g[i % 2][:, :], xh[i % 2][:, k, :], xl[i % 2][:, k, :], gu_of(w_hi[b])[:, k, :],
                             gu_of(w_lo[b])[:, k, :], k == 0, k == KD - 1)
                mm.then_inc(gu.sem, 1)

            def turn(h, i):
                n = h * 4 + i
                wait(pe, gated, n)
                wait(pe, a_lo, n, -2)
                for k in range(KI):
                    mm = pe.transpose(ps_a[i % 2][:, k, :], a[i % 2][:, k * P:(k + 1) * P], ident[:, :])
                mm.then_inc(turned.sem, 1)

            def project_down(h, i):
                n, s, b = h * 4 + i, h * 2 + i // 2, i // 2 % 2
                if i % 2 == 0:
                    wait(pe, d_lo, s)
                wait(pe, a_lo, n)
                wait(pe, y_out, n, -2)
                for k in range(KI):
                    mm = mm3(pe, ps_y[i % 2][:, :], aT_hi[i % 2][:, k, :], aT_lo[i % 2][:, k, :],
                             down_of(w_hi[b])[:, k, :], down_of(w_lo[b])[:, k, :], k == 0, k == KI - 1)
                mm.then_inc(down_mm.sem, 1)

            def step(h, i):
                if has(h, i + 1):
                    turn_x(h, i + 1)
                if has(h, i):
                    project(h, i)
                if has(h, i - 1):
                    turn(h, i - 1)
                if has(h, i - 2):
                    project_down(h, i - 2)

            turn_x(0, 0)
            run_units(pe, step)

        @block.scalar
        def _(act):
            y_out.open(act)
            for i in range(2):
                y_put[i].open(act)

            def split(h, i, part):
                s, b = h * 2 + i, i % 2
                e = act.value_load(who_i[0:1, bass.ds(s, 1)], min_val=0, max_val=E - 1)
                act.wait_ge(w_in, e * 16 + 16)
                wait(act, (gu, down_mm)[part], h * 4 + 2 * i, -3)
                act.sem_inc(ticks, 1)
                cols = (slice(0, GW), slice(GW, WW))[part]
                act.activation(w_hi[b][:, cols], raw[:, bass.ds(e, 1), cols].rearrange("p o w -> p (o w)"), ACT.Copy)\
                    .then_inc((g_hi, d_hi)[part].sem, 1)

            def turn_x(h, i):
                n = h * 4 + i
                wait(act, x_turned, n)
                wait(act, gu, n, -2)
                act.activation(xh[i % 2][:, :, :], ps_x[i % 2][:, :, :], ACT.Copy).then_inc(x_hi.sem, 1)

            def sigmoids(h, i):
                n = h * 4 + i
                wait(act, gu, n)
                wait(act, turned, n, -2)
                act.activation(sig[i % 2][:, :], ps_g[i % 2][:, 0:INTER], ACT.Sigmoid).then_inc(sigmoid.sem, 1)

            def high(h, i):
                n = h * 4 + i
                wait(act, turned, n)
                wait(act, down_mm, n, -2)
                act.activation(aT_hi[i % 2][:, :, :], ps_a[i % 2][:, :, :], ACT.Copy).then_inc(a_hi.sem, 1)

            def copy_y(h, i):
                n = h * 4 + i
                wait(act, down_mm, n)
                act.wait_ge(y_put[i % 2].sem, (h * 2 + i // 2) * 16 + 16)
                act.activation(yt[i % 2][:, :], ps_y[i % 2][:, :], ACT.Copy).then_inc(y_out.sem, 1)

            def store(h, i):
                wait(act, y_out, h * 4 + i)
                rows = rows_y[bass.ds((h * 2 + i // 2) * ST, ST), :].rearrange("(p h) d -> h p d", h=2)[i % 2]
                act.dma_start(rows, yt[i % 2][:, :]).then_inc(y_put[i % 2].sem, 16)

            def step(h, i):
                if has(h, i + 1):
                    turn_x(h, i + 1)
                if has(h, i):
                    sigmoids(h, i)
                if has(h, i - 1):
                    high(h, i - 1)
                if has(h, i - 2):
                    copy_y(h, i - 2)
                if i % 2 == 1 and has(h, i + 3):
                    split(h, (i + 3) // 2, 0)
                if i % 2 == 0 and has(h, i):
                    split(h, i // 2, 1)
                if has(h, i - 2):
                    store(h, i - 2)
                if i % 2 == 0 and has(h, i + 2 * AHEAD):
                    load_list(h, i // 2 + AHEAD)

            def load_list(h, i):
                s = h * 2 + i
                at = act.value_load(where_i[0:1, bass.ds(s, 1)], min_val=0, max_val=DUMP - ST)
                if not isinstance(s, int) or s:
                    wait(act, list_in, s, -1)
                act.dma_start(list_i[:, bass.ds(s, 1), :].rearrange("p o h -> p (o h)"),
                              tokens[bass.ds(at, ST), :].rearrange("(p h) o -> p (h o)", h=2)).then_inc(list_in.sem, 16)

            act.wait_ge(planned, 1)
            for s in range(AHEAD):
                load_list(0, s)
            split(0, 0, 0)
            turn_x(0, 0)
            split(0, 1, 0)
            run_units(act, step)

        @block.vector
        def _(dve):
            gated.open(dve)
            a_lo.open(dve)
            count = [0]

            def then(ins):
                count[0] += 1
                ins.then_inc(plan_step, 1)
                dve.wait_ge(plan_step, count[0])

            ROUND = RopeTables.ROUND
            dve.wait_ge(id_ready, 1)
            dve.tensor_copy(slot[:, :], slot_i[:, :])
            dve.tensor_scalar(tiles[:, :], run[:, :], 1.0 / ST, (ST - 1) / (2.0 * ST), ALU.mult, ALU.add)
            then(dve.memset(begin[:, :], 0.0))
            then(dve.tensor_scalar(tiles[:, :], tiles[:, :], ROUND, ROUND, ALU.add, ALU.subtract))
            for e in range(1, E):
                then(dve.tensor_tensor(begin[:, e:e + 1], begin[:, e - 1:e], tiles[:, e - 1:e], ALU.add))
            then(dve.tensor_tensor(behind[:, :, :], over_heads(slot[:, :], E), along(begin[:, :], NS + 1), ALU.is_ge))
            dve.tensor_tensor(past[:, 1:E, :], behind[:, 1:E, :], along(tiles[:, 0:E - 1], NS + 1), ALU.mult)
            then(dve.tensor_reduce(who[:, :], behind[:, 1:E, :].rearrange("p e s -> p s e"), AX.X, ALU.add))
            then(dve.tensor_reduce(skip[:, :], past[:, 1:E, :].rearrange("p e s -> p s e"), AX.X, ALU.add))
            then(dve.tensor_tensor(skip[:, :], slot[:, :], skip[:, :], ALU.subtract))
            then(dve.tensor_scalar(where[:, :], who[:, :], float(REGION), None, ALU.mult))
            then(dve.scalar_tensor_tensor(where[:, :], skip[:, :], float(ST), where[:, :], ALU.mult, ALU.add))
            dve.tensor_copy(who_i[:, :], who[:, :])
            dve.tensor_copy(where_i[:, :], where[:, :]).then_inc(planned, 1)

            def low_d(h, i):
                s, b = h * 2 + i, i % 2
                e = dve.value_load(who_i[0:1, bass.ds(s, 1)], min_val=0, max_val=E - 1)
                wait(dve, d_hi, s)
                dve.tensor_tensor(w_lo[b][:, GW:WW], raw[:, bass.ds(e, 1), GW:WW].rearrange("p o w -> p (o w)"),
                                  w_hi[b][:, GW:WW], ALU.subtract).then_inc(d_lo.sem, 1)

            def turn_x(h, i):
                wait(dve, x_hi, h * 4 + i)
                dve.tensor_tensor(xl[i % 2][:, :, :], ps_x[i % 2][:, :, :], xh[i % 2][:, :, :], ALU.subtract).then_inc(x_lo.sem, 1)

            def gate(h, i):
                n = h * 4 + i
                d, g = sig[i % 2], ps_g[i % 2]
                wait(dve, sigmoid, n)
                dve.tensor_tensor(d[:, :], g[:, 0:INTER], d[:, :], ALU.mult).then_inc(silu.sem, 1)
                wait(dve, silu, n)
                wait(dve, turned, n, -2)
                dve.tensor_tensor(a[i % 2][:, :], g[:, INTER:2 * INTER], d[:, :], ALU.mult).then_inc(gated.sem, 1)

            def low(h, i):
                wait(dve, a_hi, h * 4 + i)
                dve.tensor_tensor(aT_lo[i % 2][:, :, :], ps_a[i % 2][:, :, :], aT_hi[i % 2][:, :, :], ALU.subtract)\
                    .then_inc(a_lo.sem, 1)

            def step(h, i):
                if has(h, i + 1):
                    turn_x(h, i + 1)
                if has(h, i):
                    gate(h, i)
                if has(h, i - 1):
                    low(h, i - 1)
                if i % 2 == 0 and has(h, i):
                    low_d(h, i // 2)

            turn_x(0, 0)
            chosen = oh[:, :, :].rearrange("p t (c e) -> p t c e", c=2)
            one_hot = lambda n: chosen[:, :, :, 0:n]
            both = lambda ap: ap.unsqueeze(2).broadcast_to((P, TT, 2, ap.shape[2]))
            then(dve.scalar_tensor_tensor(place[:, :, :], begin[:, :].unsqueeze(1).broadcast_to((P, TT, E)), float(ST),
                                          place[:, :, :], ALU.mult, ALU.add))
            then(dve.tensor_tensor(fetch[:, :, :, :], one_hot(E), both(place[:, :, :]), ALU.mult))
            then(dve.tensor_reduce(fetch_f[:, :, :], fetch[:, :, :, :], AX.X, ALU.add))
            then(dve.tensor_copy(fetch_i[:, :, :], fetch_f[:, :, :]))
            then(dve.tensor_tensor(fetch[:, :, :, :], one_hot(E), both(weight[:, :, 0:E]), ALU.mult))
            then(dve.tensor_reduce(share[:, :, :], fetch[:, :, :, :], AX.X, ALU.add))
            run_units(dve, step)
            for t in range(TT):
                for c in range(2):
                    dve.wait_ge(fetched[2 * (t % 2) + c], 16 * (t // 2 + 1))
                    if c:
                        dve.wait_ge(summed, 2 * t + 1)
                    dve.scalar_tensor_tensor(acc[:, t, :], xg[2 * (t % 2) + c][:, :], share[:, t, c:c + 1],
                                             acc[:, t, :], ALU.mult, ALU.add).then_inc(summed, 1)
    return ctx


def build(nc, x, ctxT, pos_ctx, pos_x, inv_freq, q_proj, wq_rotT, wkvaT, kv_ln, kv_b, woT, xwqT, xwkT, xwvT,
          xwoT, q_norm, k_norm, clsT, bias, expert_w, out):
    dram = lambda name, shape: nc.dram_tensor(name, shape, F32).ap()
    tables = dram("rope_tables", (B, P, 5, 2, HD))
    vo = dram("value_output_weights", (P, H, D))
    x0T = dram("x0T_hi", (P, KD, T)), dram("x0T_lo", (P, KD, T))
    x1T = dram("x1T_hi", (P, KD, T)), dram("x1T_lo", (P, KD, T))
    o1T, o2T = dram("self_outT", (P, H, T)), dram("cross_outT", (P, H, T))
    x1 = dram("x1", (T, D))
    rows_n, rows_y = dram("x2_normed", (T, D)), dram("expert_rows", (NS * ST, D))
    tokens = nc.dram_tensor("tokens_of_experts", (DUMP + P, 1), I32).ap()
    x_rows = x.rearrange("b s d -> (b s) d")
    out_rows = out.rearrange("b s d -> (b s) d")
    kv_heads = kv_b.rearrange("(h c d) r -> c d h r", h=H, c=2)

    with ExitStack() as ctx:
        sb = lambda name, shape, dt=F32: ctx.enter_context(nc.sbuf_tensor(name, shape, dt))
        qf = sb("qf_hi", [P, KD, H, RANK], F32R), sb("qf_lo", [P, KD, H, RANK], F32R)
        qr = sb("qr_hi", [P, KD, H * ROPE], F32R), sb("qr_lo", [P, KD, H * ROPE], F32R)
        lat_kT = sb("lat_kT", [P, 3, T])
        lat_v = sb("lat_v", [S, B, RANK])
        with ExitStack() as early:
            esb = lambda name, shape, dt: early.enter_context(nc.sbuf_tensor(name, shape, dt))
            kva = esb("kva_hi", [P, KD, RANK + ROPE], F32R), esb("kva_lo", [P, KD, RANK + ROPE], F32R)
            fold = fold_weights(nc, q_proj, kv_heads[0], kv_heads[1], woT, wq_rotT, wkvaT, *qf, *qr, *kva,
                                lat_kT[:, :, :].rearrange("p c t -> p (c t)"), vo)
            lat = latents(nc, x, kv_ln, *kva, lat_kT, lat_v, *x0T)
        sa = self_attention(nc, *x0T, *qf, *qr, lat_kT, lat_v, o1T)
    clear(nc, fold, lat, sa)
    out1 = project_out(nc, o1T, vo, x_rows, x1, x1T, rope=(pos_ctx, pos_x, inv_freq, k_norm, q_norm, tables))
    ca = cross_attention(nc, ctxT, *x1T, xwqT, xwkT, xwvT, tables, o2T)
    clear(nc, out1, ca)
    with ExitStack() as ctx:
        sb = lambda name, shape, dt=F32: ctx.enter_context(nc.sbuf_tensor(name, shape, dt))
        acc = sb("acc", [P, TT, D])
        oh = sb("choices_one_hot", [P, TT, 2 * TOTAL])
        place = sb("choice_place", [P, TT, E])
        weight = sb("choice_weight", [P, TT, TOTAL])
        run = sb("tokens_of_expert", [P, E])
        keep = acc, oh, place, weight, run, rows_n, tokens
        project_out(nc, o2T, xwoT, x1, None, None, router=(clsT, bias), keep=keep)
        experts(nc, expert_w, *keep, rows_y, out_rows)


def layouts(x, ctx_2048, pos_BxS2, itok_BxS_4096_4607, L0_attn_q_proj_w, L0_attn_kv_a_proj_w, L0_attn_kv_a_ln_w,
            L0_attn_kv_b_proj_w, L0_attn_o_proj_w, L0_xattn_Wq, L0_xattn_Wk, L0_xattn_Wv, L0_xattn_Wo,
            L0_xattn_q_norm_w, L0_xattn_k_norm_w, L0_ffn_classifier_w, L0_ffn_e_score_correction_bias,
            L0_ffn_gate_w, L0_ffn_up_w, L0_ffn_down_w):
    kT = lambda w: w.T.reshape(KD, P, -1).transpose(1, 0, 2)
    rows = lambda w, n: np.broadcast_to(w, (n, w.shape[0]))
    heads = lambda w: w.reshape(D, H, P).transpose(2, 1, 0)
    rot = L0_attn_q_proj_w.reshape(H, NOPE + ROPE, D)[:, NOPE:].reshape(H * ROPE, D)
    gu = np.concatenate([L0_ffn_gate_w, L0_ffn_up_w], axis=1)
    per_k = lambda w: w.transpose(0, 2, 1).reshape(E, -1, P, w.shape[1]).transpose(0, 2, 1, 3).reshape(E, P, -1)
    freq = 1.0 / np.float32(10000.0) ** (np.arange(0, HD, 2, dtype=np.float32) / np.float32(HD))
    return {
        "x": x,
        "ctxT": ctx_2048.reshape(B, C, KD, P).transpose(0, 3, 2, 1),
        "pos_ctx": pos_BxS2.reshape(B, 3, CT).transpose(2, 1, 0),
        "pos_x": itok_BxS_4096_4607.T,
        "inv_freq": rows(freq.astype(np.float32), P),
        "q_proj": L0_attn_q_proj_w,
        "wq_rotT": kT(rot),
        "wkvaT": kT(L0_attn_kv_a_proj_w),
        "kv_ln": rows(L0_attn_kv_a_ln_w, S),
        "kv_b": L0_attn_kv_b_proj_w,
        "woT": heads(L0_attn_o_proj_w),
        "xwqT": kT(L0_xattn_Wq),
        "xwkT": kT(L0_xattn_Wk),
        "xwvT": kT(L0_xattn_Wv),
        "xwoT": heads(L0_xattn_Wo),
        "q_norm": rows(L0_xattn_q_norm_w, P),
        "k_norm": rows(L0_xattn_k_norm_w, P),
        "clsT": kT(L0_ffn_classifier_w),
        "bias": rows(L0_ffn_e_score_correction_bias, P),
        "expert_w": np.concatenate([per_k(gu), per_k(L0_ffn_down_w)], axis=2),
    }


def kernel(**inputs):
    import concourse.bacc as bacc
    from concourse.bass_utils import run_bass_kernel_spmd

    nc = bacc.Bacc("TRN2", target_bir_lowering=False, num_devices=1)
    arrays, args = {}, {}
    for name, a in layouts(**{k: np.asarray(v) for k, v in inputs.items()}).items():
        a = np.ascontiguousarray(a)
        arrays[f"in_{name}"] = a
        args[name] = nc.dram_tensor(f"in_{name}", a.shape, mybir.dt.from_np(a.dtype), kind="ExternalInput").ap()
    out = nc.dram_tensor("out", (B, S, D), F32, kind="ExternalOutput").ap()
    build(nc, **args, out=out)
    r = run_bass_kernel_spmd(nc, [arrays], core_ids=[0])
    return r.results[0]["out"]
```
